# Optimizing a Trainium2 kernel written in Bass

```python
import numpy as np
import jax
import jax.numpy as jnp

def _softmax(x, axis=-1):
    return jax.nn.softmax(x, axis=axis)

def _gelu(x):
    return jax.nn.gelu(x, approximate=True)

def _silu(x):
    return jax.nn.silu(x)

def _sigmoid(x):
    return jax.nn.sigmoid(x)

def _layernorm(x, axis=-1, eps=1e-05):
    m = jnp.mean(x, axis=axis, keepdims=True)
    v = jnp.var(x, axis=axis, keepdims=True)
    return (x - m) / jnp.sqrt(v + eps)

def _scatter_add(tgt, idx, src, axis=0):
    return tgt.at[idx].add(src)

def _segment_sum(src, seg, n):
    return jax.ops.segment_sum(src, seg, n)
kernel_name = 'mk_xattn_ffn_d2_seqx_r8_b9f777'

def setup_inputs(seed: int=0):
    np.random.seed(seed)
    _w = jnp.asarray

    def _rec_inputs():
        import jax
        import jax.numpy as jnp
        _rk = jax.random.key(seed)
        x = -0.0003929 + 0.9999 * jax.random.normal(jax.random.fold_in(_rk, 1), (4, 256, 128), jnp.float32)
        _lenS = 256 - jax.random.randint(jax.random.fold_in(_rk, 7), (4,), 0, max(1, 256 // 4) + 1, jnp.int32)
        _lenS2 = 256 - jax.random.randint(jax.random.fold_in(_rk, 8), (4,), 0, max(1, 256 // 4) + 1, jnp.int32)
        _ctx_1024P = jax.random.normal(jax.random.fold_in(_rk, 11), (4, 16, 128), jnp.float32)
        _ctx_1024c = jax.random.dirichlet(jax.random.fold_in(_rk, 511), 0.3 * jnp.ones((16,), jnp.float32), (4, 256))
        _ctx_1024t = jnp.einsum('bsk,bkd->bsd', _ctx_1024c, _ctx_1024P)
        _ctx_1024t = _ctx_1024t * jax.lax.rsqrt(jnp.mean(jnp.square(_ctx_1024t)) + 1e-12) * 0.953939
        ctx_1024 = -1.39393e-06 + 0.999914 * (_ctx_1024t + 0.3 * jax.random.normal(jax.random.fold_in(_rk, 611), (4, 256, 128), jnp.float32))
        return (x, ctx_1024)
    x, ctx_1024 = _rec_inputs()

    def _L0_xattn_setup():
        import jax, jax.numpy as jnp
        import numpy as np
        B, C_LEN, Q_LEN, D = (8, 256, 64, 128)
        key = jax.random.key(seed)
        ks = jax.random.split(key, 10)
        scale = 1.0 / np.sqrt(D)
        return {'c': jax.random.normal(ks[0], (B, C_LEN, D), dtype=jnp.float32), 'q': jax.random.normal(ks[1], (B, Q_LEN, D), dtype=jnp.float32), 'w_cq': jax.random.normal(ks[2], (D,), dtype=jnp.float32) * scale, 'b_cq': jax.random.normal(ks[3], (), dtype=jnp.float32) * scale, 'w_c': jax.random.normal(ks[4], (D,), dtype=jnp.float32) * scale, 'b_c': jax.random.normal(ks[5], (), dtype=jnp.float32) * scale, 'w_q': jax.random.normal(ks[6], (D,), dtype=jnp.float32) * scale, 'b_q': jax.random.normal(ks[7], (), dtype=jnp.float32) * scale, 'W_l': jax.random.normal(ks[8], (D, 4 * D), dtype=jnp.float32) * (1.0 / np.sqrt(4 * D)), 'b_l': jax.random.normal(ks[9], (D,), dtype=jnp.float32) * (1.0 / np.sqrt(4 * D))}
    _L0_xattn_all = _L0_xattn_setup()
    _L0_xattn_in = {k: v for k, v in _L0_xattn_all.items() if k in ('w_cq', 'b_cq', 'w_c', 'b_c', 'w_q', 'b_q', 'W_l', 'b_l')}
    del _L0_xattn_all

    def _L0_ffn_setup():
        import jax, jax.numpy as jnp
        import numpy as np
        E = 8
        TOP_K = 2
        D = 128
        H = 2 * D
        key = jax.random.key(seed)
        k0, k1, k2, k3, k4 = jax.random.split(key, 5)
        scale = 0.02
        x = jax.random.normal(k0, (4, 256, D), dtype=jnp.float32)
        Wg = jax.random.normal(k1, (D, E), dtype=jnp.float32) * scale
        W1 = jax.random.normal(k2, (E, D, H), dtype=jnp.float32) * scale
        W2 = jax.random.normal(k3, (E, D, H), dtype=jnp.float32) * scale
        W3 = jax.random.normal(k4, (E, H, D), dtype=jnp.float32) * scale
        return {'x': x, 'Wg': Wg, 'W1': W1, 'W2': W2, 'W3': W3}
    _L0_ffn_all = _L0_ffn_setup()
    _L0_ffn_in = {k: v for k, v in _L0_ffn_all.items() if k in ('Wg', 'W1', 'W2', 'W3')}
    del _L0_ffn_all

    def _L1_xattn_setup():
        import jax, jax.numpy as jnp
        import numpy as np
        EMBED = 128
        HEADS = 16
        HEAD_DIM = EMBED // HEADS
        key = jax.random.key(seed)
        ks = jax.random.split(key, 7)
        B, Sd, Se = (4, 256, 256)
        dec = jax.random.normal(ks[0], (B, Sd, EMBED), dtype=jnp.float32)
        enc = jax.random.normal(ks[1], (B, Se, EMBED), dtype=jnp.float32)
        scale = 1.0 / np.sqrt(EMBED)
        W_q = jax.random.normal(ks[2], (EMBED, EMBED), dtype=jnp.float32) * scale
        W_k = jax.random.normal(ks[3], (EMBED, EMBED), dtype=jnp.float32) * scale
        W_v = jax.random.normal(ks[4], (EMBED, EMBED), dtype=jnp.float32) * scale
        W_o = jax.random.normal(ks[5], (EMBED, EMBED), dtype=jnp.float32) * scale
        b_o = jax.random.normal(ks[6], (EMBED,), dtype=jnp.float32) * 0.01
        return {'decoder_input': dec, 'encoder_output': enc, 'W_q': W_q, 'W_k': W_k, 'W_v': W_v, 'W_o': W_o, 'b_o': b_o}
    _L1_xattn_all = _L1_xattn_setup()
    _L1_xattn_in = {k: v for k, v in _L1_xattn_all.items() if k in ('W_q', 'W_k', 'W_v', 'W_o', 'b_o')}
    del _L1_xattn_all

    def _L1_ffn_setup():
        import jax, jax.numpy as jnp
        import numpy as np
        FEATURES = 128
        D_IN = 128

        def fp8_gemm_optimized(x, input_scale, kernel, kernel_scale):
            s_in = input_scale[0]
            s_k = kernel_scale[0]
            x_q = (x.astype(jnp.float32) / s_in).astype(jnp.float8_e4m3fn)
            k_q = (kernel.astype(jnp.float32) / s_k).astype(jnp.float8_e4m3fn)
            y = jnp.dot(x_q.astype(jnp.float32), k_q.astype(jnp.float32), preferred_element_type=jnp.float32)
            return y * (s_in * s_k)
        key = jax.random.key(seed)
        kx, kk, kb = jax.random.split(key, 3)
        x = jax.random.normal(kx, (4, 1024, D_IN), dtype=jnp.float32)
        limit = np.sqrt(6.0 / (D_IN + FEATURES)).astype(np.float32)
        kernel = jax.random.uniform(kk, (D_IN, FEATURES), dtype=jnp.float32, minval=-limit, maxval=limit).astype(jnp.bfloat16)
        input_scale = jnp.ones((1,), dtype=jnp.float32)
        kernel_scale = jnp.ones((1,), dtype=jnp.float32)
        bias = jnp.zeros((FEATURES,), dtype=jnp.bfloat16)
        return {'x': x, 'kernel': kernel, 'input_scale': input_scale, 'kernel_scale': kernel_scale, 'bias': bias}
    _L1_ffn_all = _L1_ffn_setup()
    _L1_ffn_in = {k: v for k, v in _L1_ffn_all.items() if k in ('kernel', 'input_scale', 'kernel_scale', 'bias')}
    del _L1_ffn_all
    return {'x': x, 'ctx_1024': ctx_1024, 'L0_xattn_w_cq': _L0_xattn_in['w_cq'], 'L0_xattn_b_cq': _L0_xattn_in['b_cq'], 'L0_xattn_w_c': _L0_xattn_in['w_c'], 'L0_xattn_b_c': _L0_xattn_in['b_c'], 'L0_xattn_w_q': _L0_xattn_in['w_q'], 'L0_xattn_b_q': _L0_xattn_in['b_q'], 'L0_xattn_W_l': _L0_xattn_in['W_l'], 'L0_xattn_b_l': _L0_xattn_in['b_l'], 'L0_ffn_Wg': _L0_ffn_in['Wg'], 'L0_ffn_W1': _L0_ffn_in['W1'], 'L0_ffn_W2': _L0_ffn_in['W2'], 'L0_ffn_W3': _L0_ffn_in['W3'], 'L1_xattn_W_q': _L1_xattn_in['W_q'], 'L1_xattn_W_k': _L1_xattn_in['W_k'], 'L1_xattn_W_v': _L1_xattn_in['W_v'], 'L1_xattn_W_o': _L1_xattn_in['W_o'], 'L1_xattn_b_o': _L1_xattn_in['b_o'], 'L1_ffn_kernel': _L1_ffn_in['kernel'], 'L1_ffn_input_scale': _L1_ffn_in['input_scale'], 'L1_ffn_kernel_scale': _L1_ffn_in['kernel_scale'], 'L1_ffn_bias': _L1_ffn_in['bias']}

def reference(x, ctx_1024, L0_xattn_w_cq, L0_xattn_b_cq, L0_xattn_w_c, L0_xattn_b_c, L0_xattn_w_q, L0_xattn_b_q, L0_xattn_W_l, L0_xattn_b_l, L0_ffn_Wg, L0_ffn_W1, L0_ffn_W2, L0_ffn_W3, L1_xattn_W_q, L1_xattn_W_k, L1_xattn_W_v, L1_xattn_W_o, L1_xattn_b_o, L1_ffn_kernel, L1_ffn_input_scale, L1_ffn_kernel_scale, L1_ffn_bias):
    import jax
    import jax.numpy as jnp

    def _L0_xattn_ref(c, q, w_cq, b_cq, w_c, b_c, w_q, b_q, W_l, b_l):
        import jax, jax.numpy as jnp
        import numpy as np
        B, C_LEN, Q_LEN, D = (8, 256, 64, 128)
        cq = jnp.einsum('bcd,bqd,d->bcq', c, q, w_cq) + b_cq
        s = (c @ w_c + b_c)[:, :, None] + (q @ w_q + b_q)[:, None, :] + cq
        a = jax.nn.softmax(s, axis=2)
        c2q_att = jnp.einsum('bcq,bqd->bcd', a, q)
        b_att = jax.nn.softmax(jnp.max(s, axis=2), axis=1)
        q2c_att = jnp.einsum('bc,bcd->bd', b_att, c)[:, None, :]
        x = jnp.concatenate([c, c2q_att, c * c2q_att, c * q2c_att], axis=-1)
        z = x @ W_l.T + b_l
        return z

    def _L0_ffn_ref(x, Wg, W1, W2, W3):
        import jax, jax.numpy as jnp
        import numpy as np
        E = 8
        TOP_K = 2
        D = 128
        H = 2 * D
        logits = jnp.einsum('bsd,de->bse', x, Wg)
        top_vals, top_idx = jax.lax.top_k(logits, TOP_K)
        probs = jax.nn.softmax(top_vals, axis=-1)
        onehot = jax.nn.one_hot(top_idx, E, dtype=x.dtype)
        weights = jnp.einsum('bsk,bske->bse', probs, onehot)
        out = jnp.zeros_like(x)
        for e in range(E):
            u = jnp.einsum('bsd,dh->bsh', x, W1[e])
            v = jnp.einsum('bsd,dh->bsh', x, W2[e])
            h = u * jax.nn.sigmoid(u) * v
            y = jnp.einsum('bsh,hd->bsd', h, W3[e])
            out = out + y * weights[..., e][..., None]
        return out

    def _L1_xattn_ref(decoder_input, encoder_output, W_q, W_k, W_v, W_o, b_o):
        import jax, jax.numpy as jnp
        import numpy as np
        EMBED = 128
        HEADS = 16
        HEAD_DIM = EMBED // HEADS
        B, Sd, E = decoder_input.shape
        Se = encoder_output.shape[1]
        Q = (decoder_input @ W_q).reshape(B, Sd, HEADS, HEAD_DIM)
        K = (encoder_output @ W_k).reshape(B, Se, HEADS, HEAD_DIM)
        V = (encoder_output @ W_v).reshape(B, Se, HEADS, HEAD_DIM)
        scores = jnp.einsum('bqhd,bkhd->bhqk', Q, K) / jnp.sqrt(jnp.float32(HEAD_DIM))
        attn = jax.nn.softmax(scores, axis=-1)
        out = jnp.einsum('bhqk,bkhd->bqhd', attn, V).reshape(B, Sd, E)
        return out @ W_o + b_o

    def _L1_ffn_ref(x, kernel, input_scale, kernel_scale, bias):
        import jax, jax.numpy as jnp
        import numpy as np
        FEATURES = 128
        D_IN = 128

        def fp8_gemm_optimized(x, input_scale, kernel, kernel_scale):
            s_in = input_scale[0]
            s_k = kernel_scale[0]
            x_q = (x.astype(jnp.float32) / s_in).astype(jnp.float8_e4m3fn)
            k_q = (kernel.astype(jnp.float32) / s_k).astype(jnp.float8_e4m3fn)
            y = jnp.dot(x_q.astype(jnp.float32), k_q.astype(jnp.float32), preferred_element_type=jnp.float32)
            return y * (s_in * s_k)
        dtype = jnp.bfloat16
        x = x.astype(dtype)
        orig_shape = x.shape
        x2 = x.reshape(-1, x.shape[-1])
        y = fp8_gemm_optimized(x2, input_scale, kernel, kernel_scale)
        y = y.astype(dtype) + bias
        return y.reshape(orig_shape[:-1] + (FEATURES,))
    x = x + _L0_xattn_ref(_layernorm(x, axis=-1), ctx_1024, L0_xattn_w_cq, L0_xattn_b_cq, L0_xattn_w_c, L0_xattn_b_c, L0_xattn_w_q, L0_xattn_b_q, L0_xattn_W_l, L0_xattn_b_l)
    x = x + _L0_ffn_ref(_layernorm(x, axis=-1), L0_ffn_Wg, L0_ffn_W1, L0_ffn_W2, L0_ffn_W3)
    x = x + _L1_xattn_ref(_layernorm(x, axis=-1), ctx_1024, L1_xattn_W_q, L1_xattn_W_k, L1_xattn_W_v, L1_xattn_W_o, L1_xattn_b_o)
    x = x + _L1_ffn_ref(_layernorm(x, axis=-1), L1_ffn_kernel, L1_ffn_input_scale, L1_ffn_kernel_scale, L1_ffn_bias)
    return x

_drawn_inputs = setup_inputs


def setup_inputs(seed=0):
    import zlib

    import numpy as np

    out = dict(_drawn_inputs(seed))
    spreads = {'L1_ffn_bias': (0.0, 0.1)}
    factors = {'L0_ffn_Wg': 6.845,
     'L0_ffn_W1': 6.284,
     'L0_ffn_W2': 6.245,
     'L0_ffn_W3': 6.283,
     'L1_xattn_b_o': 4.471}
    for name, (base, spread) in spreads.items():
        noise = np.random.default_rng([zlib.crc32(name.encode()), seed]).standard_normal(out[name].shape)
        drawn = base * np.exp(spread * noise) if base else spread * noise
        out[name] = jnp.asarray(drawn.astype(out[name].dtype))
    for name, factor in factors.items():
        out[name] = (out[name] * factor).astype(out[name].dtype)
    return out
```

```python
import concourse.bass as bass
from concourse import mybir
from contextlib import ExitStack

P = 128
BATCH, SEQ = 4, 256
TOK = BATCH * SEQ
NT = TOK // P
TPB = SEQ // P
HALF = TOK // 2
TPH = NT // 2
E, HID = 8, 256
HB = HID // P
UNITS = 2 * E
HEADS, HD = 16, 8
HPG = 4
G = HEADS // HPG
QUAD = 32
SHIFT_ROW = 24
EPS = 1e-5
ATT_SCALE = HD ** -0.5
C_AQ, C_AK, C_ONE, C_IOTA, C_ID = 0, 1, 2, 3, 3 + E
N_CONST = C_ID + P
S_WCQ, S_WQ, S_WC, S_B, S_SIN, S_SK, N_SMALL = 0, 1, 2, 3, 6, 7, 8


def build(nc, x_d, ctx_d, ctxT_d, small_d, const_d, wl_d, bl_d, wg_d, w12_d, w3_d,
          wq_d, wk_d, wv_d, wo_d, bo_d, fk_d, fb_d, out_d):
    fp32, r32 = mybir.dt.float32, mybir.dt.float32r
    bf16, fp16 = mybir.dt.bfloat16, mybir.dt.float16
    i32, u32 = mybir.dt.int32, mybir.dt.uint32
    ALU = mybir.AluOpType
    ACT = mybir.ActivationFunctionType
    AX = mybir.AxisListType

    stack = ExitStack()
    with stack:
        def sb(name, shape, dt=fp32):
            return stack.enter_context(nc.sbuf_tensor(name, shape, dt))

        def sem(name):
            return stack.enter_context(nc.semaphore(name))

        def plain(ap):
            return ap.bitcast(fp32)

        const = sb("const", [P, N_CONST])
        small = sb("small", [P, N_SMALL])
        ident = const[:, C_ID:C_ID + P]
        ident16 = sb("ident16", [P, P], bf16)
        expo = sb("expo", [P, NT])
        wl = sb("wl", [P, 4, P])
        bl = sb("bl", [P, P])
        wg = sb("wg", [P, E])
        wgs = sb("wgs", [P, 2, E], r32)
        raw = sb("raw", [P, E * 2 * HID + E * HB * P])
        w12raw = raw[:, 0:E * 2 * HID].rearrange("p (e c) -> p e c", e=E)
        w3raw = raw[:, E * 2 * HID:].rearrange("p (e c) -> p e c", e=E)
        w12 = sb("w12", [P, E, 2, 2 * HID], r32)
        w3 = sb("w3", [P, E, 2, HB * P], r32)
        w12s = sb("w12s", [P, 2, 2, 2 * HID], r32)
        wqkraw = sb("wqkraw", [P, 2, G * P])
        wqk = sb("wqk", [P, 2, 2, G * P], r32)
        wv = sb("wv", [P, P])
        wo = sb("wo", [P, P])
        bo = sb("bo", [P, P])
        fk = sb("fk", [P, P], bf16)
        fb = sb("fb", [P, P], bf16)

        xs = sb("xs", [P, NT, P])
        xn = sb("xn", [P, NT, P])
        xT = sb("xT", [P, 2, TOK], r32)
        ctx = sb("ctx", [P, NT, P])
        ctxT = sb("ctxT", [P, TOK])
        ctxTs = sb("ctxTs", [P, 2, TOK], r32)
        stats = sb("stats", [P, NT, 6])
        mv = sb("mv", [P, NT, 2])
        vpe = sb("vpe", [P, NT])
        rstd = sb("rstd", [P, NT])

        cT = sb("cT", [P, TOK])
        cpT = sb("cpT", [P, TOK])
        att = sb("att", [P, NT, SEQ])
        attT = sb("attT", [P, BATCH, TPB, SEQ])
        c2qT = cpT
        ccT = sb("ccT", [P, TOK])
        nmax = sb("nmax", [P, NT])
        rsum = sb("rsum", [P, NT])
        rinv = sb("rinv", [P, NT])
        bsum = sb("bsum", [P, 2])
        cv = sb("cv", [P, NT])
        bnmax = sb("bnmax", [1, BATCH])
        brow = ccT[0:1, :]
        bden = sb("bden", [1, 2 * BATCH])
        bcol = sb("bcol", [P, NT])
        q2c = sb("q2c", [P, BATCH])
        w14 = sb("w14", [P, BATCH, P])

        logit = sb("logit", [P, NT, E])
        top = sb("top", [P, NT, 8])
        topi = sb("topi", [P, NT, 8], u32)
        topf = sb("topf", [P, NT, 2])
        gap = sb("gap", [P, 4, NT])
        route = sb("route", [P, 3, NT, E])
        rw = sb("rw", [P, NT, E])
        att_flat = att[:, :, :].rearrange("p t q -> p (t q)")
        tanhs = att_flat[:, 0:TOK].rearrange("p (k t) -> p k t", k=HB)
        gated = att_flat[:, TOK:2 * TOK].rearrange("p (k t) -> p k t", k=HB)
        hid = attT[:, 0:2, :, :].rearrange("p a b c -> p a (b c)")
        hids = sb("hids", [P, 2, 2, HB, HALF], r32)

        vall = sb("vall", [P, NT, P])
        vones = sb("vones", [P, TPB, HEADS, QUAD])
        w12_flat = w12[:, :, :, :].rearrange("p e s c -> p (e s c)")
        km = w12_flat[:, 0:G * HPG * SEQ].rearrange("p (g h k) -> p g h k", g=G, h=HPG)
        qs, qa = (w12_flat[:, (G * HPG + G * n) * SEQ:(G * HPG + G * (n + 1)) * SEQ]
                  .rearrange("p (g q) -> p g q", g=G) for n in range(2))
        N_PROBS = HPG * TPB * SEQ
        probs = raw[:, 0:2 * N_PROBS].rearrange("p (u h k q) -> p u h k q", u=2, h=HPG, k=TPB)
        rest = raw[:, 2 * N_PROBS:]
        ks = rest[:, 0:2 * SEQ].rearrange("p (u k) -> p u k", u=2)
        hiQ = rest[:, 2 * SEQ:3 * SEQ]
        hiK = rest[:, 3 * SEQ:4 * SEQ]
        os_ = rest[:, 4 * SEQ:(4 + G) * SEQ].rearrange("p (g q) -> p g q", g=G)
        negm = sb("negm", [P, TPB, P])
        den = sb("den", [P, TPB, G, HPG])
        ao = sb("ao", [P, TPB, P])
        aoT = sb("aoT", [P, SEQ])

        rs = sb("rs", [P, 3])
        f16, xq = (cpT[:, n * HALF:(n + 1) * HALF].bitcast(bf16) for n in range(2))
        xqT, fovf = ctxT[:, 0:HALF].bitcast(bf16), ctxT[:, HALF:TOK].bitcast(fp16)
        vflat = vall[:, :, :].rearrange("p t d -> p (t d)")
        yb, yz = (vflat[:, n * HALF:(n + 1) * HALF].bitcast(bf16) for n in range(2))
        fv = ccT
        fe = attT[:, 0:2, :, :].rearrange("p a b c -> p (a b c)")
        fq = attT[:, 2:4, :, :].rearrange("p a b c -> p (a b c)")
        kq = sb("kq", [P, P], bf16)
        res = cT[:, :].rearrange("p (t d) -> p t d", t=NT)

        bk = [stack.enter_context(nc.psum_tensor(f"bank{i}", [P, 512], fp32)) for i in range(8)]

        names = """ld_x ld_ctx ld_par ld_w ld_att stored
          setup ident16_s v_zero km_zero km_free split12 split3 ctx_hi ctx_lo wqk_hi wqk_lo wg_hi wg_lo v_ps v_ev bl_added bo_added
          st1 ag1 ve1 rs1 ln1 st2 ag2 ve2 rs2 ln2 st3 ag3 ve3 rs3 ln3 st4 ag4 ve4 rs4 ln4
          cT_ps cT_ev cpT_ev cw_ps s_ps s_max s_exp s_rinv s_norm aT_ps aT_ev c2q_ps c2q_ev cc_ev
          bsum_s cv_s row_ps row_max row_exp row_inv bcol_ps bcol_ev q2c_ps q2c_ev w14_s z_ps z_add
          xT_ps xT_hi xT_lo logit_ps logit_ev top_s topi_s gap_s gap_exp route_s
          staged0 staged1 uv_ps tanh_s gate_s hid_s hid_hi hid_lo y_ps y_acc
          x3T_ps x3T_hi x3T_lo proj_ps q_hi k_hi qs_s ks_s km_s s1_ps s1_max mT_ps qa_s s2_ps p_s
          v_s pv_ps o_ev oT_ps den_s ao_s aoT_ps aoT_ev wo_ps x3_s
          rs_s kq_s f_s fT_ps fT_ev f_ps y_s out_s""".split()
        S = {n: sem(n) for n in names}

        block = stack.enter_context(nc.Block())

        @block.sync
        def _(sp):
            sp.dma_start(xs[:, :, :], x_d).then_inc(S["ld_x"], 16)
            sp.dma_start(ctxT[:, :], ctxT_d).then_inc(S["ld_ctx"], 16)
            sp.dma_start(ctx[:, :, :], ctx_d).then_inc(S["ld_ctx"], 16)
            sp.dma_start(wl[:, :, :], wl_d).then_inc(S["ld_par"], 16)
            sp.dma_start(w12raw, w12_d).then_inc(S["ld_w"], 16)
            sp.dma_start(w3raw, w3_d).then_inc(S["ld_w"], 16)

            def stage(e, parity, reused):
                if reused:
                    sp.wait_ge(S["uv_ps"], 2 * HB * (e - 1))
                src = w12[:, e:e + 1, :, :] if isinstance(e, int) else w12[:, bass.ds(e, 1), :, :]
                sp.dma_start(plain(w12s[:, parity:parity + 1, :, :]), plain(src)).then_inc(S[f"staged{parity}"], 16)

            sp.wait_ge(S["split12"], 2 * E)
            stage(0, 0, False)
            stage(1, 1, False)
            with sp.Fori(1, E // 2) as i:
                stage(2 * i, 0, True)
                stage(2 * i + 1, 1, True)

            for h in range(2):
                sp.wait_ge(S["out_s"], h + 1)
                sp.dma_start(out_d[:, h * TPH:(h + 1) * TPH, :], res[:, h * TPH:(h + 1) * TPH, :])\
                    .then_inc(S["stored"], 16)
            sp.wait_ge(S["stored"], 32)

        @block.gpsimd
        def _(pool):
            pool.memset(expo[:, :], -0.5)
            pool.memset(negm[:, :, :], 0.0)
            pool.memset(vones[:, :, :, :], 0.0).then_inc(S["v_zero"], 1)
            pool.wait_ge(S["v_zero"], 1)
            pool.memset(vones[:, :, :, HD:HD + 1], 1.0).then_inc(S["setup"], 1)

            def inverse_deviation(n):
                pool.wait_ge(S[f"ag{n}"], NT)
                if n > 1:
                    pool.wait_ge(S[f"rs{n - 1}"], 1)
                pool.tensor_scalar(vpe[:, :], mv[:, :, 1], EPS, None, ALU.add).then_inc(S[f"ve{n}"], 1)
                pool.wait_ge(S[f"ve{n}"], 1)
                pool.tensor_tensor(rstd[:, :], vpe[:, :], expo[:, :], ALU.pow).then_inc(S[f"rs{n}"], 1)

            pool.wait_ge(S["setup"], 1)
            inverse_deviation(1)
            pool.wait_ge(S["ld_w"], 32)
            for e in range(E):
                pool.tensor_copy(w12[:, e, 0, :], w12raw[:, e, :]).then_inc(S["split12"], 1)
                pool.wait_ge(S["split12"], 2 * e + 1)
                pool.tensor_tensor(w12[:, e, 1, :], w12raw[:, e, :], plain(w12[:, e, 0, :]), ALU.subtract)\
                    .then_inc(S["split12"], 1)
            for e in range(E):
                pool.tensor_copy(w3[:, e, 0, :], w3raw[:, e, :]).then_inc(S["split3"], 1)
                pool.wait_ge(S["split3"], 2 * e + 1)
                pool.tensor_tensor(w3[:, e, 1, :], w3raw[:, e, :], plain(w3[:, e, 0, :]), ALU.subtract)\
                    .then_inc(S["split3"], 1)
            inverse_deviation(2)

            def hidden_lo(n, p, first):
                for k in range(HB):
                    pool.wait_ge(S["hid_hi"], HB * n + k + 1)
                    if not first:
                        pool.wait_ge(S["y_ps"], n - 1)
                    pool.tensor_tensor(hids[:, p, 1, k, :], hid[:, k, :], plain(hids[:, p, 0, k, :]),
                                       ALU.subtract).then_inc(S["hid_lo"], 1)

            for n in range(4):
                hidden_lo(n, n % 2, n < 2)
            with pool.Fori(1, UNITS // 4) as i:
                for j in range(4):
                    hidden_lo(4 * i + j, j % 2, False)
            for parity in range(2):
                pool.wait_ge(S[f"staged{parity}"], 16 * E // 2)
            pool.memset(km.bitcast(i32), 0).then_inc(S["km_zero"], 1)
            inverse_deviation(3)

            def masked_keys(m, g, reused):
                pool.wait_ge(S["ks_s"], m + 1)
                if reused:
                    pool.wait_ge(S["s2_ps"], 2 * (m - 3))
                pool.sem_inc(S["km_free"], 1)
                pool.wait_ge(S["km_zero"], 1)
                for j in range(HPG):
                    rows = slice(QUAD * j, QUAD * (j + 1))
                    pool.tensor_copy(km[rows, g, j, :], ks[rows, g % 2, :]).then_inc(S["km_s"], 1)
                    pool.wait_ge(S["km_s"], HPG * m + j + 1)
                    pool.sem_inc(S["km_free"], 1)

            def values(b, first):
                if not first:
                    pool.wait_ge(S["pv_ps"], G * b)
                pool.wait_ge(S["v_ev"], 2)
                src = vall[:, 0:TPB, :] if first else vall[:, bass.ds(TPB * b, TPB), :]
                pool.tensor_copy(vones[:, :, :, 0:HD], src.rearrange("p t (h d) -> p t h d", h=HEADS))\
                    .then_inc(S["v_s"], 1)

            def pool_batch(b, first, last):
                for g in range(G):
                    if not (last and g >= 2):
                        masked_keys(G * b + g + 2, (g + 2) % G, not (first and g < 2))
                    if g == 0:
                        values(b, first)

            masked_keys(0, 0, False)
            masked_keys(1, 1, False)
            pool_batch(0, True, False)
            with pool.Fori(1, BATCH - 1) as b:
                pool_batch(b, False, False)
            pool_batch(BATCH - 1, False, True)
            inverse_deviation(4)

        @block.scalar
        def _(act):
            act.dma_start(const[:, :], const_d).then_inc(S["ld_par"], 16)
            act.dma_start(small[:, :], small_d).then_inc(S["ld_par"], 16)
            act.dma_start(bl[:, :], bl_d).then_inc(S["ld_par"], 16)
            act.dma_start(wg[:, :], wg_d).then_inc(S["ld_par"], 16)
            for dst, src in ((wqkraw[:, 0, :], wq_d), (wqkraw[:, 1, :], wk_d), (wv[:, :], wv_d),
                             (wo[:, :], wo_d), (bo[:, :], bo_d), (fk[:, :], fk_d), (fb[:, :], fb_d)):
                act.dma_start(dst, src).then_inc(S["ld_att"], 16)
            act.wait_ge(S["ld_par"], 80)
            act.copy(ident16[:, :], ident).then_inc(S["ident16_s"], 1)

            for h in range(2):
                cols = slice(h * HALF, (h + 1) * HALF)
                act.wait_ge(S["cT_ps"], h + 1)
                act.activation(cpT[:, cols], bk[h][:, :], ACT.Identity, scale=small[:, S_WCQ:S_WCQ + 1],
                               bias=small[:, S_WQ:S_WQ + 1]).then_inc(S["cpT_ev"], 1)
                act.copy(cT[:, cols], bk[h][:, :]).then_inc(S["cT_ev"], 1)
            for t in range(NT):
                act.wait_ge(S["s_max"], t // TPB + 1)
                c0 = (t % TPB) * SEQ
                act.activation(att[:, t, :], bk[2 + t // TPB][:, c0:c0 + SEQ], ACT.Exp,
                               bias=nmax[:, t:t + 1], accum_out=rsum[:, t:t + 1]).then_inc(S["s_exp"], 1)
            act.wait_ge(S["ld_ctx"], 32)
            act.copy(ctxTs[:, 0, :], ctxT[:, :]).then_inc(S["ctx_hi"], 1)
            act.wait_ge(S["ld_att"], 7 * 16)
            act.copy(wqk[:, 0, :, :], wqkraw[:, :, :]).then_inc(S["wqk_hi"], 1)
            act.copy(wgs[:, 0, :], wg[:, :]).then_inc(S["wg_hi"], 1)
            for b in range(BATCH):
                act.wait_ge(S["row_max"], b // 2 + 1)
                c0 = (b % 2) * SEQ
                act.activation(brow[:, b * SEQ:(b + 1) * SEQ], bk[b // 2][0:1, c0:c0 + SEQ], ACT.Exp,
                               bias=bnmax[:, b:b + 1], accum_out=bden[:, b:b + 1]).then_inc(S["row_exp"], 1)
            for b in range(BATCH):
                act.wait_ge(S["aT_ps"], b + 1)
                act.copy(attT[:, b, :, :], bk[2 + b][:, :]).then_inc(S["aT_ev"], 1)
            act.wait_ge(S["bcol_ps"], 1)
            act.copy(bcol[:, :], bk[7][:, 16:16 + NT]).then_inc(S["bcol_ev"], 1)
            for h in range(2):
                act.wait_ge(S["c2q_ps"], h + 1)
                act.copy(c2qT[:, h * HALF:(h + 1) * HALF], bk[h][:, :]).then_inc(S["c2q_ev"], 1)
            act.wait_ge(S["q2c_ps"], 1)
            act.copy(q2c[:, :], bk[7][:, 32:32 + BATCH]).then_inc(S["q2c_ev"], 1)
            for h in range(2):
                act.wait_ge(S["v_ps"], h + 1)
                act.copy(vall[:, h * TPH:(h + 1) * TPH, :], bk[2 + h][:, :]).then_inc(S["v_ev"], 1)
            for h in range(2):
                act.wait_ge(S["xT_ps"], h + 1)
                act.copy(xT[:, 0, h * HALF:(h + 1) * HALF], bk[h][:, :]).then_inc(S["xT_hi"], 1)
            act.wait_ge(S["gap_s"], 1)
            act.activation(gap[:, 1, :], gap[:, 0, :], ACT.Exp).then_inc(S["gap_exp"], 1)

            def hidden(n, p, first, second):
                for k in range(HB):
                    act.wait_ge(S["uv_ps"], HB * n + k + 1)
                    if not first:
                        act.wait_ge(S["gate_s"], HB * (n - 1) + k + 1)
                    act.activation(tanhs[:, k, :], bk[2 * k][:, :], ACT.Tanh, scale=0.5).then_inc(S["tanh_s"], 1)
                for k in range(HB):
                    act.wait_ge(S["hid_s"], HB * n + k + 1)
                    if not (first or second):
                        act.wait_ge(S["y_ps"], n - 1)
                    act.copy(hids[:, p, 0, k, :], hid[:, k, :]).then_inc(S["hid_hi"], 1)

            for n in range(4):
                hidden(n, n % 2, n == 0, n == 1)
            with act.Fori(1, UNITS // 4) as i:
                for j in range(4):
                    hidden(4 * i + j, j % 2, False, False)
            for h in range(2):
                act.wait_ge(S["x3T_ps"], h + 1)
                act.copy(xT[:, 0, h * HALF:(h + 1) * HALF], bk[h][:, :]).then_inc(S["x3T_hi"], 1)

            def proj_hi(m, first):
                act.wait_ge(S["proj_ps"], m + 1)
                if not first:
                    act.wait_ge(S["ks_s"], m)
                act.copy(hiQ.bitcast(r32), bk[0][:, 0:SEQ]).then_inc(S["q_hi"], 1)
                act.activation(hiK.bitcast(r32), bk[0][:, SEQ:2 * SEQ], ACT.Identity,
                               bias=const[:, C_ONE:C_ONE + 1]).then_inc(S["k_hi"], 1)

            def exps(m, g, first):
                for r in range(2):
                    act.wait_ge(S["s2_ps"], 2 * m + r + 1)
                    if not first:
                        act.wait_ge(S["pv_ps"], m - 1)
                    for a in range(2):
                        ins = act.activation(probs[:, g % 2, 2 * r + a, :, :],
                                             bk[3 + 2 * r + a][:, :].rearrange("p (k q) -> p k q", k=TPB),
                                             ACT.Exp, scale=ATT_SCALE)
                    ins.then_inc(S["p_s"], 1)

            def o_copy(m, g):
                act.wait_ge(S["pv_ps"], m + 1)
                act.copy(os_[:, g, :], bk[7][:, SEQ:2 * SEQ]).then_inc(S["o_ev"], 1)

            def act_batch(b, first, last):
                for g in range(G):
                    m = G * b + g
                    if not (last and g >= 2):
                        proj_hi(m + 2, False)
                    if g == 2 and not first:
                        act.wait_ge(S["aoT_ps"], b)
                        act.copy(aoT[:, :], bk[7][:, 0:SEQ]).then_inc(S["aoT_ev"], 1)
                    exps(m, g, first and g < 2)
                    if not (first and g == 0):
                        o_copy(m - 1, (g - 1) % G)

            proj_hi(0, True)
            proj_hi(1, False)
            act_batch(0, True, False)
            with act.Fori(1, BATCH - 1) as b:
                act_batch(b, False, False)
            act_batch(BATCH - 1, False, True)
            o_copy(G * BATCH - 1, G - 1)
            act.wait_ge(S["aoT_ps"], BATCH)
            act.copy(aoT[:, :], bk[7][:, 0:SEQ]).then_inc(S["aoT_ev"], 1)

            for h in range(2):
                act.wait_ge(S["fT_ps"], h + 1)
                act.copy(xqT[:, h * HALF:(h + 1) * HALF], bk[h][:, 0:HALF // 2].bitcast(bf16)).then_inc(S["fT_ev"], 1)

        @block.vector
        def _(dve):
            def norm(n, ready):
                if n > 1:
                    dve.wait_ge(S[f"ln{n - 1}"], NT)
                for t in range(NT):
                    ready(t)
                    dve.bn_stats(stats[:, t, :], xs[:, t, :]).then_inc(S[f"st{n}"], 1)
                for t in range(NT):
                    dve.wait_ge(S[f"st{n}"], t + 1)
                    dve.bn_aggr(mv[:, t, :], stats[:, t, :]).then_inc(S[f"ag{n}"], 1)
                dve.wait_ge(S[f"ag{n}"], NT)
                dve.wait_ge(S[f"rs{n}"], 1)
                for t in range(NT):
                    dve.tensor_scalar(xn[:, t, :], xs[:, t, :], mv[:, t, 0:1], rstd[:, t:t + 1],
                                      ALU.subtract, ALU.mult).then_inc(S[f"ln{n}"], 1)

            dve.wait_ge(S["ld_x"], 16)
            norm(1, lambda t: None)
            dve.wait_ge(S["ln1"], NT)
            dve.wait_ge(S["ld_par"], 80)
            dve.tensor_tensor(xs[:, :, :], xs[:, :, :], bl[:, :].unsqueeze(1).broadcast_to([P, NT, P]),
                              ALU.add).then_inc(S["bl_added"], 1)
            dve.tensor_tensor(bsum[:, 0:1], small[:, S_B:S_B + 1], small[:, S_B + 1:S_B + 2], ALU.add)\
                .then_inc(S["bsum_s"], 1)
            dve.wait_ge(S["bsum_s"], 1)
            dve.tensor_tensor(bsum[:, 1:2], bsum[:, 0:1], small[:, S_B + 2:S_B + 3], ALU.add)\
                .then_inc(S["bsum_s"], 1)
            for b in range(BATCH):
                dve.wait_ge(S["s_ps"], b + 1)
                dve.tensor_reduce(nmax[:, TPB * b:TPB * (b + 1)], bk[2 + b][:, :].rearrange("p (t q) -> p t q", t=TPB),
                                  AX.X, ALU.max, negate=True).then_inc(S["s_max"], 1)
            dve.wait_ge(S["cw_ps"], 1)
            dve.wait_ge(S["s_max"], BATCH)
            dve.wait_ge(S["bsum_s"], 2)
            dve.scalar_tensor_tensor(cv[:, :], bk[7][:, 0:NT], bsum[:, 1:2], nmax[:, :], ALU.add, ALU.subtract)\
                .then_inc(S["cv_s"], 1)
            for t in range(NT):
                dve.wait_ge(S["s_exp"], t + 1)
                dve.reciprocal(rinv[:, t:t + 1], rsum[:, t:t + 1]).then_inc(S["s_rinv"], 1)
                dve.wait_ge(S["s_rinv"], t + 1)
                dve.tensor_scalar(att[:, t, :], att[:, t, :], rinv[:, t:t + 1], None, ALU.mult)\
                    .then_inc(S["s_norm"], 1)
                if t % 4 == 1:
                    h = t // 4
                    dve.wait_ge(S["row_ps"], h + 1)
                    dve.tensor_reduce(bnmax[:, 2 * h:2 * h + 2], bk[h][0:1, :].rearrange("p (b c) -> p b c", b=2),
                                      AX.X, ALU.max, negate=True).then_inc(S["row_max"], 1)
            dve.wait_ge(S["row_exp"], BATCH)
            dve.reciprocal(bden[:, BATCH:2 * BATCH], bden[:, 0:BATCH]).then_inc(S["row_inv"], 1)
            dve.wait_ge(S["ctx_hi"], 1)
            dve.tensor_tensor(ctxTs[:, 1, :], ctxT[:, :], plain(ctxTs[:, 0, :]), ALU.subtract).then_inc(S["ctx_lo"], 1)
            dve.wait_ge(S["wqk_hi"], 1)
            dve.tensor_tensor(wqk[:, 1, :, :], wqkraw[:, :, :], plain(wqk[:, 0, :, :]), ALU.subtract)\
                .then_inc(S["wqk_lo"], 1)
            dve.wait_ge(S["wg_hi"], 1)
            dve.tensor_tensor(wgs[:, 1, :], wg[:, :], plain(wgs[:, 0, :]), ALU.subtract).then_inc(S["wg_lo"], 1)
            for h in range(2):
                cols = slice(h * HALF, (h + 1) * HALF)
                dve.wait_ge(S["c2q_ev"], h + 1)
                dve.tensor_tensor(ccT[:, cols], c2qT[:, cols], cT[:, cols], ALU.mult).then_inc(S["cc_ev"], 1)
            dve.wait_ge(S["q2c_ev"], 1)
            for b in range(BATCH):
                dve.scalar_tensor_tensor(w14[:, b, :], wl[:, 3, :], q2c[:, b:b + 1], wl[:, 0, :], ALU.mult, ALU.add)\
                    .then_inc(S["w14_s"], 1)
            dve.wait_ge(S["bl_added"], 1)
            for h in range(2):
                dve.wait_ge(S["z_ps"], h + 1)
                dve.tensor_tensor(xs[:, h * TPH:(h + 1) * TPH, :], xs[:, h * TPH:(h + 1) * TPH, :],
                                  bk[4 + h][:, :].rearrange("p (t d) -> p t d", t=TPH), ALU.add)\
                    .then_inc(S["z_add"], 1)
            norm(2, lambda t: dve.wait_ge(S["z_add"], t // TPH + 1))
            for h in range(2):
                cols = slice(h * HALF, (h + 1) * HALF)
                dve.wait_ge(S["xT_hi"], h + 1)
                dve.tensor_tensor(xT[:, 1, cols], bk[h][:, :], plain(xT[:, 0, cols]), ALU.subtract)\
                    .then_inc(S["xT_lo"], 1)

            dve.wait_ge(S["logit_ps"], 1)
            dve.tensor_copy(logit[:, :, :], bk[7][:, 0:NT * E].rearrange("p (t e) -> p t e", t=NT))\
                .then_inc(S["logit_ev"], 1)
            dve.wait_ge(S["logit_ev"], 1)
            for t in range(NT):
                dve.max(top[:, t, :], logit[:, t, :]).then_inc(S["top_s"], 1)
            for t in range(NT):
                dve.wait_ge(S["top_s"], t + 1)
                dve.max_index(topi[:, t, :], top[:, t, :], logit[:, t, :]).then_inc(S["topi_s"], 1)
            dve.wait_ge(S["top_s"], NT)
            dve.tensor_tensor(gap[:, 0, :], top[:, :, 1], top[:, :, 0], ALU.subtract).then_inc(S["gap_s"], 1)
            dve.wait_ge(S["topi_s"], NT)
            dve.tensor_copy(topf[:, :, :], topi[:, :, 0:2]).then_inc(S["route_s"], 1)
            dve.wait_ge(S["gap_exp"], 1)
            dve.tensor_scalar(gap[:, 2, :], gap[:, 1, :], 1.0, 2.0, ALU.add, ALU.mult).then_inc(S["route_s"], 1)
            dve.wait_ge(S["route_s"], 2)
            dve.reciprocal(gap[:, 2, :], gap[:, 2, :]).then_inc(S["route_s"], 1)
            dve.wait_ge(S["route_s"], 3)
            dve.tensor_tensor(gap[:, 3, :], gap[:, 1, :], gap[:, 2, :], ALU.mult).then_inc(S["route_s"], 1)
            iota = const[:, C_IOTA:C_IOTA + E].unsqueeze(1).broadcast_to([P, NT, E])
            for r in range(2):
                dve.wait_ge(S["route_s"], 4)
                dve.tensor_tensor(route[:, r, :, :], iota, topf[:, :, r:r + 1].broadcast_to([P, NT, E]),
                                  ALU.is_equal).then_inc(S["route_s"], 1)
            for r in range(2):
                dve.wait_ge(S["route_s"], 5 + r)
                dve.tensor_tensor(route[:, r, :, :], route[:, r, :, :],
                                  gap[:, 2 + r, :].unsqueeze(2).broadcast_to([P, NT, E]), ALU.mult)\
                    .then_inc(S["route_s"], 1)
            dve.wait_ge(S["route_s"], 8)
            dve.tensor_tensor(rw[:, :, :], route[:, 0, :, :], route[:, 1, :, :], ALU.add).then_inc(S["route_s"], 1)

            def hidden(n, first):
                for k in range(HB):
                    dve.wait_ge(S["tanh_s"], HB * n + k + 1)
                    if not first:
                        dve.wait_ge(S["hid_s"], HB * (n - 1) + k + 1)
                    dve.scalar_tensor_tensor(gated[:, k, :], tanhs[:, k, :], 1.0, bk[2 * k][:, :],
                                             ALU.add, ALU.mult).then_inc(S["gate_s"], 1)
                for k in range(HB):
                    dve.wait_ge(S["gate_s"], HB * n + k + 1)
                    if not first:
                        dve.wait_ge(S["hid_lo"], HB * (n - 1) + k + 1)
                    dve.tensor_tensor(hid[:, k, :], gated[:, k, :], bk[2 * k + 1][:, :], ALU.mult)\
                        .then_inc(S["hid_s"], 1)

            def accumulate(n, e, h, first):
                dve.wait_ge(S["y_ps"], n + 1)
                if not first:
                    dve.wait_ge(S["y_acc"], TPH * (n - 1))
                for t in range(TPH):
                    tile = h * TPH + t
                    weight = rw[:, tile, e:e + 1] if isinstance(e, int) else rw[:, tile, bass.ds(e, 1)]
                    dve.scalar_tensor_tensor(xs[:, tile, :], bk[4 + h][:, t * P:(t + 1) * P], weight,
                                             xs[:, tile, :], ALU.mult, ALU.add).then_inc(S["y_acc"], 1)

            dve.wait_ge(S["route_s"], 9)
            for n in range(4):
                hidden(n, n == 0)
                if n:
                    accumulate(n - 1, (n - 1) // 2, (n - 1) % 2, n < 3)
            with dve.Fori(1, UNITS // 4) as i:
                for j in range(4):
                    hidden(4 * i + j, False)
                    accumulate(4 * i + j - 1, 2 * i + (j - 1) // 2, (j - 1) % 2, False)
            accumulate(UNITS - 1, E - 1, 1, False)

            norm(3, lambda t: dve.wait_ge(S["y_acc"], TPH * UNITS - (TPH if t < TPH else 0) - (TPH - 1) + t % TPH))
            for h in range(2):
                cols = slice(h * HALF, (h + 1) * HALF)
                dve.wait_ge(S["x3T_hi"], h + 1)
                dve.tensor_tensor(xT[:, 1, cols], bk[h][:, :], plain(xT[:, 0, cols]), ALU.subtract)\
                    .then_inc(S["x3T_lo"], 1)
            dve.wait_ge(S["ld_att"], 7 * 16)
            dve.tensor_tensor(xs[:, :, :], xs[:, :, :], bo[:, :].unsqueeze(1).broadcast_to([P, NT, P]),
                              ALU.add).then_inc(S["bo_added"], 1)

            def stacks(m, g, first):
                dve.wait_ge(S["q_hi"], m + 1)
                dve.wait_ge(S["k_hi"], m + 1)
                if not first:
                    dve.wait_ge(S["s1_ps"], 4 * (m - 3))
                    dve.wait_ge(S["qa_s"], m - 3)
                dve.scalar_tensor_tensor(qs[:, g, :], hiQ, const[:, C_AQ:C_AQ + 1],
                                         bk[0][:, 0:SEQ], ALU.mult, ALU.add).then_inc(S["qs_s"], 1)
                if not first or g >= 2:
                    dve.wait_ge(S["km_s"], HPG * (m - 1))
                dve.scalar_tensor_tensor(ks[:, g % 2, :], hiK, const[:, C_AK:C_AK + 1],
                                         bk[0][:, SEQ:2 * SEQ], ALU.mult, ALU.add).then_inc(S["ks_s"], 1)

            def maxima(m, pieces, first):
                for r in pieces:
                    dve.wait_ge(S["s1_ps"], 4 * m + r + 1)
                    if not first:
                        dve.wait_ge(S["mT_ps"], m)
                    c0 = SHIFT_ROW + 2 * QUAD * (r % 2)
                    dve.tensor_reduce(negm[:, r // 2, c0:c0 + QUAD + 1:QUAD],
                                      bk[1 + r % 2][:, :].rearrange("p (h k) -> p h k", h=2),
                                      AX.X, ALU.max, negate=True).then_inc(S["s1_max"], 1)

            def shifted(m, g, first):
                dve.wait_ge(S["mT_ps"], m + 1)
                dve.wait_ge(S["qs_s"], m + 1)
                if not first:
                    dve.wait_ge(S["s2_ps"], 2 * (m - 3))
                dve.tensor_tensor(qa[:, g, :], bk[7][:, 0:SEQ], plain(qs[:, g, :]), ALU.add).then_inc(S["qa_s"], 1)

            def normalise(b):
                for t in range(TPB):
                    bank = bk[7] if t == 0 else bk[0]
                    heads = bank[:, :].rearrange("p (g h r) -> p g h r", g=G, h=HPG)
                    dve.wait_ge(S["oT_ps"], 2 * b + t + 1)
                    dve.reciprocal(den[:, t, :, :].unsqueeze(3), heads[:, :, :, HD:HD + 1]).then_inc(S["den_s"], 1)
                    dve.wait_ge(S["den_s"], 2 * b + t + 1)
                    dve.tensor_tensor(ao[:, t, :].rearrange("p (g h d) -> p g h d", g=G, h=HPG),
                                      heads[:, :, :, 0:HD], den[:, t, :, :].unsqueeze(3).broadcast_to([P, G, HPG, HD]),
                                      ALU.mult).then_inc(S["ao_s"], 1)

            def add_attention(b, tiles):
                dve.wait_ge(S["wo_ps"], b + 1)
                dve.tensor_tensor(xs[:, tiles, :], xs[:, tiles, :],
                                  bk[7][:, 0:SEQ].rearrange("p (t d) -> p t d", t=TPB), ALU.add)\
                    .then_inc(S["x3_s"], 1)

            def dve_batch(b, first, last):
                for g in range(G):
                    m = G * b + g
                    if g == 1 and not first:
                        normalise(b - 1)
                    more = not (last and g == G - 1)
                    if more:
                        maxima(m + 1, (0, 1), False)
                    if not (last and g >= 2):
                        stacks(m + 2, (g + 2) % G, first and g < 2)
                    if g == 3 and not first:
                        tiles = bass.ds(TPB * (b - 1), TPB) if not last else slice(TPB * (b - 1), TPB * b)
                        add_attention(b - 1, tiles)
                    if more:
                        maxima(m + 1, (2, 3), False)
                        shifted(m + 1, (g + 1) % G, first and g < 3)

            dve.wait_ge(S["bo_added"], 1)
            dve.wait_ge(S["setup"], 1)
            stacks(0, 0, True)
            stacks(1, 1, True)
            maxima(0, range(4), True)
            shifted(0, 0, True)
            dve_batch(0, True, False)
            with dve.Fori(1, BATCH - 1) as b:
                dve_batch(b, False, False)
            dve_batch(BATCH - 1, False, True)
            normalise(BATCH - 1)
            add_attention(BATCH - 1, slice(NT - TPB, NT))

            dve.reciprocal(rs[:, 0:2], small[:, S_SIN:S_SIN + 2]).then_inc(S["rs_s"], 1)
            dve.tensor_tensor(rs[:, 2:3], small[:, S_SIN:S_SIN + 1], small[:, S_SK:S_SK + 1], ALU.mult)\
                .then_inc(S["rs_s"], 1)
            dve.wait_ge(S["rs_s"], 2)

            def to_e4m3(dst, src, inverse, v, e, q, ovf, count, base):
                def then(ins):
                    count[0] += 1
                    ins.then_inc(S[base], 1)
                    dve.wait_ge(S[base], count[0])

                then(dve.tensor_scalar(v, src, inverse, None, ALU.mult))
                then(dve.tensor_scalar(e.bitcast(i32), v.bitcast(i32), 0x7F800000, None, ALU.bitwise_and))
                then(dve.tensor_scalar(e, e, 2.0 ** -6, 1.5 * 2.0 ** 20, ALU.max, ALU.mult))
                then(dve.tensor_tensor(q, v, e, ALU.add))
                then(dve.tensor_tensor(q, q, e, ALU.subtract))
                then(dve.tensor_scalar(ovf, q, 144.0, None, ALU.mult))
                then(dve.tensor_tensor(ovf, ovf, ovf, ALU.subtract))
                then(dve.tensor_tensor(dst, q, ovf, ALU.add))

            kc = [0]
            to_e4m3(kq[:, :], fk[:, :], rs[:, 1:2], ccT[:, 0:P], ccT[:, P:2 * P], ccT[:, 2 * P:3 * P],
                    fovf[:, 0:P], kc, "kq_s")
            norm(4, lambda t: dve.wait_ge(S["x3_s"], t // TPB + 1))
            fc = [0]
            dve.wait_ge(S["ln4"], NT)
            flat = xn[:, :, :].rearrange("p t d -> p (t d)")
            for h in range(2):
                cols = slice(h * HALF, (h + 1) * HALF)
                dve.tensor_copy(f16[:, cols], flat[:, cols]).then_inc(S["f_s"], 1)
                fc[0] += 1
                dve.wait_ge(S["f_s"], fc[0])
                to_e4m3(xq[:, cols], f16[:, cols], rs[:, 0:1], fv[:, cols], fe[:, cols], fq[:, cols],
                        fovf[:, cols], fc, "f_s")
            for h in range(2):
                cols = slice(h * HALF, (h + 1) * HALF)
                tiles = slice(h * TPH, (h + 1) * TPH)
                dve.wait_ge(S["f_ps"], h + 1)
                dve.tensor_scalar(yb[:, cols], bk[2 + h][:, :], rs[:, 2:3], None, ALU.mult).then_inc(S["y_s"], 1)
                dve.wait_ge(S["y_s"], 2 * h + 1)
                dve.tensor_tensor(yz[:, cols].rearrange("p (t d) -> p t d", t=TPH),
                                  yb[:, cols].rearrange("p (t d) -> p t d", t=TPH),
                                  fb[:, :].unsqueeze(1).broadcast_to([P, TPH, P]), ALU.add).then_inc(S["y_s"], 1)
                dve.wait_ge(S["y_s"], 2 * h + 2)
                dve.tensor_tensor(res[:, tiles, :], xs[:, tiles, :], yz[:, cols].rearrange("p (t d) -> p t d", t=TPH),
                                  ALU.add).then_inc(S["out_s"], 1)

        @block.tensor
        def _(pe):
            def three(out, w, x, start, stop):
                pe.matmul(out, w[0], x[0], start=start, stop=False)
                pe.matmul(out, w[0], x[1], start=False, stop=False)
                return pe.matmul(out, w[1], x[0], start=False, stop=stop)

            def turn(ln, out):
                for h in range(2):
                    for t in range(TPH):
                        pe.wait_ge(S[ln], h * TPH + t + 1)
                        ins = pe.transpose(bk[h][:, t * P:(t + 1) * P], xn[:, h * TPH + t, :], ident)
                    ins.then_inc(S[out], 1)

            pe.wait_ge(S["ld_par"], 80)
            turn("ln1", "cT_ps")
            pe.wait_ge(S["ld_ctx"], 32)
            for b in range(BATCH):
                pe.wait_ge(S["cpT_ev"], b // 2 + 1)
                for t in range(TPB):
                    tile = b * TPB + t
                    ins = pe.matmul(bk[2 + b][:, t * SEQ:(t + 1) * SEQ], cpT[:, tile * P:(tile + 1) * P],
                                    ctxT[:, b * SEQ:(b + 1) * SEQ], start=True, stop=True)
                ins.then_inc(S["s_ps"], 1)
            pe.wait_ge(S["cT_ev"], 2)
            for t in range(NT):
                ins = pe.matmul(bk[7][:, t:t + 1], cT[:, t * P:(t + 1) * P], small[:, S_WC:S_WC + 1],
                                start=True, stop=True)
            ins.then_inc(S["cw_ps"], 1)
            pe.wait_ge(S["cv_s"], 1)
            for h in range(2):
                for t in range(TPH):
                    ins = pe.matmul(bk[h][0:1, t * P:(t + 1) * P], cv[:, h * TPH + t:h * TPH + t + 1], ident,
                                    start=True, stop=True)
                ins.then_inc(S["row_ps"], 1)
            for b in range(BATCH):
                for t in range(TPB):
                    tile = b * TPB + t
                    pe.wait_ge(S["s_norm"], b * TPB + TPB)
                    for q in range(TPB):
                        ins = pe.transpose(bk[2 + b][:, q * SEQ + t * P:q * SEQ + (t + 1) * P],
                                           att[:, tile, q * P:(q + 1) * P], ident)
                ins.then_inc(S["aT_ps"], 1)
            pe.wait_ge(S["row_inv"], 1)
            for t in range(NT):
                b = t // TPB
                ins = pe.matmul(bk[7][:, 16 + t:17 + t], brow[:, t * P:(t + 1) * P],
                                bden[:, BATCH + b:BATCH + b + 1], start=True, stop=True)
            ins.then_inc(S["bcol_ps"], 1)
            for b in range(BATCH):
                pe.wait_ge(S["aT_ev"], b + 1)
                for q in range(TPB):
                    ins = pe.matmul(bk[b // 2][:, (b % 2) * SEQ:(b % 2 + 1) * SEQ], ctx[:, b * TPB + q, :],
                                    attT[:, b, q, :], start=q == 0, stop=q == TPB - 1)
                if b % 2:
                    ins.then_inc(S["c2q_ps"], 1)
            pe.wait_ge(S["bcol_ev"], 1)
            for b in range(BATCH):
                for t in range(TPB):
                    tile = b * TPB + t
                    ins = pe.matmul(bk[7][:, 32 + b:33 + b], xn[:, tile, :], bcol[:, tile:tile + 1],
                                    start=t == 0, stop=t == TPB - 1)
            ins.then_inc(S["q2c_ps"], 1)
            pe.wait_ge(S["ld_att"], 7 * 16)
            for h in range(2):
                for t in range(TPH):
                    tile = h * TPH + t
                    ins = pe.matmul(bk[2 + h][:, t * P:(t + 1) * P], ctxT[:, tile * P:(tile + 1) * P], wv[:, :],
                                    start=True, stop=True)
                ins.then_inc(S["v_ps"], 1)
            for h in range(2):
                pe.wait_ge(S["cc_ev"], h + 1)
                for t in range(TPH):
                    tile = h * TPH + t
                    b = tile // TPB
                    out = bk[4 + h][:, t * P:(t + 1) * P]
                    cols = slice(tile * P, (tile + 1) * P)
                    pe.matmul(out, c2qT[:, cols], wl[:, 1, :], start=True, stop=False)
                    pe.matmul(out, ccT[:, cols], wl[:, 2, :], start=False, stop=False)
                    pe.wait_ge(S["w14_s"], b + 1)
                    ins = pe.matmul(out, cT[:, cols], w14[:, b, :], start=False, stop=True)
                ins.then_inc(S["z_ps"], 1)
            turn("ln2", "xT_ps")
            pe.wait_ge(S["wg_lo"], 1)
            for h in range(2):
                pe.wait_ge(S["xT_lo"], h + 1)
                for t in range(TPH):
                    tile = h * TPH + t
                    cols = slice(tile * P, (tile + 1) * P)
                    ins = three(bk[7][:, tile * E:(tile + 1) * E], (xT[:, 0, cols], xT[:, 1, cols]),
                                (wgs[:, 0, :], wgs[:, 1, :]), True, True)
            ins.then_inc(S["logit_ps"], 1)

            def up(n, pair, parity, h, first):
                if h == 0:
                    pe.wait_ge(S[f"staged{parity}"], 16 * pair + 16)
                cols = slice(h * HALF, (h + 1) * HALF)
                x = (xT[:, 0, cols], xT[:, 1, cols])
                for k in range(HB):
                    if not first:
                        pe.wait_ge(S["hid_s"], HB * (n - 1) + k + 1)
                    for w in range(2):
                        c0 = w * HID + k * P
                        ins = three(bk[2 * k + w][:, :], (w12s[:, parity, 0, c0:c0 + P], w12s[:, parity, 1, c0:c0 + P]),
                                    x, True, True)
                    ins.then_inc(S["uv_ps"], 1)

            def down(n, e, h, first):
                pe.wait_ge(S["hid_lo"], HB * (n + 1))
                if not first:
                    pe.wait_ge(S["y_acc"], TPH * (n - 1))
                for t in range(TPH):
                    for k in range(HB):
                        rows = slice(t * P, (t + 1) * P)
                        c0 = k * P
                        pick = (lambda s: w3[:, e, s, c0:c0 + P]) if isinstance(e, int) else \
                            (lambda s: w3[:, bass.ds(e, 1), s, c0:c0 + P].rearrange("p a c -> p (a c)"))
                        ins = three(bk[4 + h][:, t * P:(t + 1) * P],
                                    (hids[:, n_parity(h), 0, k, rows], hids[:, n_parity(h), 1, k, rows]),
                                    (pick(0), pick(1)), k == 0, k == HB - 1)
                ins.then_inc(S["y_ps"], 1)

            def n_parity(h):
                return h

            pe.wait_ge(S["xT_lo"], 2)
            pe.wait_ge(S["v_ev"], 2)
            up(0, 0, 0, 0, True)
            pe.wait_ge(S["split3"], 2 * E)
            for n in range(3):
                up(n + 1, (n + 1) // 4, (n + 1) // 2 % 2, (n + 1) % 2, False)
                down(n, n // 2, n % 2, n < 2)
            with pe.Fori(1, UNITS // 4) as i:
                for j in range(4):
                    up(4 * i + j, i, j // 2, j % 2, False)
                    down(4 * i + j - 1, 2 * i + (j - 1) // 2, (j - 1) % 2, False)
            down(UNITS - 1, E - 1, 1, False)
            turn("ln3", "x3T_ps")

            def project(m, g, b, first, late):
                if not first:
                    pe.wait_ge(S["ks_s"], m)
                if late is not None:
                    pe.wait_ge(S["ao_s"], late)
                cols = slice(b * SEQ, (b + 1) * SEQ) if isinstance(b, int) else bass.ds(SEQ * b, SEQ)
                for a, src in enumerate((xT, ctxTs)):
                    ins = three(bk[0][:, a * SEQ:(a + 1) * SEQ],
                                (wqk[:, 0, a, g * P:(g + 1) * P], wqk[:, 1, a, g * P:(g + 1) * P]),
                                (src[:, 0, cols], src[:, 1, cols]), True, True)
                ins.then_inc(S["proj_ps"], 1)

            def scores(m, g, r, first):
                pe.wait_ge(S["qs_s"], m + 1)
                pe.wait_ge(S["km_s"], HPG * (m + 1))
                if not (first and r < 2):
                    pe.wait_ge(S["s1_max"], 4 * m + r - 1)
                t, pair = r // 2, r % 2
                pe.matmul(bk[1 + r % 2][:, :], qs[:, g, t * P:(t + 1) * P],
                          km[:, g, 2 * pair:2 * pair + 2, :].rearrange("p h k -> p (h k)"),
                          start=True, stop=True).then_inc(S["s1_ps"], 1)

            def turn_maxima(m, first):
                pe.wait_ge(S["s1_max"], 4 * (m + 1))
                if not first:
                    pe.wait_ge(S["o_ev"], m - 1)
                for t in range(TPB):
                    ins = pe.transpose(bk[7][:, t * P:(t + 1) * P], negm[:, t, :], ident)
                ins.then_inc(S["mT_ps"], 1)

            def shifted_scores(m, g, r, first):
                pe.wait_ge(S["qa_s"], m + 1)
                if not first:
                    pe.wait_ge(S["p_s"], 2 * (m - 1) + r + 1)
                for a in range(2):
                    j = 2 * r + a
                    for t in range(TPB):
                        ins = pe.matmul(bk[3 + j][:, t * SEQ:(t + 1) * SEQ], km[:, g, j, t * P:(t + 1) * P],
                                        qa[:, g, :], start=True, stop=True)
                ins.then_inc(S["s2_ps"], 1)

            def outputs(m, g, b, qa_done):
                pe.wait_ge(S["p_s"], 2 * m + 2)
                pe.wait_ge(S["v_s"], b + 1)
                pe.wait_ge(S["qa_s"], qa_done)
                for j in range(HPG):
                    for t in range(TPB):
                        ins = pe.matmul(bk[7][QUAD * j:QUAD * (j + 1), SEQ:2 * SEQ], vones[:, t, g * HPG + j, :],
                                        probs[:, g % 2, j, t, :], start=t == 0, stop=t == TPB - 1,
                                        tile_position=(0, QUAD * j))
                ins.then_inc(S["pv_ps"], 1)

            def turn_outputs(b):
                pe.wait_ge(S["o_ev"], G * (b + 1))
                for t in range(TPB):
                    bank = bk[7] if t == 0 else bk[0]
                    for g in range(G):
                        ins = pe.transpose(bank[:, g * P:(g + 1) * P], os_[:, g, t * P:(t + 1) * P], ident)
                    ins.then_inc(S["oT_ps"], 1)

            def turn_normalised(b):
                pe.wait_ge(S["ao_s"], 2 * (b + 1))
                for t in range(TPB):
                    ins = pe.transpose(bk[7][:, t * P:(t + 1) * P], ao[:, t, :], ident)
                ins.then_inc(S["aoT_ps"], 1)

            def output_layer(b):
                pe.wait_ge(S["aoT_ev"], b + 1)
                for t in range(TPB):
                    ins = pe.matmul(bk[7][:, t * P:(t + 1) * P], aoT[:, t * P:(t + 1) * P], wo[:, :],
                                    start=True, stop=True)
                ins.then_inc(S["wo_ps"], 1)

            def pe_batch(b, first, last):
                for g in range(G):
                    m = G * b + g
                    more = not (last and g == G - 1)
                    if not first and g == 1:
                        pe.wait_ge(S["qa_s"], m + 1)
                        pe.wait_ge(S["ks_s"], m + 2 if not last or g < 3 else 0)
                        turn_outputs(b - 1)
                    if not first and g == 2:
                        pe.wait_ge(S["qa_s"], m + 1)
                        pe.wait_ge(S["o_ev"], m - 1)
                        turn_normalised(b - 1)
                    if not first and g == 3:
                        pe.wait_ge(S["qa_s"], m + 1)
                        pe.wait_ge(S["o_ev"], m - 1)
                        output_layer(b - 1)
                    if g != 1 and not (last and g >= 2):
                        project(m + 2, (g + 2) % G, b + (g + 2) // G, False, None)
                    if more:
                        scores(m + 1, (g + 1) % G, 0, False)
                        scores(m + 1, (g + 1) % G, 1, False)
                    shifted_scores(m, g, 0, first and g == 0)
                    if g == 1:
                        project(m + 2, (g + 2) % G, b, False, None if first else TPB * b)
                    if more:
                        scores(m + 1, (g + 1) % G, 2, False)
                    shifted_scores(m, g, 1, first and g == 0)
                    if more:
                        scores(m + 1, (g + 1) % G, 3, False)
                    if not first and g == 1:
                        pe.wait_ge(S["ao_s"], TPB * b)
                    if not first and g == 2:
                        pe.wait_ge(S["aoT_ev"], b)
                    if not first and g == 3:
                        pe.wait_ge(S["x3_s"], b)
                    if not (first and g == 0):
                        outputs(m - 1, (g - 1) % G, b if g else b - 1, m + 1)
                    if more:
                        turn_maxima_after(m + 1, first and g == 0)

            def turn_maxima_after(m, first):
                pe.wait_ge(S["s1_max"], 4 * (m + 1))
                if first:
                    pe.wait_ge(S["qa_s"], m)
                else:
                    pe.wait_ge(S["o_ev"], m - 1)
                for t in range(TPB):
                    ins = pe.transpose(bk[7][:, t * P:(t + 1) * P], negm[:, t, :], ident)
                ins.then_inc(S["mT_ps"], 1)

            pe.wait_ge(S["x3T_lo"], 2)
            pe.wait_ge(S["ctx_lo"], 1)
            pe.wait_ge(S["wqk_lo"], 1)
            project(0, 0, 0, True, None)
            project(1, 1, 0, False, None)
            for r in range(4):
                scores(0, 0, r, True)
            turn_maxima(0, True)
            pe_batch(0, True, False)
            with pe.Fori(1, BATCH - 1) as b:
                pe_batch(b, False, False)
            pe_batch(BATCH - 1, False, True)
            last = G * BATCH - 1
            pe.wait_ge(S["o_ev"], last)
            outputs(last, G - 1, BATCH - 1, last + 1)
            turn_outputs(BATCH - 1)
            turn_normalised(BATCH - 1)
            output_layer(BATCH - 1)

            pe.wait_ge(S["ident16_s"], 1)
            for h in range(2):
                pe.wait_ge(S["f_s"], 9 * (h + 1))
                for t in range(TPH):
                    tile = h * TPH + t
                    ins = pe.transpose(bk[h][:, t * P // 2:(t + 1) * P // 2].bitcast(bf16),
                                       xq[:, tile * P:(tile + 1) * P], ident16[:, :])
                ins.then_inc(S["fT_ps"], 1)
            pe.wait_ge(S["kq_s"], 8)
            for h in range(2):
                pe.wait_ge(S["fT_ev"], h + 1)
                for t in range(TPH):
                    tile = h * TPH + t
                    ins = pe.matmul(bk[2 + h][:, t * P:(t + 1) * P], xqT[:, tile * P:(tile + 1) * P], kq[:, :],
                                    start=True, stop=True)
                ins.then_inc(S["f_ps"], 1)


def kernel(**inputs):
    import numpy as np
    import concourse.bacc as bacc
    from concourse import mybir
    from concourse.bass_utils import run_bass_kernel_spmd as run

    a = {k: np.asarray(v) for k, v in inputs.items()}

    def rows(v):
        return np.ascontiguousarray(np.broadcast_to(v.reshape(1, -1), (P, v.size)))

    def tiles(v):
        return np.ascontiguousarray(v.reshape(NT, P, P).transpose(1, 0, 2))

    def stacked(w):
        out = np.zeros((P, G, HPG, 4, HD), w.dtype)
        out[:, :, :, 0:3, :] = w.reshape(P, G, HPG, 1, HD)
        return out.reshape(P, G * P)

    const = np.zeros((P, N_CONST), np.float32)
    row = np.arange(P) % QUAD
    const[:, C_AQ] = -1.0 * (row // HD == 1)
    const[:, C_AK] = -1.0 * (row // HD == 2) + 1.0 * (row == SHIFT_ROW)
    const[:, C_ONE] = row == SHIFT_ROW
    const[:, C_IOTA:C_IOTA + E] = np.arange(E)
    const[:, C_ID:C_ID + P] = np.eye(P)
    small = np.concatenate(
        [a["L0_xattn_w_cq"].reshape(P, 1), a["L0_xattn_w_q"].reshape(P, 1), a["L0_xattn_w_c"].reshape(P, 1),
         rows(a["L0_xattn_b_cq"]), rows(a["L0_xattn_b_c"]), rows(a["L0_xattn_b_q"]),
         rows(a["L1_ffn_input_scale"]), rows(a["L1_ffn_kernel_scale"])], axis=1)
    arrays = {
        "x": tiles(a["x"]), "ctx": tiles(a["ctx_1024"]), "ctxT": np.ascontiguousarray(a["ctx_1024"].reshape(TOK, P).T),
        "small": small, "const": const,
        "wl": np.ascontiguousarray(a["L0_xattn_W_l"].T.reshape(4, P, P).transpose(1, 0, 2)),
        "bl": rows(a["L0_xattn_b_l"]), "wg": a["L0_ffn_Wg"],
        "w12": np.ascontiguousarray(np.concatenate([a["L0_ffn_W1"], a["L0_ffn_W2"]], axis=2).transpose(1, 0, 2)),
        "w3": np.ascontiguousarray(a["L0_ffn_W3"].reshape(E, HB, P, P).transpose(2, 0, 1, 3).reshape(P, E, HB * P)),
        "wq": stacked(a["L1_xattn_W_q"]), "wk": stacked(a["L1_xattn_W_k"]), "wv": a["L1_xattn_W_v"],
        "wo": a["L1_xattn_W_o"], "bo": rows(a["L1_xattn_b_o"]), "fk": a["L1_ffn_kernel"], "fb": rows(a["L1_ffn_bias"]),
    }
    nc = bacc.Bacc("TRN2", target_bir_lowering=False, num_devices=1)
    args = [nc.dram_tensor(f"in_{k}", v.shape, mybir.dt.from_np(v.dtype), kind="ExternalInput").ap()
            for k, v in arrays.items()]
    out = nc.dram_tensor("out", (P, NT, P), mybir.dt.float32, kind="ExternalOutput").ap()
    build(nc, *args, out)
    r = run(nc, [{f"in_{k}": np.ascontiguousarray(v) for k, v in arrays.items()}], core_ids=[0])
    return r.results[0]["out"].transpose(1, 0, 2).reshape(BATCH, SEQ, P)
```

```python
import concourse.bass as bass
from concourse import mybir
from contextlib import ExitStack

P = 128
BATCH, SEQ = 4, 256
TOK = BATCH * SEQ
NT = TOK // P
TPB = SEQ // P
HALF = TOK // 2
TPH = NT // 2
E, HID = 8, 256
HB = HID // P
UNITS = 2 * E
HEADS, HD = 16, 8
HPG = 4
G = HEADS // HPG
QUAD = 32
SHIFT_ROW = 24
EPS = 1e-5
ATT_SCALE = HD ** -0.5
C_AQ, C_AK, C_ONE, C_IOTA, C_ID = 0, 1, 2, 3, 3 + E
N_CONST = C_ID + P
S_WCQ, S_WQ, S_WC, S_B, S_SIN, S_SK, N_SMALL = 0, 1, 2, 3, 6, 7, 8


def build(nc, x_d, ctx_d, ctxT_d, small_d, const_d, wl_d, bl_d, wg_d, w12_d, w3_d,
          wq_d, wk_d, wv_d, wo_d, bo_d, fk_d, fb_d, out_d):
    fp32, r32 = mybir.dt.float32, mybir.dt.float32r
    bf16, fp16 = mybir.dt.bfloat16, mybir.dt.float16
    i32, u32 = mybir.dt.int32, mybir.dt.uint32
    ALU = mybir.AluOpType
    ACT = mybir.ActivationFunctionType
    AX = mybir.AxisListType

    stack = ExitStack()
    with stack:
        def sb(name, shape, dt=fp32):
            return stack.enter_context(nc.sbuf_tensor(name, shape, dt))

        def sem(name):
            return stack.enter_context(nc.semaphore(name))

        def plain(ap):
            return ap.bitcast(fp32)

        const = sb("const", [P, N_CONST])
        small = sb("small", [P, N_SMALL])
        ident = const[:, C_ID:C_ID + P]
        ident16 = sb("ident16", [P, P], bf16)
        expo = sb("expo", [P, NT])
        wl = sb("wl", [P, 4, P])
        bl = sb("bl", [P, P])
        wg = sb("wg", [P, E])
        wgs = sb("wgs", [P, 2, E], r32)
        raw = sb("raw", [P, E * 2 * HID + E * HB * P])
        w12raw = raw[:, 0:E * 2 * HID].rearrange("p (e c) -> p e c", e=E)
        w3raw = raw[:, E * 2 * HID:].rearrange("p (e c) -> p e c", e=E)
        w12 = sb("w12", [P, E, 2, 2 * HID], r32)
        w3 = sb("w3", [P, E, 2, HB * P], r32)
        w12s = sb("w12s", [P, 2, 2, 2 * HID], r32)
        wqkraw = sb("wqkraw", [P, 2, G * P])
        wqk = sb("wqk", [P, 2, 2, G * P], r32)
        wv = sb("wv", [P, P])
        wo = sb("wo", [P, P])
        bo = sb("bo", [P, P])
        fk = sb("fk", [P, P], bf16)
        fb = sb("fb", [P, P], bf16)

        xs = sb("xs", [P, NT, P])
        xn = sb("xn", [P, NT, P])
        xT = sb("xT", [P, 2, TOK], r32)
        ctx = sb("ctx", [P, NT, P])
        ctxT = sb("ctxT", [P, TOK])
        ctxTs = sb("ctxTs", [P, 2, TOK], r32)
        stats = sb("stats", [P, NT, 6])
        mv = sb("mv", [P, NT, 2])
        vpe = sb("vpe", [P, NT])
        rstd = sb("rstd", [P, NT])

        cT = sb("cT", [P, TOK])
        cpT = sb("cpT", [P, TOK])
        att = sb("att", [P, NT, SEQ])
        attT = sb("attT", [P, BATCH, TPB, SEQ])
        c2qT = cpT
        ccT = sb("ccT", [P, TOK])
        nmax = sb("nmax", [P, NT])
        rsum = sb("rsum", [P, NT])
        rinv = sb("rinv", [P, NT])
        bsum = sb("bsum", [P, 2])
        cv = sb("cv", [P, NT])
        bnmax = sb("bnmax", [1, BATCH])
        brow = ccT[0:1, :]
        bden = sb("bden", [1, 2 * BATCH])
        bcol = sb("bcol", [P, NT])
        q2c = sb("q2c", [P, BATCH])
        w14 = sb("w14", [P, BATCH, P])

        logit = sb("logit", [P, NT, E])
        top = sb("top", [P, NT, 8])
        topi = sb("topi", [P, NT, 8], u32)
        topf = sb("topf", [P, NT, 2])
        gap = sb("gap", [P, 4, NT])
        route = sb("route", [P, 3, NT, E])
        rw = sb("rw", [P, NT, E])
        att_flat = att[:, :, :].rearrange("p t q -> p (t q)")
        tanhs = att_flat[:, 0:TOK].rearrange("p (k t) -> p k t", k=HB)
        gated = att_flat[:, TOK:2 * TOK].rearrange("p (k t) -> p k t", k=HB)
        hid = attT[:, 0:2, :, :].rearrange("p a b c -> p a (b c)")
        hids = sb("hids", [P, 2, 2, HB, HALF], r32)

        vall = sb("vall", [P, NT, P])
        vones = sb("vones", [P, TPB, HEADS, QUAD])
        w12_flat = w12[:, :, :, :].rearrange("p e s c -> p (e s c)")
        km = w12_flat[:, 0:G * HPG * SEQ].rearrange("p (g h k) -> p g h k", g=G, h=HPG)
        qs, qa = (w12_flat[:, (G * HPG + G * n) * SEQ:(G * HPG + G * (n + 1)) * SEQ]
                  .rearrange("p (g q) -> p g q", g=G) for n in range(2))
        N_PROBS = HPG * TPB * SEQ
        probs = raw[:, 0:2 * N_PROBS].rearrange("p (u h k q) -> p u h k q", u=2, h=HPG, k=TPB)
        rest = raw[:, 2 * N_PROBS:]
        ks = rest[:, 0:2 * SEQ].rearrange("p (u k) -> p u k", u=2)
        hiQ = rest[:, 2 * SEQ:3 * SEQ]
        hiK = rest[:, 3 * SEQ:4 * SEQ]
        os_ = rest[:, 4 * SEQ:(4 + G) * SEQ].rearrange("p (g q) -> p g q", g=G)
        negm = sb("negm", [P, TPB, P])
        den = sb("den", [P, TPB, G, HPG])
        ao = sb("ao", [P, TPB, P])
        aoT = sb("aoT", [P, SEQ])

        rs = sb("rs", [P, 3])
        f16, xq = (cpT[:, n * HALF:(n + 1) * HALF].bitcast(bf16) for n in range(2))
        xqT, fovf = ctxT[:, 0:HALF].bitcast(bf16), ctxT[:, HALF:TOK].bitcast(fp16)
        vflat = vall[:, :, :].rearrange("p t d -> p (t d)")
        yb, yz = (vflat[:, n * HALF:(n + 1) * HALF].bitcast(bf16) for n in range(2))
        fv = ccT
        fe = attT[:, 0:2, :, :].rearrange("p a b c -> p (a b c)")
        fq = attT[:, 2:4, :, :].rearrange("p a b c -> p (a b c)")
        kq = sb("kq", [P, P], bf16)
        kovf = sb("kovf", [P, P], fp16)
        kv, ke, kr = (bl[:, :], wv[:, :], wl[:, 0, :])
        res = cT[:, :].rearrange("p (t d) -> p t d", t=NT)

        bk = [stack.enter_context(nc.psum_tensor(f"bank{i}", [P, 512], fp32)) for i in range(8)]

        names = """ld_x ld_ctx ld_par ld_w ld_att stored
          setup ident16_s v_zero km_zero w12_hi w12_lo w3_hi w3_lo ctx_hi ctx_lo wqk_hi wqk_lo wg_hi wg_lo v_ps v_ev bl_added bo_added
          st1 ag1 ve1 rs1 ln1 st2 ag2 ve2 rs2 ln2 st3 ag3 ve3 rs3 ln3 st4 ag4 ve4 rs4 ln4
          cT_ps cT_ev cpT_ev cw_ps s_ps s_max s_exp s_rinv s_norm aT_ps aT_ev c2q_ps c2q_ev cc_ev
          bsum_s cv_s row_ps row_max row_exp row_inv bcol_ps bcol_ev q2c_ps q2c_ev w14_s z_ps z_add
          xT_ps xT_hi xT_lo logit_ps logit_ev top_s topi_s gap_s gap_exp route_s
          staged0 staged1 uv_ps tanh_s gate_s hid_s hid_hi hid_lo y_ps y_acc
          x3T_ps x3T_hi x3T_lo proj_ps q_hi k_hi qs_s ks_s km_act km_dve s1_ps s1_max mT_ps qa_s s2_ps p_s
          v_s pv_ps o_ev oT_ps den_s ao_s aoT_ps aoT_ev wo_ps x3_s
          rs_s fv_s q_s ovf_s f_s xq_s fT_ps fT_ev f_ps y_s out_s""".split()
        S = {n: sem(n) for n in names}

        block = stack.enter_context(nc.Block())

        @block.sync
        def _(sp):
            sp.dma_start(xs[:, :, :], x_d).then_inc(S["ld_x"], 16)
            sp.dma_start(ctxT[:, :], ctxT_d).then_inc(S["ld_ctx"], 16)
            sp.dma_start(ctx[:, :, :], ctx_d).then_inc(S["ld_ctx"], 16)
            sp.dma_start(wl[:, :, :], wl_d).then_inc(S["ld_par"], 16)
            sp.dma_start(w12raw, w12_d).then_inc(S["ld_w"], 16)
            sp.dma_start(w3raw, w3_d).then_inc(S["ld_w"], 16)

            def stage(e, parity, reused):
                if reused:
                    sp.wait_ge(S["uv_ps"], 2 * HB * (e - 1))
                src = w12[:, e:e + 1, :, :] if isinstance(e, int) else w12[:, bass.ds(e, 1), :, :]
                sp.dma_start(plain(w12s[:, parity:parity + 1, :, :]), plain(src)).then_inc(S[f"staged{parity}"], 16)

            sp.wait_ge(S["w12_lo"], E)
            stage(0, 0, False)
            stage(1, 1, False)
            with sp.Fori(1, E // 2) as i:
                stage(2 * i, 0, True)
                stage(2 * i + 1, 1, True)

            for h in range(2):
                sp.wait_ge(S["out_s"], h + 1)
                sp.dma_start(out_d[:, h * TPH:(h + 1) * TPH, :], res[:, h * TPH:(h + 1) * TPH, :])\
                    .then_inc(S["stored"], 16)
            sp.wait_ge(S["stored"], 32)

        @block.gpsimd
        def _(pool):
            pool.memset(expo[:, :], -0.5)
            pool.memset(negm[:, :, :], 0.0)
            pool.memset(vones[:, :, :, :], 0.0).then_inc(S["v_zero"], 1)
            pool.wait_ge(S["v_zero"], 1)
            pool.memset(vones[:, :, :, HD:HD + 1], 1.0).then_inc(S["setup"], 1)

            def inverse_deviation(n, h):
                tiles = slice(h * TPH, (h + 1) * TPH)
                pool.wait_ge(S[f"ag{n}"], TPH * (h + 1))
                pool.tensor_scalar(vpe[:, tiles], mv[:, tiles, 1], EPS, None, ALU.add).then_inc(S[f"ve{n}"], 1)
                pool.wait_ge(S[f"ve{n}"], h + 1)
                pool.tensor_tensor(rstd[:, tiles], vpe[:, tiles], expo[:, tiles], ALU.pow).then_inc(S[f"rs{n}"], 1)
                pool.wait_ge(S[f"rs{n}"], h + 1)

            pool.wait_ge(S["setup"], 1)
            for h in range(2):
                inverse_deviation(1, h)
            for e in range(E):
                pool.wait_ge(S["w12_hi"], e + 1)
                pool.tensor_tensor(w12[:, e, 1, :], w12raw[:, e, :], plain(w12[:, e, 0, :]), ALU.subtract)\
                    .then_inc(S["w12_lo"], 1)
            pool.wait_ge(S["w3_hi"], E // 2)
            for e in range(0, E, 2):
                pool.tensor_tensor(w3[:, e:e + 2, 1, :], w3raw[:, e:e + 2, :], plain(w3[:, e:e + 2, 0, :]),
                                   ALU.subtract).then_inc(S["w3_lo"], 1)
            for h in range(2):
                inverse_deviation(2, h)
            pool.wait_ge(S["ctx_hi"], 1)
            pool.tensor_tensor(ctxTs[:, 1, :], ctxT[:, :], plain(ctxTs[:, 0, :]), ALU.subtract)\
                .then_inc(S["ctx_lo"], 1)
            pool.wait_ge(S["wqk_hi"], 1)
            pool.tensor_tensor(wqk[:, 1, :, :], wqkraw[:, :, :], plain(wqk[:, 0, :, :]), ALU.subtract)\
                .then_inc(S["wqk_lo"], 1)

            def hidden_lo(n, p, first):
                for k in range(HB):
                    pool.wait_ge(S["hid_hi"], HB * n + k + 1)
                    if not first:
                        pool.wait_ge(S["y_ps"], n - 1)
                    pool.tensor_tensor(hids[:, p, 1, k, :], hid[:, k, :], plain(hids[:, p, 0, k, :]),
                                       ALU.subtract).then_inc(S["hid_lo"], 1)

            for n in range(4):
                hidden_lo(n, n % 2, n < 2)
            with pool.Fori(1, UNITS // 4) as i:
                for j in range(4):
                    hidden_lo(4 * i + j, j % 2, False)
            for parity in range(2):
                pool.wait_ge(S[f"staged{parity}"], 16 * E // 2)
            pool.memset(km.bitcast(i32), 0).then_inc(S["km_zero"], 1)
            for h in range(2):
                inverse_deviation(3, h)

            def values(b, first):
                if not first:
                    pool.wait_ge(S["pv_ps"], G * b)
                pool.wait_ge(S["v_ev"], 2)
                src = vall[:, 0:TPB, :] if first else vall[:, bass.ds(TPB * b, TPB), :]
                pool.tensor_copy(vones[:, :, :, 0:HD], src.rearrange("p t (h d) -> p t h d", h=HEADS))\
                    .then_inc(S["v_s"], 1)

            values(0, True)
            with pool.Fori(1, BATCH) as b:
                values(b, False)
            for h in range(2):
                inverse_deviation(4, h)

        @block.scalar
        def _(act):
            act.dma_start(const[:, :], const_d).then_inc(S["ld_par"], 16)
            act.dma_start(small[:, :], small_d).then_inc(S["ld_par"], 16)
            act.dma_start(bl[:, :], bl_d).then_inc(S["ld_par"], 16)
            act.dma_start(wg[:, :], wg_d).then_inc(S["ld_par"], 16)
            for dst, src in ((wqkraw[:, 0, :], wq_d), (wqkraw[:, 1, :], wk_d), (wv[:, :], wv_d),
                             (wo[:, :], wo_d), (bo[:, :], bo_d), (fk[:, :], fk_d), (fb[:, :], fb_d)):
                act.dma_start(dst, src).then_inc(S["ld_att"], 16)
            act.wait_ge(S["ld_par"], 80)
            act.copy(ident16[:, :], ident).then_inc(S["ident16_s"], 1)

            for h in range(2):
                cols = slice(h * HALF, (h + 1) * HALF)
                act.wait_ge(S["cT_ps"], h + 1)
                act.activation(cpT[:, cols], bk[h][:, :], ACT.Identity, scale=small[:, S_WCQ:S_WCQ + 1],
                               bias=small[:, S_WQ:S_WQ + 1]).then_inc(S["cpT_ev"], 1)
                act.copy(cT[:, cols], bk[h][:, :]).then_inc(S["cT_ev"], 1)
            for t in range(NT):
                act.wait_ge(S["s_max"], t // TPB + 1)
                c0 = (t % TPB) * SEQ
                act.activation(att[:, t, :], bk[2 + t // TPB][:, c0:c0 + SEQ], ACT.Exp,
                               bias=nmax[:, t:t + 1], accum_out=rsum[:, t:t + 1]).then_inc(S["s_exp"], 1)
            act.wait_ge(S["ld_w"], 32)
            act.copy(wgs[:, 0, :], wg[:, :]).then_inc(S["wg_hi"], 1)
            for e in range(E):
                act.copy(w12[:, e, 0, :], w12raw[:, e, :]).then_inc(S["w12_hi"], 1)
            for b in range(BATCH):
                act.wait_ge(S["row_max"], b // 2 + 1)
                c0 = (b % 2) * SEQ
                act.activation(brow[:, b * SEQ:(b + 1) * SEQ], bk[b // 2][0:1, c0:c0 + SEQ], ACT.Exp,
                               bias=bnmax[:, b:b + 1], accum_out=bden[:, b:b + 1]).then_inc(S["row_exp"], 1)
            for b in range(BATCH):
                act.wait_ge(S["aT_ps"], b + 1)
                act.copy(attT[:, b, :, :], bk[2 + b][:, :]).then_inc(S["aT_ev"], 1)
            act.wait_ge(S["bcol_ps"], 1)
            act.copy(bcol[:, :], bk[7][:, 16:16 + NT]).then_inc(S["bcol_ev"], 1)
            for h in range(2):
                act.wait_ge(S["c2q_ps"], h + 1)
                act.copy(c2qT[:, h * HALF:(h + 1) * HALF], bk[h][:, :]).then_inc(S["c2q_ev"], 1)
            act.wait_ge(S["q2c_ps"], 1)
            act.copy(q2c[:, :], bk[7][:, 32:32 + BATCH]).then_inc(S["q2c_ev"], 1)
            for e in range(0, E, 2):
                act.copy(w3[:, e:e + 2, 0, :], w3raw[:, e:e + 2, :]).then_inc(S["w3_hi"], 1)
            act.wait_ge(S["ld_att"], 7 * 16)
            act.copy(ctxTs[:, 0, :], ctxT[:, :]).then_inc(S["ctx_hi"], 1)
            act.copy(wqk[:, 0, :, :], wqkraw[:, :, :]).then_inc(S["wqk_hi"], 1)
            for h in range(2):
                act.wait_ge(S["v_ps"], h + 1)
                act.copy(vall[:, h * TPH:(h + 1) * TPH, :], bk[2 + h][:, :]).then_inc(S["v_ev"], 1)
            for h in range(2):
                act.wait_ge(S["xT_ps"], h + 1)
                act.copy(xT[:, 0, h * HALF:(h + 1) * HALF], bk[5 + h][:, :]).then_inc(S["xT_hi"], 1)
            def hidden(n, p, first, second):
                for k in range(HB):
                    act.wait_ge(S["uv_ps"], HB * n + k + 1)
                    if not first:
                        act.wait_ge(S["gate_s"], HB * (n - 1) + k + 1)
                    act.activation(tanhs[:, k, :], bk[2 * k][:, :], ACT.Tanh, scale=0.5).then_inc(S["tanh_s"], 1)
                for k in range(HB):
                    act.wait_ge(S["hid_s"], HB * n + k + 1)
                    if not (first or second):
                        act.wait_ge(S["y_ps"], n - 1)
                    act.copy(hids[:, p, 0, k, :], hid[:, k, :]).then_inc(S["hid_hi"], 1)

            hidden(0, 0, True, False)
            act.wait_ge(S["gap_s"], 1)
            act.activation(gap[:, 1, :], gap[:, 0, :], ACT.Exp).then_inc(S["gap_exp"], 1)
            for n in range(1, 4):
                hidden(n, n % 2, False, n == 1)
            with act.Fori(1, UNITS // 4) as i:
                for j in range(4):
                    hidden(4 * i + j, j % 2, False, False)
            for h in range(2):
                act.wait_ge(S["x3T_ps"], h + 1)
                act.copy(xT[:, 0, h * HALF:(h + 1) * HALF], bk[h][:, :]).then_inc(S["x3T_hi"], 1)

            def proj_hi(m, first):
                act.wait_ge(S["proj_ps"], m + 1)
                if not first:
                    act.wait_ge(S["ks_s"], m)
                act.copy(hiQ.bitcast(r32), bk[0][:, 0:SEQ]).then_inc(S["q_hi"], 1)
                act.activation(hiK.bitcast(r32), bk[0][:, SEQ:2 * SEQ], ACT.Identity,
                               bias=const[:, C_ONE:C_ONE + 1]).then_inc(S["k_hi"], 1)

            def masked_keys(m, g, first):
                act.wait_ge(S["ks_s"], m + 1)
                if not first:
                    act.wait_ge(S["s2_ps"], 2 * (m - 3))
                for j in range(1, HPG):
                    rows = slice(QUAD * j, QUAD * (j + 1))
                    ins = act.copy(km[rows, g, j, :], ks[rows, g % 2, :])
                ins.then_inc(S["km_act"], 1)

            def exps(m, g, first, between):
                for r in range(2):
                    act.wait_ge(S["s2_ps"], 2 * m + r + 1)
                    if not first:
                        act.wait_ge(S["pv_ps"], m - 1)
                    for a in range(2):
                        ins = act.activation(probs[:, g % 2, 2 * r + a, :, :],
                                             bk[3 + 2 * r + a][:, :].rearrange("p (k q) -> p k q", k=TPB),
                                             ACT.Exp, scale=ATT_SCALE)
                    ins.then_inc(S["p_s"], 1)
                    if r == 0:
                        between()

            def o_copy(m, g):
                act.wait_ge(S["pv_ps"], m + 1)
                act.copy(os_[:, g, :], bk[7][:, SEQ:2 * SEQ]).then_inc(S["o_ev"], 1)

            def act_batch(b, first, last):
                for g in range(G):
                    m = G * b + g
                    if not (last and g >= 2):
                        proj_hi(m + 2, False)
                    if g == 2 and not first:
                        act.wait_ge(S["aoT_ps"], b)
                        act.copy(aoT[:, :], bk[7][:, 0:SEQ]).then_inc(S["aoT_ev"], 1)
                    exps(m, g, first and g < 2, lambda: None if last and g >= 2 else
                         masked_keys(m + 2, (g + 2) % G, first and g < 2))
                    if not (first and g == 0):
                        o_copy(m - 1, (g - 1) % G)

            act.wait_ge(S["km_zero"], 1)
            proj_hi(0, True)
            masked_keys(0, 0, True)
            proj_hi(1, False)
            masked_keys(1, 1, True)
            act_batch(0, True, False)
            with act.Fori(1, BATCH - 1) as b:
                act_batch(b, False, False)
            act_batch(BATCH - 1, False, True)
            o_copy(G * BATCH - 1, G - 1)
            act.wait_ge(S["aoT_ps"], BATCH)
            act.copy(aoT[:, :], bk[7][:, 0:SEQ]).then_inc(S["aoT_ev"], 1)

            act.wait_ge(S["rs_s"], 2)
            act.activation(kv, fk[:, :], ACT.Copy, scale=rs[:, 1:2]).then_inc(S["fv_s"], 1)
            for h in range(2):
                cols = slice(h * HALF, (h + 1) * HALF)
                act.wait_ge(S["ln4"], TPH * (h + 1))
                act.activation(fv[:, cols], f16[:, cols], ACT.Copy, scale=rs[:, 0:1]).then_inc(S["fv_s"], 1)
            act.wait_ge(S["q_s"], 1)
            act.activation(kovf[:, :], kr, ACT.Copy, scale=144.0).then_inc(S["ovf_s"], 1)
            for h in range(2):
                cols = slice(h * HALF, (h + 1) * HALF)
                act.wait_ge(S["q_s"], h + 2)
                act.activation(fovf[:, cols], fq[:, cols], ACT.Copy, scale=144.0).then_inc(S["ovf_s"], 1)
            for h in range(2):
                act.wait_ge(S["fT_ps"], h + 1)
                act.copy(xqT[:, h * HALF:(h + 1) * HALF], bk[h][:, 0:HALF // 2].bitcast(bf16)).then_inc(S["fT_ev"], 1)

        @block.vector
        def _(dve):
            def moments(n, h, ready):
                if n > 1 and h == 0:
                    dve.wait_ge(S[f"ln{n - 1}"], NT)
                for t in range(h * TPH, (h + 1) * TPH):
                    ready(t)
                    dve.bn_stats(stats[:, t, :], xs[:, t, :]).then_inc(S[f"st{n}"], 1)
                for t in range(h * TPH, (h + 1) * TPH):
                    dve.wait_ge(S[f"st{n}"], t + 1)
                    dve.bn_aggr(mv[:, t, :], stats[:, t, :]).then_inc(S[f"ag{n}"], 1)

            def scaled(n, h, out=xn):
                dve.wait_ge(S[f"ag{n}"], TPH * (h + 1))
                dve.wait_ge(S[f"rs{n}"], h + 1)
                for t in range(h * TPH, (h + 1) * TPH):
                    dve.tensor_scalar(out[:, t, :], xs[:, t, :], mv[:, t, 0:1], rstd[:, t:t + 1],
                                      ALU.subtract, ALU.mult).then_inc(S[f"ln{n}"], 1)

            def norm(n, ready):
                for h in range(2):
                    moments(n, h, ready)
                for h in range(2):
                    scaled(n, h)

            dve.wait_ge(S["ld_x"], 16)
            norm(1, lambda t: None)
            dve.wait_ge(S["ln1"], NT)
            dve.wait_ge(S["ld_par"], 80)
            dve.tensor_tensor(xs[:, :, :], xs[:, :, :], bl[:, :].unsqueeze(1).broadcast_to([P, NT, P]),
                              ALU.add).then_inc(S["bl_added"], 1)
            dve.tensor_tensor(bsum[:, 0:1], small[:, S_B:S_B + 1], small[:, S_B + 1:S_B + 2], ALU.add)\
                .then_inc(S["bsum_s"], 1)
            dve.wait_ge(S["bsum_s"], 1)
            dve.tensor_tensor(bsum[:, 1:2], bsum[:, 0:1], small[:, S_B + 2:S_B + 3], ALU.add)\
                .then_inc(S["bsum_s"], 1)
            for b in range(BATCH):
                dve.wait_ge(S["s_ps"], b + 1)
                dve.tensor_reduce(nmax[:, TPB * b:TPB * (b + 1)], bk[2 + b][:, :].rearrange("p (t q) -> p t q", t=TPB),
                                  AX.X, ALU.max, negate=True).then_inc(S["s_max"], 1)
            dve.wait_ge(S["cw_ps"], 1)
            dve.wait_ge(S["s_max"], BATCH)
            dve.wait_ge(S["bsum_s"], 2)
            dve.scalar_tensor_tensor(cv[:, :], bk[7][:, 0:NT], bsum[:, 1:2], nmax[:, :], ALU.add, ALU.subtract)\
                .then_inc(S["cv_s"], 1)
            for t in range(NT):
                dve.wait_ge(S["s_exp"], t + 1)
                dve.reciprocal(rinv[:, t:t + 1], rsum[:, t:t + 1]).then_inc(S["s_rinv"], 1)
                dve.wait_ge(S["s_rinv"], t + 1)
                dve.tensor_scalar(att[:, t, :], att[:, t, :], rinv[:, t:t + 1], None, ALU.mult)\
                    .then_inc(S["s_norm"], 1)
                if t % 4 == 1:
                    h = t // 4
                    dve.wait_ge(S["row_ps"], h + 1)
                    dve.tensor_reduce(bnmax[:, 2 * h:2 * h + 2], bk[h][0:1, :].rearrange("p (b c) -> p b c", b=2),
                                      AX.X, ALU.max, negate=True).then_inc(S["row_max"], 1)
            dve.wait_ge(S["row_exp"], BATCH)
            dve.reciprocal(bden[:, BATCH:2 * BATCH], bden[:, 0:BATCH]).then_inc(S["row_inv"], 1)
            dve.wait_ge(S["wg_hi"], 1)
            dve.tensor_tensor(wgs[:, 1, :], wg[:, :], plain(wgs[:, 0, :]), ALU.subtract).then_inc(S["wg_lo"], 1)
            for h in range(2):
                cols = slice(h * HALF, (h + 1) * HALF)
                dve.wait_ge(S["c2q_ev"], h + 1)
                dve.tensor_tensor(ccT[:, cols], c2qT[:, cols], cT[:, cols], ALU.mult).then_inc(S["cc_ev"], 1)
            dve.wait_ge(S["q2c_ev"], 1)
            for b in range(BATCH):
                dve.scalar_tensor_tensor(w14[:, b, :], wl[:, 3, :], q2c[:, b:b + 1], wl[:, 0, :], ALU.mult, ALU.add)\
                    .then_inc(S["w14_s"], 1)
            dve.wait_ge(S["bl_added"], 1)
            for h in range(2):
                dve.wait_ge(S["z_ps"], h + 1)
                dve.tensor_tensor(xs[:, h * TPH:(h + 1) * TPH, :], xs[:, h * TPH:(h + 1) * TPH, :],
                                  bk[4 + h][:, :].rearrange("p (t d) -> p t d", t=TPH), ALU.add)\
                    .then_inc(S["z_add"], 1)
                moments(2, h, lambda t: dve.wait_ge(S["z_add"], h + 1))
            for h in range(2):
                scaled(2, h)
            for h in range(2):
                cols = slice(h * HALF, (h + 1) * HALF)
                dve.wait_ge(S["xT_hi"], h + 1)
                dve.tensor_tensor(xT[:, 1, cols], bk[5 + h][:, :], plain(xT[:, 0, cols]), ALU.subtract)\
                    .then_inc(S["xT_lo"], 1)

            def routing():
                dve.wait_ge(S["logit_ps"], 1)
                dve.tensor_copy(logit[:, :, :], bk[7][:, 0:NT * E].rearrange("p (t e) -> p t e", t=NT))\
                    .then_inc(S["logit_ev"], 1)
                dve.wait_ge(S["logit_ev"], 1)
                for t in range(NT):
                    dve.max(top[:, t, :], logit[:, t, :]).then_inc(S["top_s"], 1)
                for t in range(NT):
                    dve.wait_ge(S["top_s"], t + 1)
                    dve.max_index(topi[:, t, :], top[:, t, :], logit[:, t, :]).then_inc(S["topi_s"], 1)
                dve.wait_ge(S["top_s"], NT)
                dve.tensor_tensor(gap[:, 0, :], top[:, :, 1], top[:, :, 0], ALU.subtract).then_inc(S["gap_s"], 1)
                dve.wait_ge(S["topi_s"], NT)
                dve.tensor_copy(topf[:, :, :], topi[:, :, 0:2]).then_inc(S["route_s"], 1)
                dve.wait_ge(S["gap_exp"], 1)
                dve.tensor_scalar(gap[:, 2, :], gap[:, 1, :], 1.0, 2.0, ALU.add, ALU.mult).then_inc(S["route_s"], 1)
                dve.wait_ge(S["route_s"], 2)
                dve.reciprocal(gap[:, 2, :], gap[:, 2, :]).then_inc(S["route_s"], 1)
                dve.wait_ge(S["route_s"], 3)
                dve.tensor_tensor(gap[:, 3, :], gap[:, 1, :], gap[:, 2, :], ALU.mult).then_inc(S["route_s"], 1)
                iota = const[:, C_IOTA:C_IOTA + E].unsqueeze(1).broadcast_to([P, NT, E])
                for r in range(2):
                    dve.wait_ge(S["route_s"], 4)
                    dve.tensor_tensor(route[:, r, :, :], iota, topf[:, :, r:r + 1].broadcast_to([P, NT, E]),
                                      ALU.is_equal).then_inc(S["route_s"], 1)
                for r in range(2):
                    dve.wait_ge(S["route_s"], 5 + r)
                    dve.tensor_tensor(route[:, r, :, :], route[:, r, :, :],
                                      gap[:, 2 + r, :].unsqueeze(2).broadcast_to([P, NT, E]), ALU.mult)\
                        .then_inc(S["route_s"], 1)
                dve.wait_ge(S["route_s"], 8)
                dve.tensor_tensor(rw[:, :, :], route[:, 0, :, :], route[:, 1, :, :], ALU.add).then_inc(S["route_s"], 1)

            def hidden(n, first):
                for k in range(HB):
                    dve.wait_ge(S["tanh_s"], HB * n + k + 1)
                    if not first:
                        dve.wait_ge(S["hid_s"], HB * (n - 1) + k + 1)
                    dve.scalar_tensor_tensor(gated[:, k, :], tanhs[:, k, :], 1.0, bk[2 * k][:, :],
                                             ALU.add, ALU.mult).then_inc(S["gate_s"], 1)
                    dve.wait_ge(S["gate_s"], HB * n + k + 1)
                    if not first:
                        dve.wait_ge(S["hid_lo"], HB * (n - 1) + k + 1)
                    dve.tensor_tensor(hid[:, k, :], gated[:, k, :], bk[2 * k + 1][:, :], ALU.mult)\
                        .then_inc(S["hid_s"], 1)

            def accumulate(n, e, h, first):
                dve.wait_ge(S["y_ps"], n + 1)
                if not first:
                    dve.wait_ge(S["y_acc"], TPH * (n - 1))
                for t in range(TPH):
                    tile = h * TPH + t
                    weight = rw[:, tile, e:e + 1] if isinstance(e, int) else rw[:, tile, bass.ds(e, 1)]
                    dve.scalar_tensor_tensor(xs[:, tile, :], bk[4 + h][:, t * P:(t + 1) * P], weight,
                                             xs[:, tile, :], ALU.mult, ALU.add).then_inc(S["y_acc"], 1)

            hidden(0, True)
            routing()
            hidden(1, False)
            dve.wait_ge(S["route_s"], 9)
            for n in range(2, 4):
                hidden(n, False)
                accumulate(n - 2, (n - 2) // 2, n % 2, True)
            with dve.Fori(1, UNITS // 4) as i:
                for j in range(4):
                    hidden(4 * i + j, False)
                    accumulate(4 * i + j - 2, 2 * i + j // 2 - 1, j % 2, False)
            accumulate(UNITS - 2, E - 1, 0, False)
            moments(3, 0, lambda t: dve.wait_ge(S["y_acc"], TPH * (UNITS - 2) + t + 1))
            accumulate(UNITS - 1, E - 1, 1, False)
            moments(3, 1, lambda t: dve.wait_ge(S["y_acc"], TPH * (UNITS - 2) + t + 1))
            for h in range(2):
                scaled(3, h)
            for h in range(2):
                cols = slice(h * HALF, (h + 1) * HALF)
                dve.wait_ge(S["x3T_hi"], h + 1)
                dve.tensor_tensor(xT[:, 1, cols], bk[h][:, :], plain(xT[:, 0, cols]), ALU.subtract)\
                    .then_inc(S["x3T_lo"], 1)
            dve.wait_ge(S["ld_att"], 7 * 16)
            dve.tensor_tensor(xs[:, :, :], xs[:, :, :], bo[:, :].unsqueeze(1).broadcast_to([P, NT, P]),
                              ALU.add).then_inc(S["bo_added"], 1)

            def stacks(m, g, first):
                dve.wait_ge(S["q_hi"], m + 1)
                dve.wait_ge(S["k_hi"], m + 1)
                if not first:
                    dve.wait_ge(S["s1_ps"], 4 * (m - 3))
                    dve.wait_ge(S["qa_s"], m - 3)
                dve.scalar_tensor_tensor(qs[:, g, :], hiQ, const[:, C_AQ:C_AQ + 1],
                                         bk[0][:, 0:SEQ], ALU.mult, ALU.add).then_inc(S["qs_s"], 1)
                if not first or g >= 2:
                    dve.wait_ge(S["km_act"], m - 1)
                    dve.wait_ge(S["km_dve"], m - 1)
                dve.scalar_tensor_tensor(ks[:, g % 2, :], hiK, const[:, C_AK:C_AK + 1],
                                         bk[0][:, SEQ:2 * SEQ], ALU.mult, ALU.add).then_inc(S["ks_s"], 1)

            def first_keys(m, g, first):
                dve.wait_ge(S["ks_s"], m + 1)
                if not first:
                    dve.wait_ge(S["s2_ps"], 2 * (m - 3))
                dve.tensor_copy(km[0:QUAD, g, 0, :], ks[0:QUAD, g % 2, :]).then_inc(S["km_dve"], 1)

            def maxima(m, pieces, first):
                for r in pieces:
                    dve.wait_ge(S["s1_ps"], 4 * m + r + 1)
                    if not first:
                        dve.wait_ge(S["mT_ps"], m)
                    c0 = SHIFT_ROW + 2 * QUAD * (r % 2)
                    dve.tensor_reduce(negm[:, r // 2, c0:c0 + QUAD + 1:QUAD],
                                      bk[1 + r % 2][:, :].rearrange("p (h k) -> p h k", h=2),
                                      AX.X, ALU.max, negate=True).then_inc(S["s1_max"], 1)

            def shifted(m, g, first):
                dve.wait_ge(S["mT_ps"], m + 1)
                dve.wait_ge(S["qs_s"], m + 1)
                if not first:
                    dve.wait_ge(S["s2_ps"], 2 * (m - 3))
                dve.tensor_tensor(qa[:, g, :], bk[7][:, 0:SEQ], plain(qs[:, g, :]), ALU.add).then_inc(S["qa_s"], 1)

            def normalise(b):
                for t in range(TPB):
                    bank = bk[7] if t == 0 else bk[0]
                    heads = bank[:, :].rearrange("p (g h r) -> p g h r", g=G, h=HPG)
                    dve.wait_ge(S["oT_ps"], 2 * b + t + 1)
                    dve.reciprocal(den[:, t, :, :].unsqueeze(3), heads[:, :, :, HD:HD + 1]).then_inc(S["den_s"], 1)
                    dve.wait_ge(S["den_s"], 2 * b + t + 1)
                    dve.tensor_tensor(ao[:, t, :].rearrange("p (g h d) -> p g h d", g=G, h=HPG),
                                      heads[:, :, :, 0:HD], den[:, t, :, :].unsqueeze(3).broadcast_to([P, G, HPG, HD]),
                                      ALU.mult).then_inc(S["ao_s"], 1)

            def add_attention(b, tiles):
                dve.wait_ge(S["wo_ps"], b + 1)
                dve.tensor_tensor(xs[:, tiles, :], xs[:, tiles, :],
                                  bk[7][:, 0:SEQ].rearrange("p (t d) -> p t d", t=TPB), ALU.add)\
                    .then_inc(S["x3_s"], 1)

            def dve_batch(b, first, last):
                for g in range(G):
                    m = G * b + g
                    if g == 1 and not first:
                        normalise(b - 1)
                    more = not (last and g == G - 1)
                    if more:
                        maxima(m + 1, (0, 1), False)
                    if not (last and g >= 2):
                        stacks(m + 2, (g + 2) % G, first and g < 2)
                        first_keys(m + 2, (g + 2) % G, first and g < 2)
                    if g == 3 and not first:
                        tiles = bass.ds(TPB * (b - 1), TPB) if not last else slice(TPB * (b - 1), TPB * b)
                        add_attention(b - 1, tiles)
                    if more:
                        maxima(m + 1, (2, 3), False)
                        shifted(m + 1, (g + 1) % G, first and g < 3)

            dve.wait_ge(S["bo_added"], 1)
            dve.wait_ge(S["setup"], 1)
            dve.wait_ge(S["km_zero"], 1)
            for m in range(2):
                stacks(m, m, True)
                first_keys(m, m, True)
            maxima(0, range(4), True)
            shifted(0, 0, True)
            dve_batch(0, True, False)
            with dve.Fori(1, BATCH - 1) as b:
                dve_batch(b, False, False)
            dve_batch(BATCH - 1, False, True)
            normalise(BATCH - 1)
            add_attention(BATCH - 1, slice(NT - TPB, NT))

            dve.reciprocal(rs[:, 0:2], small[:, S_SIN:S_SIN + 2]).then_inc(S["rs_s"], 1)
            dve.tensor_tensor(rs[:, 2:3], small[:, S_SIN:S_SIN + 1], small[:, S_SK:S_SK + 1], ALU.mult)\
                .then_inc(S["rs_s"], 1)
            dve.wait_ge(S["rs_s"], 2)

            def to_e4m3(dst, v, e, q, ovf, scaled_s, step, base, q_s, ovf_s, h):
                dve.wait_ge(S[scaled_s], h + 1)
                dve.tensor_scalar(e.bitcast(i32), v.bitcast(i32), 0x7F800000, None, ALU.bitwise_and)\
                    .then_inc(S[step], 1)
                dve.wait_ge(S[step], base + 1)
                dve.tensor_scalar(e, e, 2.0 ** -6, 1.5 * 2.0 ** 20, ALU.max, ALU.mult).then_inc(S[step], 1)
                dve.wait_ge(S[step], base + 2)
                dve.tensor_tensor(q, v, e, ALU.add).then_inc(S[step], 1)
                dve.wait_ge(S[step], base + 3)
                dve.tensor_tensor(q, q, e, ALU.subtract).then_inc(S[q_s], 1)
                dve.wait_ge(S[q_s], h + 1)
                dve.wait_ge(S[ovf_s], h + 1)
                dve.scalar_tensor_tensor(dst, ovf, 0.0, q, ALU.mult, ALU.add).then_inc(S["xq_s"], 1)

            for h in range(2):
                moments(4, h, lambda t: dve.wait_ge(S["x3_s"], t // TPB + 1))
            for h in range(2):
                scaled(4, h, f16.rearrange("p (t d) -> p t d", t=NT))
            to_e4m3(kq[:, :], kv, ke, kr, kovf[:, :],
                    "fv_s", "f_s", 0, "q_s", "ovf_s", 0)
            for h in range(2):
                cols = slice(h * HALF, (h + 1) * HALF)
                to_e4m3(xq[:, cols], fv[:, cols], fe[:, cols], fq[:, cols], fovf[:, cols],
                        "fv_s", "f_s", 3 * (h + 1), "q_s", "ovf_s", h + 1)
            for h in range(2):
                cols = slice(h * HALF, (h + 1) * HALF)
                tiles = slice(h * TPH, (h + 1) * TPH)
                dve.wait_ge(S["f_ps"], h + 1)
                dve.tensor_scalar(yb[:, cols], bk[2 + h][:, :], rs[:, 2:3], None, ALU.mult).then_inc(S["y_s"], 1)
                dve.wait_ge(S["y_s"], 2 * h + 1)
                dve.tensor_tensor(yz[:, cols].rearrange("p (t d) -> p t d", t=TPH),
                                  yb[:, cols].rearrange("p (t d) -> p t d", t=TPH),
                                  fb[:, :].unsqueeze(1).broadcast_to([P, TPH, P]), ALU.add).then_inc(S["y_s"], 1)
                dve.wait_ge(S["y_s"], 2 * h + 2)
                dve.tensor_tensor(res[:, tiles, :], xs[:, tiles, :], yz[:, cols].rearrange("p (t d) -> p t d", t=TPH),
                                  ALU.add).then_inc(S["out_s"], 1)

        @block.tensor
        def _(pe):
            def three(out, w, x, start, stop):
                pe.matmul(out, w[0], x[0], start=start, stop=False)
                pe.matmul(out, w[0], x[1], start=False, stop=False)
                return pe.matmul(out, w[1], x[0], start=False, stop=stop)

            def turn(ln, out, banks):
                for h in range(2):
                    for t in range(TPH):
                        pe.wait_ge(S[ln], h * TPH + t + 1)
                        ins = pe.transpose(bk[banks[h]][:, t * P:(t + 1) * P], xn[:, h * TPH + t, :], ident)
                    ins.then_inc(S[out], 1)

            pe.wait_ge(S["ld_par"], 80)
            turn("ln1", "cT_ps", (0, 1))
            pe.wait_ge(S["ld_ctx"], 32)
            for b in range(BATCH):
                pe.wait_ge(S["cpT_ev"], b // 2 + 1)
                for t in range(TPB):
                    tile = b * TPB + t
                    ins = pe.matmul(bk[2 + b][:, t * SEQ:(t + 1) * SEQ], cpT[:, tile * P:(tile + 1) * P],
                                    ctxT[:, b * SEQ:(b + 1) * SEQ], start=True, stop=True)
                ins.then_inc(S["s_ps"], 1)
            pe.wait_ge(S["cT_ev"], 2)
            for t in range(NT):
                ins = pe.matmul(bk[7][:, t:t + 1], cT[:, t * P:(t + 1) * P], small[:, S_WC:S_WC + 1],
                                start=True, stop=True)
            ins.then_inc(S["cw_ps"], 1)
            pe.wait_ge(S["cv_s"], 1)
            for h in range(2):
                for t in range(TPH):
                    ins = pe.matmul(bk[h][0:1, t * P:(t + 1) * P], cv[:, h * TPH + t:h * TPH + t + 1], ident,
                                    start=True, stop=True)
                ins.then_inc(S["row_ps"], 1)
            for b in range(BATCH):
                for t in range(TPB):
                    tile = b * TPB + t
                    pe.wait_ge(S["s_norm"], b * TPB + TPB)
                    for q in range(TPB):
                        ins = pe.transpose(bk[2 + b][:, q * SEQ + t * P:q * SEQ + (t + 1) * P],
                                           att[:, tile, q * P:(q + 1) * P], ident)
                ins.then_inc(S["aT_ps"], 1)
            pe.wait_ge(S["row_inv"], 1)
            for t in range(NT):
                b = t // TPB
                ins = pe.matmul(bk[7][:, 16 + t:17 + t], brow[:, t * P:(t + 1) * P],
                                bden[:, BATCH + b:BATCH + b + 1], start=True, stop=True)
            ins.then_inc(S["bcol_ps"], 1)
            for b in range(BATCH):
                pe.wait_ge(S["aT_ev"], b + 1)
                for q in range(TPB):
                    ins = pe.matmul(bk[b // 2][:, (b % 2) * SEQ:(b % 2 + 1) * SEQ], ctx[:, b * TPB + q, :],
                                    attT[:, b, q, :], start=q == 0, stop=q == TPB - 1)
                if b % 2:
                    ins.then_inc(S["c2q_ps"], 1)
            pe.wait_ge(S["bcol_ev"], 1)
            for b in range(BATCH):
                for t in range(TPB):
                    tile = b * TPB + t
                    ins = pe.matmul(bk[7][:, 32 + b:33 + b], xn[:, tile, :], bcol[:, tile:tile + 1],
                                    start=t == 0, stop=t == TPB - 1)
            ins.then_inc(S["q2c_ps"], 1)
            pe.wait_ge(S["ld_att"], 7 * 16)
            for h in range(2):
                for t in range(TPH):
                    tile = h * TPH + t
                    ins = pe.matmul(bk[2 + h][:, t * P:(t + 1) * P], ctxT[:, tile * P:(tile + 1) * P], wv[:, :],
                                    start=True, stop=True)
                ins.then_inc(S["v_ps"], 1)
            for h in range(2):
                pe.wait_ge(S["cc_ev"], h + 1)
                for t in range(TPH):
                    tile = h * TPH + t
                    b = tile // TPB
                    out = bk[4 + h][:, t * P:(t + 1) * P]
                    cols = slice(tile * P, (tile + 1) * P)
                    pe.matmul(out, c2qT[:, cols], wl[:, 1, :], start=True, stop=False)
                    pe.matmul(out, ccT[:, cols], wl[:, 2, :], start=False, stop=False)
                    pe.wait_ge(S["w14_s"], b + 1)
                    ins = pe.matmul(out, cT[:, cols], w14[:, b, :], start=False, stop=True)
                ins.then_inc(S["z_ps"], 1)
            turn("ln2", "xT_ps", (5, 6))

            def logits():
                pe.wait_ge(S["wg_lo"], 1)
                for tile in range(NT):
                    cols = slice(tile * P, (tile + 1) * P)
                    ins = three(bk[7][:, tile * E:(tile + 1) * E], (xT[:, 0, cols], xT[:, 1, cols]),
                                (wgs[:, 0, :], wgs[:, 1, :]), True, True)
                ins.then_inc(S["logit_ps"], 1)

            def up(n, pair, parity, h, first):
                if h == 0:
                    pe.wait_ge(S[f"staged{parity}"], 16 * pair + 16)
                cols = slice(h * HALF, (h + 1) * HALF)
                x = (xT[:, 0, cols], xT[:, 1, cols])
                for k in range(HB):
                    for w, used in enumerate(("gate_s", "hid_s")):
                        if not first:
                            pe.wait_ge(S[used], HB * (n - 1) + k + 1)
                        c0 = w * HID + k * P
                        ins = three(bk[2 * k + w][:, :], (w12s[:, parity, 0, c0:c0 + P], w12s[:, parity, 1, c0:c0 + P]),
                                    x, True, True)
                    ins.then_inc(S["uv_ps"], 1)

            def down(n, e, h, first):
                pe.wait_ge(S["hid_lo"], HB * (n + 1))
                if not first:
                    pe.wait_ge(S["y_acc"], TPH * (n - 1))
                for t in range(TPH):
                    for k in range(HB):
                        rows = slice(t * P, (t + 1) * P)
                        c0 = k * P
                        pick = (lambda s: w3[:, e, s, c0:c0 + P]) if isinstance(e, int) else \
                            (lambda s: w3[:, bass.ds(e, 1), s, c0:c0 + P].rearrange("p a c -> p (a c)"))
                        ins = three(bk[4 + h][:, t * P:(t + 1) * P],
                                    (hids[:, n_parity(h), 0, k, rows], hids[:, n_parity(h), 1, k, rows]),
                                    (pick(0), pick(1)), k == 0, k == HB - 1)
                ins.then_inc(S["y_ps"], 1)

            def n_parity(h):
                return h

            pe.wait_ge(S["xT_lo"], 1)
            pe.wait_ge(S["v_ev"], 2)
            up(0, 0, 0, 0, True)
            pe.wait_ge(S["xT_lo"], 2)
            logits()
            up(1, 0, 0, 1, False)
            pe.wait_ge(S["w3_lo"], E // 2)
            for n in range(2, 4):
                up(n, 0, 1, n % 2, False)
                down(n - 2, 0, n % 2, True)
            with pe.Fori(1, UNITS // 4) as i:
                for j in range(4):
                    up(4 * i + j, i, j // 2, j % 2, False)
                    down(4 * i + j - 2, 2 * i + j // 2 - 1, j % 2, False)
            down(UNITS - 2, E - 1, 0, False)
            down(UNITS - 1, E - 1, 1, False)
            turn("ln3", "x3T_ps", (0, 1))

            def project(m, g, b, first, late):
                if not first:
                    pe.wait_ge(S["ks_s"], m)
                if late is not None:
                    pe.wait_ge(S["ao_s"], late)
                cols = slice(b * SEQ, (b + 1) * SEQ) if isinstance(b, int) else bass.ds(SEQ * b, SEQ)
                for a, src in enumerate((xT, ctxTs)):
                    ins = three(bk[0][:, a * SEQ:(a + 1) * SEQ],
                                (wqk[:, 0, a, g * P:(g + 1) * P], wqk[:, 1, a, g * P:(g + 1) * P]),
                                (src[:, 0, cols], src[:, 1, cols]), True, True)
                ins.then_inc(S["proj_ps"], 1)

            def scores(m, g, r, first):
                pe.wait_ge(S["qs_s"], m + 1)
                pe.wait_ge(S["km_act"], m + 1)
                pe.wait_ge(S["km_dve"], m + 1)
                if not (first and r < 2):
                    pe.wait_ge(S["s1_max"], 4 * m + r - 1)
                t, pair = r // 2, r % 2
                pe.matmul(bk[1 + r % 2][:, :], qs[:, g, t * P:(t + 1) * P],
                          km[:, g, 2 * pair:2 * pair + 2, :].rearrange("p h k -> p (h k)"),
                          start=True, stop=True).then_inc(S["s1_ps"], 1)

            def turn_maxima(m, first):
                pe.wait_ge(S["s1_max"], 4 * (m + 1))
                if not first:
                    pe.wait_ge(S["o_ev"], m - 1)
                for t in range(TPB):
                    ins = pe.transpose(bk[7][:, t * P:(t + 1) * P], negm[:, t, :], ident)
                ins.then_inc(S["mT_ps"], 1)

            def shifted_scores(m, g, r, first):
                pe.wait_ge(S["qa_s"], m + 1)
                if not first:
                    pe.wait_ge(S["p_s"], 2 * (m - 1) + r + 1)
                for a in range(2):
                    j = 2 * r + a
                    for t in range(TPB):
                        ins = pe.matmul(bk[3 + j][:, t * SEQ:(t + 1) * SEQ], km[:, g, j, t * P:(t + 1) * P],
                                        qa[:, g, :], start=True, stop=True)
                ins.then_inc(S["s2_ps"], 1)

            def outputs(m, g, b, qa_done):
                pe.wait_ge(S["p_s"], 2 * m + 2)
                pe.wait_ge(S["v_s"], b + 1)
                pe.wait_ge(S["qa_s"], qa_done)
                for j in range(HPG):
                    for t in range(TPB):
                        ins = pe.matmul(bk[7][QUAD * j:QUAD * (j + 1), SEQ:2 * SEQ], vones[:, t, g * HPG + j, :],
                                        probs[:, g % 2, j, t, :], start=t == 0, stop=t == TPB - 1,
                                        tile_position=(0, QUAD * j))
                ins.then_inc(S["pv_ps"], 1)

            def turn_outputs(b):
                pe.wait_ge(S["o_ev"], G * (b + 1))
                for t in range(TPB):
                    bank = bk[7] if t == 0 else bk[0]
                    for g in range(G):
                        ins = pe.transpose(bank[:, g * P:(g + 1) * P], os_[:, g, t * P:(t + 1) * P], ident)
                    ins.then_inc(S["oT_ps"], 1)

            def turn_normalised(b):
                pe.wait_ge(S["ao_s"], 2 * (b + 1))
                for t in range(TPB):
                    ins = pe.transpose(bk[7][:, t * P:(t + 1) * P], ao[:, t, :], ident)
                ins.then_inc(S["aoT_ps"], 1)

            def output_layer(b):
                pe.wait_ge(S["aoT_ev"], b + 1)
                for t in range(TPB):
                    ins = pe.matmul(bk[7][:, t * P:(t + 1) * P], aoT[:, t * P:(t + 1) * P], wo[:, :],
                                    start=True, stop=True)
                ins.then_inc(S["wo_ps"], 1)

            def pe_batch(b, first, last):
                for g in range(G):
                    m = G * b + g
                    more = not (last and g == G - 1)
                    if not first and g == 1:
                        pe.wait_ge(S["qa_s"], m + 1)
                        pe.wait_ge(S["ks_s"], m + 2 if not last or g < 3 else 0)
                        turn_outputs(b - 1)
                    if not first and g == 2:
                        pe.wait_ge(S["qa_s"], m + 1)
                        pe.wait_ge(S["o_ev"], m - 1)
                        turn_normalised(b - 1)
                    if not first and g == 3:
                        pe.wait_ge(S["qa_s"], m + 1)
                        pe.wait_ge(S["o_ev"], m - 1)
                        output_layer(b - 1)
                    if g != 1 and not (last and g >= 2):
                        project(m + 2, (g + 2) % G, b + (g + 2) // G, False, None)
                    if more:
                        scores(m + 1, (g + 1) % G, 0, False)
                        scores(m + 1, (g + 1) % G, 1, False)
                    shifted_scores(m, g, 0, first and g == 0)
                    if g == 1:
                        project(m + 2, (g + 2) % G, b, False, None if first else TPB * b)
                    if more:
                        scores(m + 1, (g + 1) % G, 2, False)
                    shifted_scores(m, g, 1, first and g == 0)
                    if more:
                        scores(m + 1, (g + 1) % G, 3, False)
                    if not first and g == 1:
                        pe.wait_ge(S["ao_s"], TPB * b)
                    if not first and g == 2:
                        pe.wait_ge(S["aoT_ev"], b)
                    if not first and g == 3:
                        pe.wait_ge(S["x3_s"], b)
                    if not (first and g == 0):
                        outputs(m - 1, (g - 1) % G, b if g else b - 1, m + 1)
                    if more:
                        turn_maxima_after(m + 1, first and g == 0)

            def turn_maxima_after(m, first):
                pe.wait_ge(S["s1_max"], 4 * (m + 1))
                if first:
                    pe.wait_ge(S["qa_s"], m)
                else:
                    pe.wait_ge(S["o_ev"], m - 1)
                for t in range(TPB):
                    ins = pe.transpose(bk[7][:, t * P:(t + 1) * P], negm[:, t, :], ident)
                ins.then_inc(S["mT_ps"], 1)

            pe.wait_ge(S["x3T_lo"], 2)
            pe.wait_ge(S["ctx_lo"], 1)
            pe.wait_ge(S["wqk_lo"], 1)
            project(0, 0, 0, True, None)
            project(1, 1, 0, False, None)
            for r in range(4):
                scores(0, 0, r, True)
            turn_maxima(0, True)
            pe_batch(0, True, False)
            with pe.Fori(1, BATCH - 1) as b:
                pe_batch(b, False, False)
            pe_batch(BATCH - 1, False, True)
            last = G * BATCH - 1
            pe.wait_ge(S["o_ev"], last)
            outputs(last, G - 1, BATCH - 1, last + 1)
            turn_outputs(BATCH - 1)
            turn_normalised(BATCH - 1)
            output_layer(BATCH - 1)

            pe.wait_ge(S["ident16_s"], 1)
            for h in range(2):
                pe.wait_ge(S["xq_s"], h + 2)
                for t in range(TPH):
                    tile = h * TPH + t
                    ins = pe.transpose(bk[h][:, t * P // 2:(t + 1) * P // 2].bitcast(bf16),
                                       xq[:, tile * P:(tile + 1) * P], ident16[:, :])
                ins.then_inc(S["fT_ps"], 1)
            for h in range(2):
                pe.wait_ge(S["fT_ev"], h + 1)
                for t in range(TPH):
                    tile = h * TPH + t
                    ins = pe.matmul(bk[2 + h][:, t * P:(t + 1) * P], xqT[:, tile * P:(tile + 1) * P], kq[:, :],
                                    start=True, stop=True)
                ins.then_inc(S["f_ps"], 1)


def kernel(**inputs):
    import numpy as np
    import concourse.bacc as bacc
    from concourse import mybir
    from concourse.bass_utils import run_bass_kernel_spmd as run

    a = {k: np.asarray(v) for k, v in inputs.items()}

    def rows(v):
        return np.ascontiguousarray(np.broadcast_to(v.reshape(1, -1), (P, v.size)))

    def tiles(v):
        return np.ascontiguousarray(v.reshape(NT, P, P).transpose(1, 0, 2))

    def stacked(w):
        out = np.zeros((P, G, HPG, 4, HD), w.dtype)
        out[:, :, :, 0:3, :] = w.reshape(P, G, HPG, 1, HD)
        return out.reshape(P, G * P)

    const = np.zeros((P, N_CONST), np.float32)
    row = np.arange(P) % QUAD
    const[:, C_AQ] = -1.0 * (row // HD == 1)
    const[:, C_AK] = -1.0 * (row // HD == 2) + 1.0 * (row == SHIFT_ROW)
    const[:, C_ONE] = row == SHIFT_ROW
    const[:, C_IOTA:C_IOTA + E] = np.arange(E)
    const[:, C_ID:C_ID + P] = np.eye(P)
    small = np.concatenate(
        [a["L0_xattn_w_cq"].reshape(P, 1), a["L0_xattn_w_q"].reshape(P, 1), a["L0_xattn_w_c"].reshape(P, 1),
         rows(a["L0_xattn_b_cq"]), rows(a["L0_xattn_b_c"]), rows(a["L0_xattn_b_q"]),
         rows(a["L1_ffn_input_scale"]), rows(a["L1_ffn_kernel_scale"])], axis=1)
    arrays = {
        "x": tiles(a["x"]), "ctx": tiles(a["ctx_1024"]), "ctxT": np.ascontiguousarray(a["ctx_1024"].reshape(TOK, P).T),
        "small": small, "const": const,
        "wl": np.ascontiguousarray(a["L0_xattn_W_l"].T.reshape(4, P, P).transpose(1, 0, 2)),
        "bl": rows(a["L0_xattn_b_l"]), "wg": a["L0_ffn_Wg"],
        "w12": np.ascontiguousarray(np.concatenate([a["L0_ffn_W1"], a["L0_ffn_W2"]], axis=2).transpose(1, 0, 2)),
        "w3": np.ascontiguousarray(a["L0_ffn_W3"].reshape(E, HB, P, P).transpose(2, 0, 1, 3).reshape(P, E, HB * P)),
        "wq": stacked(a["L1_xattn_W_q"]), "wk": stacked(a["L1_xattn_W_k"]), "wv": a["L1_xattn_W_v"],
        "wo": a["L1_xattn_W_o"], "bo": rows(a["L1_xattn_b_o"]), "fk": a["L1_ffn_kernel"], "fb": rows(a["L1_ffn_bias"]),
    }
    nc = bacc.Bacc("TRN2", target_bir_lowering=False, num_devices=1)
    args = [nc.dram_tensor(f"in_{k}", v.shape, mybir.dt.from_np(v.dtype), kind="ExternalInput").ap()
            for k, v in arrays.items()]
    out = nc.dram_tensor("out", (P, NT, P), mybir.dt.float32, kind="ExternalOutput").ap()
    build(nc, *args, out)
    r = run(nc, [{f"in_{k}": np.ascontiguousarray(v) for k, v in arrays.items()}], core_ids=[0])
    return r.results[0]["out"].transpose(1, 0, 2).reshape(BATCH, SEQ, P)
```

```python
import concourse.bass as bass
from concourse import mybir
from contextlib import ExitStack

P = 128
BATCH, SEQ = 4, 256
TOK = BATCH * SEQ
NT = TOK // P
TPB = SEQ // P
HALF = TOK // 2
TPH = NT // 2
E, HID = 8, 256
HB = HID // P
HALVES = ((0, TPH), (TPH, NT))
CHUNKS = ((0, TPH), (TPH, NT - TPB), (NT - TPB, NT))
UNITS = 2 * E
HEADS, HD = 16, 8
HPG = 4
G = HEADS // HPG
QUAD = 32
SHIFT_ROW = 24
WARM_UP = 10
EPS = 1e-5
ATT_SCALE = HD ** -0.5
C_AQ, C_AK, C_ONE, C_IOTA, C_ID = 0, 1, 2, 3, 3 + E
C_ZERO = C_IOTA
N_CONST = C_ID + P
S_WCQ, S_WQ, S_WC, S_B, S_SIN, S_SK, N_SMALL = 0, 1, 2, 3, 6, 7, 8


def build(nc, x_d, ctx_d, ctxT_d, small_d, const_d, wl_d, bl_d, wg_d, w12_d, w3_d,
          wq_d, wk_d, wv_d, wo_d, bo_d, fk_d, fb_d, rw_d, out_d):
    fp32, r32 = mybir.dt.float32, mybir.dt.float32r
    bf16, fp16 = mybir.dt.bfloat16, mybir.dt.float16
    i32, u32 = mybir.dt.int32, mybir.dt.uint32
    ALU = mybir.AluOpType
    ACT = mybir.ActivationFunctionType
    AX = mybir.AxisListType

    stack = ExitStack()
    with stack:
        def sb(name, shape, dt=fp32):
            return stack.enter_context(nc.sbuf_tensor(name, shape, dt))

        def sem(name):
            return stack.enter_context(nc.semaphore(name))

        def plain(ap):
            return ap.bitcast(fp32)

        const = sb("const", [P, N_CONST])
        small = sb("small", [P, N_SMALL])
        ident = const[:, C_ID:C_ID + P]
        ident16 = sb("ident16", [P, P], bf16)
        expo = sb("expo", [P, NT])
        wl = sb("wl", [P, 4, P])
        bl = sb("bl", [P, P])
        wg = sb("wg", [P, E])
        wgs = sb("wgs", [P, 2, E], r32)
        raw = sb("raw", [P, E * 2 * HID + E * HB * P])
        w12raw = raw[:, 0:E * 2 * HID].rearrange("p (e c) -> p e c", e=E)
        w3raw = raw[:, E * 2 * HID:].rearrange("p (e c) -> p e c", e=E)
        WX = 2 * HID + HB * P
        wx = sb("wx", [P, E, 2, WX], r32)
        w12, w3 = wx[:, :, :, 0:2 * HID], wx[:, :, :, 2 * HID:WX]
        wxs = sb("wxs", [P, 2, 2, WX], r32)
        wqkraw = sb("wqkraw", [P, 2, G * P])
        wqk = sb("wqk", [P, 2, 2, G * P], r32)
        wv = sb("wv", [P, P])
        wo = sb("wo", [P, P])
        bo = sb("bo", [1, P])
        ones = sb("ones", [1, P])
        fk = sb("fk", [P, P], bf16)
        fb = sb("fb", [P, P], bf16)

        xs = sb("xs", [P, NT, P])
        xn = sb("xn", [P, NT, P])
        xT = sb("xT", [P, 2, TOK], r32)
        ctx = sb("ctx", [P, NT, P])
        ctxT = sb("ctxT", [P, TOK])
        ctxTs = sb("ctxTs", [P, 2, TOK], r32)
        stats = sb("stats", [P, NT, 6])
        mv = sb("mv", [P, NT, 2])
        vpe = sb("vpe", [P, NT])
        rstd = sb("rstd", [P, NT])

        cT = sb("cT", [P, TOK])
        cpT = sb("cpT", [P, TOK])
        att = sb("att", [P, NT, SEQ])
        attT = sb("attT", [P, BATCH, TPB, SEQ])
        c2qT = cpT
        ccT = sb("ccT", [P, TOK])
        nmax = sb("nmax", [P, NT])
        rsum = sb("rsum", [P, NT])
        rinv = sb("rinv", [P, NT])
        bsum = sb("bsum", [P, 2])
        cv = sb("cv", [P, NT])
        bnmax = sb("bnmax", [1, BATCH])
        brow = ccT[0:1, :]
        bden = sb("bden", [1, 2 * BATCH])
        bcol = sb("bcol", [P, NT])
        q2c = sb("q2c", [P, BATCH])
        w14 = sb("w14", [P, BATCH, P])

        logit = sb("logit", [P, NT, E])
        top = sb("top", [P, NT, 8])
        topi = sb("topi", [P, NT, 8], u32)
        topf = sb("topf", [P, NT, 2])
        gap = sb("gap", [P, 4, NT])
        route = sb("route", [P, 3, NT, E])
        rw = sb("rw", [P, NT, E])
        rwT = sb("rwT", [E, TOK])
        logitT = rwT
        rwb = sb("rwb", [P, 2, TOK])
        accT = cpT
        yw = ccT[:, :].rearrange("p (u t) -> p u t", u=2)
        att_flat = att[:, :, :].rearrange("p t q -> p (t q)")
        tanhs = att_flat[:, 0:TOK].rearrange("p (k t) -> p k t", k=HB)
        gated = att_flat[:, TOK:2 * TOK].rearrange("p (k t) -> p k t", k=HB)
        hid = attT[:, 0:2, :, :].rearrange("p a b c -> p a (b c)")
        hids = sb("hids", [P, 2, 2, HB, HALF], r32)

        vall = sb("vall", [P, NT, P])
        vones = sb("vones", [P, TPB, HEADS, QUAD])
        wx_flat = wx[:, :, :, :].rearrange("p e s c -> p (e s c)")
        km = wx_flat[:, 0:G * HPG * SEQ].rearrange("p (g h k) -> p g h k", g=G, h=HPG)
        qs, qa = (wx_flat[:, (G * HPG + G * n) * SEQ:(G * HPG + G * (n + 1)) * SEQ]
                  .rearrange("p (g q) -> p g q", g=G) for n in range(2))
        N_PROBS = HPG * TPB * SEQ
        probs = raw[:, 0:2 * N_PROBS].rearrange("p (u h k q) -> p u h k q", u=2, h=HPG, k=TPB)
        rest = raw[:, 2 * N_PROBS:]
        ks = rest[:, 0:2 * SEQ].rearrange("p (u k) -> p u k", u=2)
        hiQ = rest[:, 2 * SEQ:3 * SEQ]
        hiK = rest[:, 3 * SEQ:4 * SEQ]
        os_ = rest[:, 4 * SEQ:(4 + G) * SEQ].rearrange("p (g q) -> p g q", g=G)
        negm = sb("negm", [P, 2, TPB, P])
        den = sb("den", [P, TPB, G, HPG])
        ao = sb("ao", [P, TPB, P])
        aoT = sb("aoT", [P, SEQ])

        nmr = sb("nmr", [P, NT])
        rs = sb("rs", [P, 3])
        f16, xq = (cpT[:, n * HALF:(n + 1) * HALF].bitcast(bf16) for n in range(2))
        xqT, fovf = ctxT[:, 0:HALF].bitcast(bf16), ctxT[:, HALF:TOK].bitcast(fp16)
        vflat = vall[:, :, :].rearrange("p t d -> p (t d)")
        yb, yz = (vflat[:, n * HALF:(n + 1) * HALF].bitcast(bf16) for n in range(2))
        fv = ccT
        fe = attT[:, 0:2, :, :].rearrange("p a b c -> p (a b c)")
        fq = attT[:, 2:4, :, :].rearrange("p a b c -> p (a b c)")
        kq = sb("kq", [P, P], bf16)
        kovf = sb("kovf", [P, P], fp16)
        kv, ke, kr = (bl[:, :], rwb[:, 0, 0:P], rwb[:, 0, P:2 * P])
        res = cT[:, :].rearrange("p (t d) -> p t d", t=NT)

        lone = {i: stack.enter_context(nc.psum_tensor(f"bank{i}", [P, 512], fp32)) for i in (0, 1, 2, 7)}
        pair = [stack.enter_context(nc.psum_tensor(f"banks{i}{i + 1}", [P, 1024], fp32)) for i in (3, 5)]
        bk = [lone[i] if i in lone else pair[(i - 3) // 2][:, 512 * ((i - 3) % 2):512 * ((i - 3) % 2 + 1)]
              for i in range(8)]

        names = """
          ld_x ld_ctx ld_par ld_w ld_att stored setup ident16_s v_zero km_zero w12_hi w12_lo w3_hi w3_lo ctx_hi
          ctx_lo wqk_hi wqk_lo wg_hi wg_lo v_ps v_ev bl_added st1 ag1 ve1 rs1 ln1 st2 ag2 ve2 rs2 ln2 st3 ag3
          ve3 rs3 ln3 st4 ag4 ve4 rs4 ln4 ln4_act cT_ps cT_ev cpT_ev cw_ps s_ps s_max s_exp s_rinv s_norm aT_ps
          aT_ev c2q_ps c2q_ev cc_ev bsum_s cv_s row_ps row_max row_exp row_inv bcol_ps bcol_ev q2c_ps q2c_ev
          w14_s z_ps z_add xT_ps xT_hi xT_lo logitT_ps logitT_ev logit_ps logit_ev top_s topi_s gap_s gap_exp
          route_s w12_in0 w12_in1 w3_in0 w3_in1 rwT_ps rwT_ev rw_out rwb0 rwb1 uv_ps tanh_s gate_s hid_s hid_hi
          hid_lo y_ps y_w y_acc accT_ps moe_s x3T_ps x3T_hi x3T_lo early_ps proj_ps q_hi k_hi qs_s ks_s km_act
          km_pool s1_ps s1_max mT_ps qa_s s2_ps p_s v_s pv_ps o_ev oT_ps den_s ao_s aoT_ps aoT_ev wo_ps x3_s
          rs_s kv_s kovf_s fv_s q_s ovf_s f_s r_s r_pool q_pool nmr_s yz_pool out_pool xq_s fT_ps fT_ev f_ps y_s
          yz_s out_s""".split()
        S = {n: sem(n) for n in names}

        block = stack.enter_context(nc.Block())

        @block.sync
        def _(sp):
            sp.dma_start(xs[:, :, :], x_d).then_inc(S["ld_x"], 16)
            sp.dma_start(ctxT[:, :], ctxT_d).then_inc(S["ld_ctx"], 16)
            sp.dma_start(ctx[:, :, :], ctx_d).then_inc(S["ld_ctx"], 16)
            sp.dma_start(wl[:, :, :], wl_d).then_inc(S["ld_par"], 16)
            sp.dma_start(w12raw, w12_d).then_inc(S["ld_w"], 16)
            sp.dma_start(w3raw, w3_d).then_inc(S["ld_w"], 16)

            def stage(e, parity, what, used):
                if used:
                    sp.wait_ge(S[used[0]], used[1])
                c0, c1 = (0, 2 * HID) if what == "w12" else (2 * HID, WX)
                src = wx[:, e:e + 1, :, c0:c1] if isinstance(e, int) else wx[:, bass.ds(e, 1), :, c0:c1]
                sp.dma_start(plain(wxs[:, parity:parity + 1, :, c0:c1]), plain(src))\
                    .then_inc(S[f"{what}_in{parity}"], 16)

            def spread(e, parity, reused):
                if reused:
                    sp.wait_ge(S["y_w"], 2 * (e - 1))
                src = rw_d[e:e + 1, :] if isinstance(e, int) else rw_d[bass.ds(e, 1), :]
                sp.dma_start(rwb[:, parity, :], src.broadcast_to([P, TOK])).then_inc(S[f"rwb{parity}"], 16)

            sp.wait_ge(S["w12_lo"], 2)
            for parity in range(2):
                stage(parity, parity, "w12", None)
            sp.wait_ge(S["w3_lo"], 1)
            for parity in range(2):
                stage(parity, parity, "w3", None)
            sp.wait_ge(S["rwT_ev"], 2)
            sp.dma_start(rw_d, rwT[:, :]).then_inc(S["rw_out"], 16)
            sp.wait_ge(S["rw_out"], 16)
            spread(0, 0, False)
            spread(1, 1, False)
            sp.wait_ge(S["w12_lo"], E)
            sp.wait_ge(S["w3_lo"], E // 2)
            with sp.Fori(1, E // 2) as i:
                for parity in range(2):
                    e = 2 * i + parity
                    stage(e, parity, "w12", ("uv_ps", 2 * HB * (e - 1)))
                    spread(e, parity, True)
                    stage(e, parity, "w3", ("y_ps", 2 * (e - 1)))

            for c, span in enumerate(CHUNKS):
                if c == 1:
                    sp.wait_ge(S["out_pool"], 1)
                else:
                    sp.wait_ge(S["out_s"], c // 2 + 1)
                sp.dma_start(out_d[:, slice(*span), :], res[:, slice(*span), :]).then_inc(S["stored"], 16)
            sp.wait_ge(S["stored"], 16 * len(CHUNKS))

        @block.gpsimd
        def _(pool):
            pool.memset(expo[:, :], -0.5)
            pool.memset(negm[:, :, :, :], 0.0)
            pool.memset(ones[:, :], 1.0)
            pool.memset(vones[:, :, :, :], 0.0).then_inc(S["v_zero"], 1)
            pool.wait_ge(S["v_zero"], 1)
            pool.memset(vones[:, :, :, HD:HD + 1], 1.0).then_inc(S["setup"], 1)

            def inverse_deviation(n, part, span):
                tiles = slice(*span)
                pool.wait_ge(S[f"ag{n}"], span[1])
                pool.tensor_scalar(vpe[:, tiles], mv[:, tiles, 1], EPS, None, ALU.add).then_inc(S[f"ve{n}"], 1)
                pool.wait_ge(S[f"ve{n}"], part + 1)
                pool.tensor_tensor(rstd[:, tiles], vpe[:, tiles], expo[:, tiles], ALU.pow).then_inc(S[f"rs{n}"], 1)
                pool.wait_ge(S[f"rs{n}"], part + 1)

            pool.wait_ge(S["setup"], 1)
            for h in range(2):
                inverse_deviation(1, h, HALVES[h])
            def w12_lo(*experts):
                for e in experts:
                    pool.wait_ge(S["w12_hi"], e + 1)
                    pool.tensor_tensor(w12[:, e, 1, :], w12raw[:, e, :], plain(w12[:, e, 0, :]), ALU.subtract)\
                        .then_inc(S["w12_lo"], 1)

            w12_lo(0, 1, 2, 3, 4)
            inverse_deviation(2, 0, HALVES[0])
            w12_lo(5)
            inverse_deviation(2, 1, HALVES[1])
            w12_lo(6, 7)
            for e in range(0, E, 2):
                pool.wait_ge(S["w3_hi"], e // 2 + 1)
                pool.tensor_tensor(w3[:, e:e + 2, 1, :], w3raw[:, e:e + 2, :], plain(w3[:, e:e + 2, 0, :]),
                                   ALU.subtract).then_inc(S["w3_lo"], 1)
            pool.wait_ge(S["ctx_hi"], 1)
            pool.tensor_tensor(ctxTs[:, 1, :], ctxT[:, :], plain(ctxTs[:, 0, :]), ALU.subtract)\
                .then_inc(S["ctx_lo"], 1)

            def hidden_lo(n, p, first):
                for k in range(HB):
                    pool.wait_ge(S["hid_hi"], HB * n + k + 1)
                    if not first:
                        pool.wait_ge(S["y_ps"], n - 1)
                    pool.tensor_tensor(hids[:, p, 1, k, :], hid[:, k, :], plain(hids[:, p, 0, k, :]),
                                       ALU.subtract).then_inc(S["hid_lo"], 1)

            def accumulate(n, p, first):
                pool.wait_ge(S["y_w"], n + 1)
                cols = slice(p * HALF, (p + 1) * HALF)
                if first:
                    pool.tensor_copy(accT[:, cols], yw[:, p, :]).then_inc(S["y_acc"], 1)
                else:
                    pool.wait_ge(S["y_acc"], n - 1)
                    pool.tensor_tensor(accT[:, cols], accT[:, cols], yw[:, p, :], ALU.add)\
                        .then_inc(S["y_acc"], 1)

            hidden_lo(0, 0, True)
            pool.wait_ge(S["wqk_hi"], 1)
            pool.tensor_tensor(wqk[:, 1, :, :], wqkraw[:, :, :], plain(wqk[:, 0, :, :]), ALU.subtract)\
                .then_inc(S["wqk_lo"], 1)
            for n in range(1, 4):
                hidden_lo(n, n % 2, n < 2)
            for n in range(2):
                accumulate(n, n, True)
            with pool.Fori(1, UNITS // 4) as i:
                for j in range(4):
                    hidden_lo(4 * i + j, j % 2, False)
                    accumulate(4 * i + j - 2, j % 2, False)
            def values(b, first):
                if not first:
                    pool.wait_ge(S["pv_ps"], G * b)
                pool.wait_ge(S["v_ev"], 2)
                src = vall[:, TPB * b:TPB * (b + 1), :] if isinstance(b, int) else vall[:, bass.ds(TPB * b, TPB), :]
                pool.tensor_copy(vones[:, :, :, 0:HD], src.rearrange("p t (h d) -> p t h d", h=HEADS))\
                    .then_inc(S["v_s"], 1)
                pool.wait_ge(S["v_s"], b + 1)

            def masked_keys(m, g, first):
                pool.wait_ge(S["ks_s"], m + 1)
                if not first:
                    pool.wait_ge(S["s2_ps"], 2 * (m - 3))
                for j in range(2, HPG):
                    rows = slice(QUAD * j, QUAD * (j + 1))
                    pool.tensor_tensor(km[rows, g, j, :], ks[rows, g % 2, :],
                                       const[rows, C_ZERO:C_ZERO + 1].broadcast_to([QUAD, SEQ]), ALU.add)\
                        .then_inc(S["km_pool"], 1)
                    pool.wait_ge(S["km_pool"], 2 * m + j - 1)

            def pool_batch(b, first, last):
                for g in range(G):
                    if g == 1 and not first:
                        values(b, False)
                    if not (last and g >= 2):
                        masked_keys(G * b + g + 2, (g + 2) % G, first and g < 2)

            inverse_deviation(3, 0, HALVES[0])
            pool.wait_ge(S["km_zero"], 1)
            for m in range(2):
                masked_keys(m, m, True)
            inverse_deviation(3, 1, HALVES[1])
            values(0, True)
            pool_batch(0, True, False)
            with pool.Fori(1, BATCH - 1) as b:
                pool_batch(b, False, False)
            pool_batch(BATCH - 1, False, True)
            inverse_deviation(4, 0, CHUNKS[0])
            inverse_deviation(4, 1, CHUNKS[1])
            cols = slice(0, CHUNKS[0][1] * P)
            pool.wait_ge(S["f_s"], 4)
            pool.tensor_tensor(fq[:, cols], fv[:, cols], fe[:, cols], ALU.add).then_inc(S["r_pool"], 1)
            inverse_deviation(4, 2, CHUNKS[2])
            pool.wait_ge(S["r_pool"], 1)
            pool.tensor_tensor(fq[:, cols], fq[:, cols], fe[:, cols], ALU.subtract).then_inc(S["q_pool"], 1)

            cols, tiles, n = slice(CHUNKS[1][0] * P, CHUNKS[1][1] * P), slice(*CHUNKS[1]), CHUNKS[1][1] - CHUNKS[1][0]
            pool.wait_ge(S["y_s"], 2)
            pool.tensor_tensor(yz[:, cols].rearrange("p (t d) -> p t d", t=n),
                               yb[:, cols].rearrange("p (t d) -> p t d", t=n),
                               fb[:, :].unsqueeze(1).broadcast_to([P, n, P]), ALU.add).then_inc(S["yz_pool"], 1)
            pool.wait_ge(S["yz_pool"], 1)
            pool.tensor_tensor(res[:, tiles, :], xs[:, tiles, :], yz[:, cols].rearrange("p (t d) -> p t d", t=n),
                               ALU.add).then_inc(S["out_pool"], 1)

        @block.scalar
        def _(act):
            act.dma_start(const[:, :], const_d).then_inc(S["ld_par"], 16)
            act.dma_start(small[:, :], small_d).then_inc(S["ld_par"], 16)
            act.dma_start(bl[:, :], bl_d).then_inc(S["ld_par"], 16)
            act.dma_start(wg[:, :], wg_d).then_inc(S["ld_par"], 16)
            for dst, src in ((wqkraw[:, 0, :], wq_d), (wqkraw[:, 1, :], wk_d), (wv[:, :], wv_d),
                             (wo[:, :], wo_d), (bo[:, :], bo_d), (fk[:, :], fk_d), (fb[:, :], fb_d)):
                act.dma_start(dst, src).then_inc(S["ld_att"], 16)
            act.wait_ge(S["ld_par"], 80)
            act.copy(ident16[:, :], ident).then_inc(S["ident16_s"], 1)

            for h in range(2):
                cols = slice(h * HALF, (h + 1) * HALF)
                act.wait_ge(S["cT_ps"], h + 1)
                act.activation(cpT[:, cols], bk[h][:, :], ACT.Identity, scale=small[:, S_WCQ:S_WCQ + 1],
                               bias=small[:, S_WQ:S_WQ + 1]).then_inc(S["cpT_ev"], 1)
                act.copy(cT[:, cols], bk[h][:, :]).then_inc(S["cT_ev"], 1)
            def w12_hi(*experts):
                act.wait_ge(S["ld_w"], 32)
                for e in experts:
                    act.copy(w12[:, e, 0, :], w12raw[:, e, :]).then_inc(S["w12_hi"], 1)

            def row_exp(b):
                act.wait_ge(S["row_max"], b // 2 + 1)
                c0 = (b % 2) * SEQ
                act.activation(brow[:, b * SEQ:(b + 1) * SEQ], bk[b // 2][0:1, c0:c0 + SEQ], ACT.Exp,
                               bias=bnmax[:, b:b + 1], accum_out=bden[:, b:b + 1]).then_inc(S["row_exp"], 1)

            def turned(b):
                act.wait_ge(S["aT_ps"], b + 1)
                act.copy(attT[:, b, :, :], bk[2 + b][:, :]).then_inc(S["aT_ev"], 1)

            for t in range(NT):
                act.wait_ge(S["s_max"], t // TPB + 1)
                c0 = (t % TPB) * SEQ
                act.activation(att[:, t, :], bk[2 + t // TPB][:, c0:c0 + SEQ], ACT.Exp,
                               bias=nmax[:, t:t + 1], accum_out=rsum[:, t:t + 1]).then_inc(S["s_exp"], 1)
            act.copy(wgs[:, 0, :], wg[:, :]).then_inc(S["wg_hi"], 1)
            w12_hi(0, 1)
            turned(0)
            turned(1)
            for b in range(BATCH):
                row_exp(b)
            act.wait_ge(S["ld_att"], 7 * 16)
            act.wait_ge(S["rs_s"], 2)
            act.wait_ge(S["bl_added"], 1)
            act.activation(kv, fk[:, :], ACT.Copy, scale=rs[:, 1:2]).then_inc(S["kv_s"], 1)
            turned(2)
            turned(3)

            def query_context(h):
                act.wait_ge(S["c2q_ps"], h + 1)
                act.copy(c2qT[:, h * HALF:(h + 1) * HALF], bk[h][:, :]).then_inc(S["c2q_ev"], 1)

            query_context(0)
            act.wait_ge(S["bcol_ps"], 1)
            act.copy(bcol[:, :], bk[7][:, 16:16 + NT]).then_inc(S["bcol_ev"], 1)
            w12_hi(2)
            query_context(1)
            act.wait_ge(S["q_s"], 1)
            act.activation(kovf[:, :], kr, ACT.Copy, scale=144.0).then_inc(S["kovf_s"], 1)
            w12_hi(3, 4)
            act.wait_ge(S["q2c_ps"], 1)
            act.copy(q2c[:, :], bk[7][:, 32:32 + BATCH]).then_inc(S["q2c_ev"], 1)
            w12_hi(5, 6, 7)
            for e in range(0, E, 2):
                act.copy(w3[:, e:e + 2, 0, :], w3raw[:, e:e + 2, :]).then_inc(S["w3_hi"], 1)
            for h in range(2):
                act.wait_ge(S["v_ps"], h + 1)
                act.copy(vall[:, h * TPH:(h + 1) * TPH, :], bk[6 + h][:, :]).then_inc(S["v_ev"], 1)
            act.copy(ctxTs[:, 0, :], ctxT[:, :]).then_inc(S["ctx_hi"], 1)
            for h in range(2):
                act.wait_ge(S["xT_ps"], h + 1)
                act.copy(xT[:, 0, h * HALF:(h + 1) * HALF], bk[4 + h][:, :]).then_inc(S["xT_hi"], 1)
            def gates(n, first):
                for k in range(HB):
                    act.wait_ge(S["uv_ps"], HB * n + k + 1)
                    if not first:
                        act.wait_ge(S["gate_s"], HB * (n - 1) + k + 1)
                    act.activation(tanhs[:, k, :], bk[2 * k][:, :], ACT.Tanh, scale=0.5).then_inc(S["tanh_s"], 1)

            def hidden_hi(n, p, early):
                for k in range(HB):
                    act.wait_ge(S["hid_s"], HB * n + k + 1)
                    if not early:
                        act.wait_ge(S["y_ps"], n - 1)
                    act.copy(hids[:, p, 0, k, :], hid[:, k, :]).then_inc(S["hid_hi"], 1)

            gates(0, True)
            for h in range(2):
                act.wait_ge(S["logitT_ps"], h + 1)
                act.copy(logitT[:, h * HALF:(h + 1) * HALF], bk[4 + 3 * h][0:E, :]).then_inc(S["logitT_ev"], 1)
            hidden_hi(0, 0, True)
            act.copy(wqk[:, 0, :, :], wqkraw[:, :, :]).then_inc(S["wqk_hi"], 1)
            act.wait_ge(S["gap_s"], 1)
            act.activation(gap[:, 1, :], gap[:, 0, :], ACT.Exp).then_inc(S["gap_exp"], 1)
            gates(1, False)
            for h in range(2):
                act.wait_ge(S["rwT_ps"], h + 1)
                act.copy(rwT[:, h * HALF:(h + 1) * HALF], bk[4 + h][0:E, :]).then_inc(S["rwT_ev"], 1)
            hidden_hi(1, 1, True)
            gates(2, False)
            hidden_hi(2, 0, False)
            gates(3, False)
            hidden_hi(3, 1, False)
            with act.Fori(1, UNITS // 4) as i:
                for j in range(4):
                    gates(4 * i + j, False)
                    hidden_hi(4 * i + j, j % 2, False)
            def norm_hi(h):
                act.wait_ge(S["x3T_ps"], h + 1)
                act.copy(xT[:, 0, h * HALF:(h + 1) * HALF], bk[3 + h][:, :]).then_inc(S["x3T_hi"], 1)

            def queries_hi(m):
                if not (isinstance(m, int) and m == 0):
                    act.wait_ge(S["qs_s"], m)
                act.copy(hiQ.bitcast(r32), bk[0][:, 0:SEQ]).then_inc(S["q_hi"], 1)

            def keys_hi(m):
                if not (isinstance(m, int) and m == 0):
                    act.wait_ge(S["ks_s"], m)
                act.activation(hiK.bitcast(r32), bk[0][:, SEQ:2 * SEQ], ACT.Identity,
                               bias=const[:, C_ONE:C_ONE + 1]).then_inc(S["k_hi"], 1)

            def proj_hi(m):
                act.wait_ge(S["proj_ps"], m + 1)
                queries_hi(m)
                keys_hi(m)

            def masked_keys(m, g, first):
                act.wait_ge(S["ks_s"], m + 1)
                if not first:
                    act.wait_ge(S["s2_ps"], 2 * (m - 3))
                for j in range(2):
                    rows = slice(QUAD * j, QUAD * (j + 1))
                    ins = act.copy(km[rows, g, j, :], ks[rows, g % 2, :])
                ins.then_inc(S["km_act"], 1)

            def exps(m, g, r, first):
                act.wait_ge(S["s2_ps"], 2 * m + r + 1)
                if not first:
                    act.wait_ge(S["pv_ps"], m - 1)
                act.activation(probs[:, g % 2, 2 * r:2 * r + 2, :, :].rearrange("p h k q -> p (h k q)"), pair[r][:, :],
                               ACT.Exp, scale=ATT_SCALE).then_inc(S["p_s"], 1)

            def o_copy(m, g, bank=7):
                act.wait_ge(S["pv_ps"], m + 1)
                act.copy(os_[:, g, :], bk[bank][:, SEQ:2 * SEQ]).then_inc(S["o_ev"], 1)

            def act_batch(b, first, last):
                for g in range(G):
                    m = G * b + g
                    ahead = not (last and g >= 2)
                    if not first or g >= 2:
                        o_copy(m - 2, (g - 2) % G)
                    if ahead:
                        masked_keys(m + 2, (g + 2) % G, first and g < 2)
                    exps(m, g, 0, first and g < 2)
                    if g == 2 and not first:
                        act.wait_ge(S["aoT_ps"], b)
                        act.copy(aoT[:, :], bk[7][:, 0:SEQ]).then_inc(S["aoT_ev"], 1)
                    if not (last and g >= 1):
                        proj_hi(m + 3)
                    exps(m, g, 1, first and g < 2)

            for parity in range(2):
                act.wait_ge(S[f"w12_in{parity}"], 16 * E // 2)
                act.wait_ge(S[f"w3_in{parity}"], 16 * E // 2)
            act.copy(wx_flat[:, 0:G * HPG * SEQ], const[:, C_ZERO:C_ZERO + 1].broadcast_to([P, G * HPG * SEQ]))\
                .then_inc(S["km_zero"], 1)
            act.wait_ge(S["km_zero"], 1)
            act.wait_ge(S["early_ps"], 1)
            keys_hi(0)
            masked_keys(0, 0, True)
            act.wait_ge(S["early_ps"], 2)
            keys_hi(1)
            norm_hi(0)
            masked_keys(1, 1, True)
            for m in range(2):
                act.wait_ge(S["proj_ps"], m + 1)
                queries_hi(m)
            norm_hi(1)
            proj_hi(2)
            act_batch(0, True, False)
            with act.Fori(1, BATCH - 1) as b:
                act_batch(b, False, False)
            act_batch(BATCH - 1, False, True)
            def chunk_norm(c):
                act.wait_ge(S["nmr_s"], c + 1)
                for t in range(*CHUNKS[c]):
                    act.activation(f16[:, t * P:(t + 1) * P], xs[:, t, :], ACT.Identity, scale=rstd[:, t:t + 1],
                                   bias=nmr[:, t:t + 1]).then_inc(S["ln4_act"], 1)

            def chunk_v(c):
                cols = slice(CHUNKS[c][0] * P, CHUNKS[c][1] * P)
                if c < 2:
                    act.wait_ge(S["ln4_act"], CHUNKS[c][1])
                else:
                    act.wait_ge(S["ln4"], TPB)
                act.activation(fv[:, cols], f16[:, cols], ACT.Copy, scale=rs[:, 0:1]).then_inc(S["fv_s"], 1)

            def chunk_overflow(c):
                cols = slice(CHUNKS[c][0] * P, CHUNKS[c][1] * P)
                if c == 0:
                    act.wait_ge(S["q_pool"], 1)
                else:
                    act.wait_ge(S["q_s"], c + 1)
                act.activation(fovf[:, cols], fq[:, cols], ACT.Copy, scale=144.0).then_inc(S["ovf_s"], 1)

            def chunk_turned(c):
                cols = slice(CHUNKS[c][0] * P, CHUNKS[c][1] * P)
                n = (CHUNKS[c][1] - CHUNKS[c][0]) * P // 2
                act.wait_ge(S["fT_ps"], c + 1)
                act.copy(xqT[:, cols], bk[c][:, 0:n].bitcast(bf16)).then_inc(S["fT_ev"], 1)

            def chunk_scaled(c):
                cols = slice(CHUNKS[c][0] * P, CHUNKS[c][1] * P)
                act.wait_ge(S["f_ps"], c + 1)
                act.activation(yb[:, cols], bk[3 + c][:, 0:(CHUNKS[c][1] - CHUNKS[c][0]) * P], ACT.Copy,
                               scale=rs[:, 2:3]).then_inc(S["y_s"], 1)

            for g in range(G - 2, G):
                o_copy(G * (BATCH - 1) + g, g, g - 1)
            chunk_norm(0)
            act.wait_ge(S["aoT_ps"], BATCH)
            act.copy(aoT[:, :], bk[7][:, 0:SEQ]).then_inc(S["aoT_ev"], 1)
            chunk_v(0)
            chunk_norm(1)
            chunk_v(1)
            chunk_v(2)
            for c in range(len(CHUNKS)):
                chunk_overflow(c)
            for c in range(len(CHUNKS)):
                chunk_turned(c)
            for c in range(len(CHUNKS)):
                chunk_scaled(c)

        @block.vector
        def _(dve):
            def moments(n, span, ready):
                if n > 1 and span[0] == 0:
                    dve.wait_ge(S[f"ln{n - 1}"], NT)
                for t in range(*span):
                    ready(t)
                    dve.bn_stats(stats[:, t, :], xs[:, t, :]).then_inc(S[f"st{n}"], 1)
                for t in range(*span):
                    dve.wait_ge(S[f"st{n}"], t + 1)
                    dve.bn_aggr(mv[:, t, :], stats[:, t, :]).then_inc(S[f"ag{n}"], 1)

            def scaled(n, part, span, out=xn):
                dve.wait_ge(S[f"ag{n}"], span[1])
                dve.wait_ge(S[f"rs{n}"], part + 1)
                for t in range(*span):
                    dve.tensor_scalar(out[:, t, :], xs[:, t, :], mv[:, t, 0:1], rstd[:, t:t + 1],
                                      ALU.subtract, ALU.mult).then_inc(S[f"ln{n}"], 1)

            def norm(n, ready):
                for h in range(2):
                    moments(n, HALVES[h], ready)
                for h in range(2):
                    scaled(n, h, HALVES[h])

            dve.wait_ge(S["ld_x"], 16)
            norm(1, lambda t: None)
            dve.wait_ge(S["ln1"], NT)
            dve.wait_ge(S["ld_par"], 80)
            dve.tensor_tensor(xs[:, :, :], xs[:, :, :], bl[:, :].unsqueeze(1).broadcast_to([P, NT, P]),
                              ALU.add).then_inc(S["bl_added"], 1)
            dve.tensor_tensor(bsum[:, 0:1], small[:, S_B:S_B + 1], small[:, S_B + 1:S_B + 2], ALU.add)\
                .then_inc(S["bsum_s"], 1)
            dve.wait_ge(S["bsum_s"], 1)
            dve.tensor_tensor(bsum[:, 1:2], bsum[:, 0:1], small[:, S_B + 2:S_B + 3], ALU.add)\
                .then_inc(S["bsum_s"], 1)
            dve.reciprocal(rs[:, 0:2], small[:, S_SIN:S_SIN + 2]).then_inc(S["rs_s"], 1)
            dve.tensor_tensor(rs[:, 2:3], small[:, S_SIN:S_SIN + 1], small[:, S_SK:S_SK + 1], ALU.mult)\
                .then_inc(S["rs_s"], 1)

            def normed(b):
                for t in range(TPB * b, TPB * (b + 1)):
                    dve.wait_ge(S["s_exp"], t + 1)
                    dve.reciprocal(rinv[:, t:t + 1], rsum[:, t:t + 1]).then_inc(S["s_rinv"], 1)
                    dve.wait_ge(S["s_rinv"], t + 1)
                    dve.tensor_scalar(att[:, t, :], att[:, t, :], rinv[:, t:t + 1], None, ALU.mult)\
                        .then_inc(S["s_norm"], 1)

            for b in range(BATCH):
                dve.wait_ge(S["s_ps"], b + 1)
                dve.tensor_reduce(nmax[:, TPB * b:TPB * (b + 1)], bk[2 + b][:, :].rearrange("p (t q) -> p t q", t=TPB),
                                  AX.X, ALU.max, negate=True).then_inc(S["s_max"], 1)
                if b > 0:
                    normed(b - 1)
            dve.wait_ge(S["cw_ps"], 1)
            dve.wait_ge(S["s_max"], BATCH)
            dve.wait_ge(S["bsum_s"], 2)
            dve.scalar_tensor_tensor(cv[:, :], bk[7][:, 0:NT], bsum[:, 1:2], nmax[:, :], ALU.add, ALU.subtract)\
                .then_inc(S["cv_s"], 1)
            normed(BATCH - 1)
            for h in range(2):
                dve.wait_ge(S["row_ps"], h + 1)
                dve.tensor_reduce(bnmax[:, 2 * h:2 * h + 2], bk[h][0:1, :].rearrange("p (b c) -> p b c", b=2),
                                  AX.X, ALU.max, negate=True).then_inc(S["row_max"], 1)
            dve.wait_ge(S["row_exp"], BATCH)
            dve.reciprocal(bden[:, BATCH:2 * BATCH], bden[:, 0:BATCH]).then_inc(S["row_inv"], 1)
            dve.wait_ge(S["wg_hi"], 1)
            dve.tensor_tensor(wgs[:, 1, :], wg[:, :], plain(wgs[:, 0, :]), ALU.subtract).then_inc(S["wg_lo"], 1)
            def power_of_two(v, e, scaled_s, count, base):
                dve.wait_ge(S[scaled_s], count)
                dve.tensor_scalar(e.bitcast(i32), v.bitcast(i32), 0x7F800000, None, ALU.bitwise_and)\
                    .then_inc(S["f_s"], 1)
                dve.wait_ge(S["f_s"], base + 1)
                dve.tensor_scalar(e, e, 2.0 ** -6, 1.5 * 2.0 ** 20, ALU.max, ALU.mult).then_inc(S["f_s"], 1)
                dve.wait_ge(S["f_s"], base + 2)

            def round_to_power(v, e, q, base):
                dve.tensor_tensor(q, v, e, ALU.add).then_inc(S["r_s"], 1)
                dve.wait_ge(S["r_s"], base + 1)
                dve.tensor_tensor(q, q, e, ALU.subtract).then_inc(S["q_s"], 1)

            def overflowed(dst, q, ovf, q_s, q_count, ovf_s, count):
                dve.wait_ge(S[q_s], q_count)
                dve.wait_ge(S[ovf_s], count)
                dve.scalar_tensor_tensor(dst, ovf, 0.0, q, ALU.mult, ALU.add).then_inc(S["xq_s"], 1)

            power_of_two(kv, ke, "kv_s", 1, 0)
            round_to_power(kv, ke, kr, 0)
            overflowed(kq[:, :], kr, kovf[:, :], "q_s", 1, "kovf_s", 1)
            for h in range(2):
                cols = slice(h * HALF, (h + 1) * HALF)
                dve.wait_ge(S["c2q_ev"], h + 1)
                dve.tensor_tensor(ccT[:, cols], c2qT[:, cols], cT[:, cols], ALU.mult).then_inc(S["cc_ev"], 1)
                if h == 0:
                    dve.wait_ge(S["q2c_ev"], 1)
                    for b in range(BATCH):
                        dve.scalar_tensor_tensor(w14[:, b, :], wl[:, 3, :], q2c[:, b:b + 1], wl[:, 0, :], ALU.mult,
                                                 ALU.add).then_inc(S["w14_s"], 1)
            dve.wait_ge(S["bl_added"], 1)
            for h in range(2):
                dve.wait_ge(S["z_ps"], h + 1)
                dve.tensor_tensor(xs[:, h * TPH:(h + 1) * TPH, :], xs[:, h * TPH:(h + 1) * TPH, :],
                                  bk[4 + h][:, :].rearrange("p (t d) -> p t d", t=TPH), ALU.add)\
                    .then_inc(S["z_add"], 1)
                moments(2, HALVES[h], lambda t: dve.wait_ge(S["z_add"], h + 1))
            for h in range(2):
                scaled(2, h, HALVES[h])
            for h in range(2):
                cols = slice(h * HALF, (h + 1) * HALF)
                dve.wait_ge(S["xT_hi"], h + 1)
                dve.tensor_tensor(xT[:, 1, cols], bk[4 + h][:, :], plain(xT[:, 0, cols]), ALU.subtract)\
                    .then_inc(S["xT_lo"], 1)

            def routing():
                dve.wait_ge(S["logit_ps"], 1)
                dve.tensor_copy(logit[:, :, :], bk[7][:, 0:NT * E].rearrange("p (t e) -> p t e", t=NT))\
                    .then_inc(S["logit_ev"], 1)
                dve.wait_ge(S["logit_ev"], 1)
                for t in range(NT):
                    dve.max(top[:, t, :], logit[:, t, :]).then_inc(S["top_s"], 1)
                for t in range(NT):
                    dve.wait_ge(S["top_s"], t + 1)
                    dve.max_index(topi[:, t, :], top[:, t, :], logit[:, t, :]).then_inc(S["topi_s"], 1)
                dve.wait_ge(S["top_s"], NT)
                dve.tensor_tensor(gap[:, 0, :], top[:, :, 1], top[:, :, 0], ALU.subtract).then_inc(S["gap_s"], 1)
                dve.wait_ge(S["topi_s"], NT)
                dve.tensor_copy(topf[:, :, :], topi[:, :, 0:2]).then_inc(S["route_s"], 1)
                dve.wait_ge(S["gap_exp"], 1)
                dve.tensor_scalar(gap[:, 2, :], gap[:, 1, :], 1.0, 2.0, ALU.add, ALU.mult).then_inc(S["route_s"], 1)
                dve.wait_ge(S["route_s"], 2)
                dve.reciprocal(gap[:, 2, :], gap[:, 2, :]).then_inc(S["route_s"], 1)
                dve.wait_ge(S["route_s"], 3)
                dve.tensor_tensor(gap[:, 3, :], gap[:, 1, :], gap[:, 2, :], ALU.mult).then_inc(S["route_s"], 1)
                iota = const[:, C_IOTA:C_IOTA + E].unsqueeze(1).broadcast_to([P, NT, E])
                for r in range(2):
                    dve.wait_ge(S["route_s"], 4)
                    dve.tensor_tensor(route[:, r, :, :], iota, topf[:, :, r:r + 1].broadcast_to([P, NT, E]),
                                      ALU.is_equal).then_inc(S["route_s"], 1)
                for r in range(2):
                    dve.wait_ge(S["route_s"], 5 + r)
                    dve.tensor_tensor(route[:, r, :, :], route[:, r, :, :],
                                      gap[:, 2 + r, :].unsqueeze(2).broadcast_to([P, NT, E]), ALU.mult)\
                        .then_inc(S["route_s"], 1)
                dve.wait_ge(S["route_s"], 8)
                dve.tensor_tensor(rw[:, :, :], route[:, 0, :, :], route[:, 1, :, :], ALU.add).then_inc(S["route_s"], 1)

            def hidden(n, first):
                for k in range(HB):
                    dve.wait_ge(S["tanh_s"], HB * n + k + 1)
                    if not first:
                        dve.wait_ge(S["hid_s"], HB * (n - 1) + k + 1)
                    dve.scalar_tensor_tensor(gated[:, k, :], tanhs[:, k, :], 1.0, bk[2 * k][:, :],
                                             ALU.add, ALU.mult).then_inc(S["gate_s"], 1)
                    dve.wait_ge(S["gate_s"], HB * n + k + 1)
                    if not first:
                        dve.wait_ge(S["hid_lo"], HB * (n - 1) + k + 1)
                    dve.tensor_tensor(hid[:, k, :], gated[:, k, :], bk[2 * k + 1][:, :], ALU.mult)\
                        .then_inc(S["hid_s"], 1)

            def weigh(n, parity, pair, h, first):
                dve.wait_ge(S["y_ps"], n + 1)
                cols = slice(h * HALF, (h + 1) * HALF)
                dve.wait_ge(S[f"rwb{parity}"], 16 * pair + 16)
                if not first:
                    dve.wait_ge(S["y_acc"], n - 1)
                dve.tensor_tensor(yw[:, h, :], bk[4 + h][:, :], rwb[:, parity, cols], ALU.mult)\
                    .then_inc(S["y_w"], 1)

            hidden(0, True)
            routing()
            hidden(1, False)
            hidden(2, False)
            hidden(3, False)
            for n in range(2):
                weigh(n, 0, 0, n, True)
            with dve.Fori(1, UNITS // 4) as i:
                for j in range(4):
                    hidden(4 * i + j, False)
                    weigh(4 * i + j - 2, 1 - j // 2, i - 1 + j // 2, j % 2, False)
            def add_experts(h):
                tiles = slice(h * TPH, (h + 1) * TPH)
                dve.wait_ge(S["accT_ps"], h + 1)
                dve.tensor_tensor(xs[:, tiles, :], xs[:, tiles, :],
                                  bk[6 + h][:, :].rearrange("p (t d) -> p t d", t=TPH), ALU.add)\
                    .then_inc(S["moe_s"], 1)

            def sum_moments(h):
                moments(3, HALVES[h], lambda t: dve.wait_ge(S["moe_s"], h + 1))

            def norm_lo(h):
                cols = slice(h * HALF, (h + 1) * HALF)
                dve.wait_ge(S["x3T_hi"], h + 1)
                dve.tensor_tensor(xT[:, 1, cols], bk[3 + h][:, :], plain(xT[:, 0, cols]), ALU.subtract)\
                    .then_inc(S["x3T_lo"], 1)

            def stack_queries(m, g, first):
                dve.wait_ge(S["q_hi"], m + 1)
                dve.wait_ge(S["k_hi"], m + 1)
                if not first:
                    dve.wait_ge(S["s1_ps"], 4 * (m - 3))
                    dve.wait_ge(S["qa_s"], m - 3)
                dve.scalar_tensor_tensor(qs[:, g, :], hiQ, const[:, C_AQ:C_AQ + 1],
                                         bk[0][:, 0:SEQ], ALU.mult, ALU.add).then_inc(S["qs_s"], 1)

            def stack_keys(m, g, first):
                dve.wait_ge(S["k_hi"], m + 1)
                if not first or g >= 2:
                    dve.wait_ge(S["km_act"], m - 1)
                    dve.wait_ge(S["km_pool"], 2 * (m - 1))
                dve.scalar_tensor_tensor(ks[:, g % 2, :], hiK, const[:, C_AK:C_AK + 1],
                                         bk[0][:, SEQ:2 * SEQ], ALU.mult, ALU.add).then_inc(S["ks_s"], 1)

            def maxima(m, g, pieces, first):
                for r in pieces:
                    dve.wait_ge(S["s1_ps"], 4 * m + r + 1)
                    if not first:
                        dve.wait_ge(S["mT_ps"], m - 1)
                    c0 = SHIFT_ROW + 2 * QUAD * (r % 2)
                    dve.tensor_reduce(negm[:, g % 2, r // 2, c0:c0 + QUAD + 1:QUAD],
                                      bk[1 + r % 2][:, :].rearrange("p (h k) -> p h k", h=2),
                                      AX.X, ALU.max, negate=True).then_inc(S["s1_max"], 1)

            def shifted(m, g, first):
                dve.wait_ge(S["mT_ps"], m + 1)
                dve.wait_ge(S["qs_s"], m + 1)
                if not first:
                    dve.wait_ge(S["s2_ps"], 2 * (m - 3))
                dve.tensor_tensor(qa[:, g, :], bk[2][:, 0:SEQ], plain(qs[:, g, :]), ALU.add).then_inc(S["qa_s"], 1)

            def normalise(b, t):
                bank = bk[7 * t]
                heads = bank[:, :].rearrange("p (g h r) -> p g h r", g=G, h=HPG)
                dve.wait_ge(S["oT_ps"], 2 * b + t + 1)
                dve.reciprocal(den[:, t, :, :].unsqueeze(3), heads[:, :, :, HD:HD + 1]).then_inc(S["den_s"], 1)
                dve.wait_ge(S["den_s"], 2 * b + t + 1)
                dve.tensor_tensor(ao[:, t, :].rearrange("p (g h d) -> p g h d", g=G, h=HPG),
                                  heads[:, :, :, 0:HD], den[:, t, :, :].unsqueeze(3).broadcast_to([P, G, HPG, HD]),
                                  ALU.mult).then_inc(S["ao_s"], 1)

            def add_attention(b, tiles):
                dve.wait_ge(S["wo_ps"], b + 1)
                dve.tensor_tensor(xs[:, tiles, :], xs[:, tiles, :],
                                  bk[7][:, 0:SEQ].rearrange("p (t d) -> p t d", t=TPB), ALU.add)\
                    .then_inc(S["x3_s"], 1)

            def dve_batch(b, first, last):
                for g in range(G):
                    m = G * b + g
                    more = not (last and g == G - 1)
                    ahead = not (last and g >= 2)
                    if more:
                        maxima(m + 1, (g + 1) % G, (0,), first and g == 0)
                    shifted(m, g, first)
                    if ahead:
                        stack_queries(m + 2, (g + 2) % G, first and g < 2)
                        stack_keys(m + 2, (g + 2) % G, first and g < 2)
                    if more:
                        maxima(m + 1, (g + 1) % G, (1, 2), first and g == 0)
                    if g == 1 and not first:
                        normalise(b - 1, 0)
                    if more:
                        maxima(m + 1, (g + 1) % G, (3,), first and g == 0)
                    if g == 1 and not first:
                        normalise(b - 1, 1)
                    if g == 3 and not first:
                        tiles = bass.ds(TPB * (b - 1), TPB) if not last else slice(TPB * (b - 1), TPB * b)
                        add_attention(b - 1, tiles)

            weigh(UNITS - 2, 1, E // 2 - 1, 0, False)
            add_experts(0)
            sum_moments(0)
            weigh(UNITS - 1, 1, E // 2 - 1, 1, False)
            dve.wait_ge(S["setup"], 1)
            dve.wait_ge(S["km_zero"], 1)
            stack_keys(0, 0, True)
            scaled(3, 0, HALVES[0])
            add_experts(1)
            stack_keys(1, 1, True)
            norm_lo(0)
            sum_moments(1)
            stack_queries(0, 0, True)
            maxima(0, 0, range(2), True)
            scaled(3, 1, HALVES[1])
            stack_queries(1, 1, True)
            maxima(0, 0, range(2, 4), True)
            norm_lo(1)
            dve_batch(0, True, False)
            with dve.Fori(1, BATCH - 1) as b:
                dve_batch(b, False, False)
            dve_batch(BATCH - 1, False, True)
            def chunk_out(c):
                cols = slice(CHUNKS[c][0] * P, CHUNKS[c][1] * P)
                tiles = slice(*CHUNKS[c])
                n = CHUNKS[c][1] - CHUNKS[c][0]
                dve.wait_ge(S["y_s"], c + 1)
                dve.tensor_tensor(yz[:, cols].rearrange("p (t d) -> p t d", t=n),
                                  yb[:, cols].rearrange("p (t d) -> p t d", t=n),
                                  fb[:, :].unsqueeze(1).broadcast_to([P, n, P]), ALU.add).then_inc(S["yz_s"], 1)
                dve.wait_ge(S["yz_s"], c // 2 + 1)
                dve.tensor_tensor(res[:, tiles, :], xs[:, tiles, :], yz[:, cols].rearrange("p (t d) -> p t d", t=n),
                                  ALU.add).then_inc(S["out_s"], 1)

            def shift(c):
                tiles = slice(*CHUNKS[c])
                dve.wait_ge(S["rs4"], c + 1)
                dve.scalar_tensor_tensor(nmr[:, tiles], mv[:, tiles, 0], -1.0, rstd[:, tiles], ALU.mult, ALU.mult)\
                    .then_inc(S["nmr_s"], 1)

            def chunk_power(c):
                cols = slice(CHUNKS[c][0] * P, CHUNKS[c][1] * P)
                power_of_two(fv[:, cols], fe[:, cols], "fv_s", c + 1, 2 * (c + 1))

            def chunk_rounded(c):
                cols = slice(CHUNKS[c][0] * P, CHUNKS[c][1] * P)
                round_to_power(fv[:, cols], fe[:, cols], fq[:, cols], c)

            def chunk_overflowed(c):
                cols = slice(CHUNKS[c][0] * P, CHUNKS[c][1] * P)
                q_s, q_count = ("q_pool", 1) if c == 0 else ("q_s", c + 1)
                overflowed(xq[:, cols], fq[:, cols], fovf[:, cols], q_s, q_count, "ovf_s", c + 1)

            for c in range(2):
                moments(4, CHUNKS[c], lambda t: dve.wait_ge(S["x3_s"], t // TPB + 1))
            shift(0)
            for t in range(TPB):
                normalise(BATCH - 1, t)
            shift(1)
            chunk_power(0)
            add_attention(BATCH - 1, slice(NT - TPB, NT))
            moments(4, CHUNKS[2], lambda t: dve.wait_ge(S["x3_s"], BATCH))
            chunk_power(1)
            chunk_rounded(1)
            scaled(4, 2, CHUNKS[2], f16.rearrange("p (t d) -> p t d", t=NT))
            chunk_power(2)
            chunk_rounded(2)
            for c in range(len(CHUNKS)):
                chunk_overflowed(c)
            chunk_out(0)
            chunk_out(2)

        @block.tensor
        def _(pe):
            def three(out, w, x, start, stop):
                pe.matmul(out, w[0], x[0], start=start, stop=False)
                pe.matmul(out, w[0], x[1], start=False, stop=False)
                return pe.matmul(out, w[1], x[0], start=False, stop=stop)

            def turn(ln, out, bank, h):
                for t in range(TPH):
                    pe.wait_ge(S[ln], h * TPH + t + 1)
                    ins = pe.transpose(bk[bank][:, t * P:(t + 1) * P], xn[:, h * TPH + t, :], ident)
                ins.then_inc(S[out], 1)

            pe.wait_ge(S["setup"], 1)
            for _ in range(WARM_UP):
                pe.matmul(bk[7][:, 0:SEQ], negm[:, 0, 0, :], negm[:, 1, :, :].rearrange("p t c -> p (t c)"),
                          start=True, stop=True)
            pe.wait_ge(S["ld_par"], 80)
            for h in range(2):
                turn("ln1", "cT_ps", h, h)
            pe.wait_ge(S["ld_ctx"], 32)
            def scores_of(b):
                pe.wait_ge(S["cpT_ev"], b // 2 + 1)
                for t in range(TPB):
                    tile = b * TPB + t
                    ins = pe.matmul(bk[2 + b][:, t * SEQ:(t + 1) * SEQ], cpT[:, tile * P:(tile + 1) * P],
                                    ctxT[:, b * SEQ:(b + 1) * SEQ], start=True, stop=True)
                ins.then_inc(S["s_ps"], 1)

            def attention_turned(b):
                pe.wait_ge(S["s_norm"], b * TPB + TPB)
                for t in range(TPB):
                    tile = b * TPB + t
                    for q in range(TPB):
                        ins = pe.transpose(bk[2 + b][:, q * SEQ + t * P:q * SEQ + (t + 1) * P],
                                           att[:, tile, q * P:(q + 1) * P], ident)
                ins.then_inc(S["aT_ps"], 1)

            for b in range(BATCH):
                scores_of(b)
            pe.wait_ge(S["cT_ev"], 2)
            for t in range(NT):
                ins = pe.matmul(bk[7][:, t:t + 1], cT[:, t * P:(t + 1) * P], small[:, S_WC:S_WC + 1],
                                start=True, stop=True)
            ins.then_inc(S["cw_ps"], 1)
            attention_turned(0)
            attention_turned(1)
            pe.wait_ge(S["cv_s"], 1)
            for h in range(2):
                for t in range(TPH):
                    ins = pe.matmul(bk[h][0:1, t * P:(t + 1) * P], cv[:, h * TPH + t:h * TPH + t + 1], ident,
                                    start=True, stop=True)
                ins.then_inc(S["row_ps"], 1)
            attention_turned(2)
            attention_turned(3)
            def context_to_query(b):
                pe.wait_ge(S["aT_ev"], b + 1)
                pe.wait_ge(S["row_exp"], TPB * (b // 2 + 1))
                for q in range(TPB):
                    ins = pe.matmul(bk[b // 2][:, (b % 2) * SEQ:(b % 2 + 1) * SEQ], ctx[:, b * TPB + q, :],
                                    attT[:, b, q, :], start=q == 0, stop=q == TPB - 1)
                if b % 2:
                    ins.then_inc(S["c2q_ps"], 1)

            context_to_query(0)
            context_to_query(1)
            pe.wait_ge(S["row_inv"], 1)
            for t in range(NT):
                b = t // TPB
                ins = pe.matmul(bk[7][:, 16 + t:17 + t], brow[:, t * P:(t + 1) * P],
                                bden[:, BATCH + b:BATCH + b + 1], start=True, stop=True)
            ins.then_inc(S["bcol_ps"], 1)
            context_to_query(2)
            context_to_query(3)
            pe.wait_ge(S["bcol_ev"], 1)
            for b in range(BATCH):
                for t in range(TPB):
                    tile = b * TPB + t
                    ins = pe.matmul(bk[7][:, 32 + b:33 + b], xn[:, tile, :], bcol[:, tile:tile + 1],
                                    start=t == 0, stop=t == TPB - 1)
            ins.then_inc(S["q2c_ps"], 1)
            for h in range(2):
                pe.wait_ge(S["cc_ev"], h + 1)
                for t in range(TPH):
                    tile = h * TPH + t
                    b = tile // TPB
                    out = bk[4 + h][:, t * P:(t + 1) * P]
                    cols = slice(tile * P, (tile + 1) * P)
                    pe.matmul(out, c2qT[:, cols], wl[:, 1, :], start=True, stop=False)
                    pe.matmul(out, ccT[:, cols], wl[:, 2, :], start=False, stop=False)
                    pe.wait_ge(S["w14_s"], b + 1)
                    ins = pe.matmul(out, cT[:, cols], w14[:, b, :], start=False, stop=True)
                ins.then_inc(S["z_ps"], 1)
            pe.wait_ge(S["ld_att"], 7 * 16)
            pe.wait_ge(S["q2c_ev"], 1)
            for h in range(2):
                for t in range(TPH):
                    tile = h * TPH + t
                    ins = pe.matmul(bk[6 + h][:, t * P:(t + 1) * P], ctxT[:, tile * P:(tile + 1) * P], wv[:, :],
                                    start=True, stop=True)
                ins.then_inc(S["v_ps"], 1)
            for h in range(2):
                turn("ln2", "xT_ps", 4 + h, h)

            def logits():
                pe.wait_ge(S["wg_lo"], 1)
                for h in range(2):
                    cols = slice(h * HALF, (h + 1) * HALF)
                    ins = three(bk[4 + 3 * h][0:E, :], (wgs[:, 0, :], wgs[:, 1, :]), (xT[:, 0, cols], xT[:, 1, cols]),
                                True, True)
                    ins.then_inc(S["logitT_ps"], 1)

            def logits_turned():
                pe.wait_ge(S["logitT_ev"], 2)
                for tile in range(NT):
                    ins = pe.transpose(bk[7][:, tile * E:(tile + 1) * E], logitT[:, tile * P:(tile + 1) * P],
                                       ident[0:E, 0:E])
                ins.then_inc(S["logit_ps"], 1)

            def up(n, pair, parity, h, first, blocks=range(HB)):
                if h == 0:
                    pe.wait_ge(S[f"w12_in{parity}"], 16 * pair + 16)
                cols = slice(h * HALF, (h + 1) * HALF)
                x = (xT[:, 0, cols], xT[:, 1, cols])
                for k in blocks:
                    for w, used in enumerate(("gate_s", "hid_s")):
                        if not first:
                            pe.wait_ge(S[used], HB * (n - 1) + k + 1)
                        c0 = w * HID + k * P
                        ins = three(bk[2 * k + w][:, :], (wxs[:, parity, 0, c0:c0 + P], wxs[:, parity, 1, c0:c0 + P]),
                                    x, True, True)
                    ins.then_inc(S["uv_ps"], 1)

            def down(n, pair, parity, h, first):
                pe.wait_ge(S[f"w3_in{parity}"], 16 * pair + 16)
                pe.wait_ge(S["hid_lo"], HB * (n + 1))
                if not first:
                    pe.wait_ge(S["y_w"], n - 1)
                for k in range(HB):
                    c0 = 2 * HID + k * P
                    ins = three(bk[4 + h][:, :], (wxs[:, parity, 0, c0:c0 + P], wxs[:, parity, 1, c0:c0 + P]),
                                (hids[:, h, 0, k, :], hids[:, h, 1, k, :]), k == 0, k == HB - 1)
                ins.then_inc(S["y_ps"], 1)

            pe.wait_ge(S["xT_lo"], 1)
            up(0, 0, 0, 0, True)
            pe.wait_ge(S["xT_lo"], 2)
            pe.wait_ge(S["v_ev"], 2)
            logits()
            up(1, 0, 0, 1, False, (0,))
            logits_turned()
            up(1, 0, 0, 1, False, (1,))
            pe.wait_ge(S["route_s"], 9)
            for h in range(2):
                for t in range(TPH):
                    ins = pe.transpose(bk[4 + h][0:E, t * P:(t + 1) * P], rw[:, h * TPH + t, :], ident)
                ins.then_inc(S["rwT_ps"], 1)
            for n in range(2, 4):
                up(n, 0, 1, n % 2, False)
                pe.wait_ge(S["rwT_ev"], 2)
                down(n - 2, 0, 0, n % 2, True)
            with pe.Fori(1, UNITS // 4) as i:
                for j in range(4):
                    up(4 * i + j, i, j // 2, j % 2, False)
                    down(4 * i + j - 2, i - 1 + j // 2, 1 - j // 2, j % 2, False)
            def sum_turned(h):
                pe.wait_ge(S["y_acc"], UNITS - 3 + h)
                pe.wait_ge(S["y_w"], UNITS - 1 + h)
                for t in range(TPH):
                    out = bk[6 + h][:, t * P:(t + 1) * P]
                    pe.matmul(out, accT[:, h * HALF + t * P:h * HALF + (t + 1) * P], ident, start=True, stop=False)
                    ins = pe.matmul(out, yw[:, h, t * P:(t + 1) * P], ident, start=False, stop=True)
                ins.then_inc(S["accT_ps"], 1)

            def project(m, g, b, a, late=None, early=False):
                if a == 0 and not early:
                    pe.wait_ge(S["ks_s"], m)
                    pe.wait_ge(S["qs_s"], m)
                if late is not None:
                    pe.wait_ge(S["ao_s"], late)
                cols = slice(b * SEQ, (b + 1) * SEQ) if isinstance(b, int) else bass.ds(SEQ * b, SEQ)
                src = (xT, ctxTs)[a]
                ins = three(bk[0][:, a * SEQ:(a + 1) * SEQ],
                            (wqk[:, 0, a, g * P:(g + 1) * P], wqk[:, 1, a, g * P:(g + 1) * P]),
                            (src[:, 0, cols], src[:, 1, cols]), True, True)
                if a == 1 and early:
                    ins.then_inc(S["early_ps"], 1)
                elif a == 1 or early:
                    ins.then_inc(S["proj_ps"], 1)

            def scores(m, g, r, first):
                pe.wait_ge(S["qs_s"], m + 1)
                if r % 2 == 0:
                    pe.wait_ge(S["km_act"], m + 1)
                else:
                    pe.wait_ge(S["km_pool"], 2 * (m + 1))
                if r == 1 and not first:
                    pe.wait_ge(S["qa_s"], m)
                elif r > 1 or not first:
                    pe.wait_ge(S["s1_max"], 4 * m + r - 1)
                t, pair = r // 2, r % 2
                pe.matmul(bk[1 + r % 2][:, :], qs[:, g, t * P:(t + 1) * P],
                          km[:, g, 2 * pair:2 * pair + 2, :].rearrange("p h k -> p (h k)"),
                          start=True, stop=True).then_inc(S["s1_ps"], 1)

            def turn_maxima(m, g):
                pe.wait_ge(S["s1_max"], 4 * (m + 1))
                for t in range(TPB):
                    ins = pe.transpose(bk[2][:, t * P:(t + 1) * P], negm[:, g % 2, t, :], ident)
                ins.then_inc(S["mT_ps"], 1)

            def shifted_scores(m, g, r, first):
                pe.wait_ge(S["qa_s"], m + 1)
                if not first:
                    pe.wait_ge(S["p_s"], 2 * (m - 1) + r + 1)
                for a in range(2):
                    j = 2 * r + a
                    for t in range(TPB):
                        ins = pe.matmul(bk[3 + j][:, t * SEQ:(t + 1) * SEQ], km[:, g, j, t * P:(t + 1) * P],
                                        qa[:, g, :], start=True, stop=True)
                ins.then_inc(S["s2_ps"], 1)

            def outputs(m, g, b, first, bank=7):
                pe.wait_ge(S["p_s"], 2 * (m + 1))
                pe.wait_ge(S["v_s"], b + 1)
                if not first and bank == 7:
                    pe.wait_ge(S["o_ev"], m)
                for j in range(HPG):
                    for t in range(TPB):
                        ins = pe.matmul(bk[bank][QUAD * j:QUAD * (j + 1), SEQ:2 * SEQ], vones[:, t, g * HPG + j, :],
                                        probs[:, g % 2, j, t, :], start=t == 0, stop=t == TPB - 1,
                                        tile_position=(0, QUAD * j))
                ins.then_inc(S["pv_ps"], 1)

            def turn_outputs(b, t):
                for g in range(G):
                    ins = pe.transpose(bk[7 * t][:, g * P:(g + 1) * P], os_[:, g, t * P:(t + 1) * P], ident)
                ins.then_inc(S["oT_ps"], 1)

            def turn_normalised(b):
                pe.wait_ge(S["ao_s"], 2 * (b + 1))
                for t in range(TPB):
                    ins = pe.transpose(bk[7][:, t * P:(t + 1) * P], ao[:, t, :], ident)
                ins.then_inc(S["aoT_ps"], 1)

            def output_layer(b):
                pe.wait_ge(S["aoT_ev"], b + 1)
                for t in range(TPB):
                    pe.matmul(bk[7][:, t * P:(t + 1) * P], ones[:, :], bo[:, :], start=True, stop=False)
                    ins = pe.matmul(bk[7][:, t * P:(t + 1) * P], aoT[:, t * P:(t + 1) * P], wo[:, :],
                                    start=False, stop=True)
                ins.then_inc(S["wo_ps"], 1)

            def pe_batch(b, first, last):
                for g in range(G):
                    m = G * b + g
                    more = not (last and g == G - 1)
                    turn_maxima(m, g)
                    if not first or g >= 2:
                        outputs(m - 2, (g - 2) % G, b if g >= 2 else b - 1, first and g == 2)
                    if more:
                        scores(m + 1, (g + 1) % G, 1, False)
                        scores(m + 1, (g + 1) % G, 2, False)
                    if g == 1 and not first:
                        pe.wait_ge(S["o_ev"], G * b)
                        pe.wait_ge(S["ks_s"], m + 3)
                        turn_outputs(b - 1, 0)
                    shifted_scores(m, g, 0, first and g == 0)
                    shifted_scores(m, g, 1, first and g == 0)
                    if last and g == G - 1:
                        outputs(m - 1, g - 1, b, False, 1)
                    if more:
                        scores(m + 1, (g + 1) % G, 3, False)
                    if not first:
                        pe.wait_ge(S["o_ev"], m - 1)
                    if g == 1 and not first:
                        turn_outputs(b - 1, 1)
                    if g == 2 and not first:
                        turn_normalised(b - 1)
                    if g == 3 and not first:
                        output_layer(b - 1)
                    if not (last and g >= 1):
                        project(m + 3, (g + 3) % G, b + (g + 3) // G, 0, TPB * b - 1 if g == 1 and not first else None)
                    if not (last and g >= 2):
                        scores(m + 2, (g + 2) % G, 0, False)
                    if not (last and g >= 1):
                        project(m + 3, (g + 3) % G, b + (g + 3) // G, 1)
                    if g == 1 and not first:
                        pe.wait_ge(S["ao_s"], TPB * b)
                    if g == 2 and not first:
                        pe.wait_ge(S["aoT_ev"], b)
                    if g == 3 and not first:
                        pe.wait_ge(S["x3_s"], b)

            down(UNITS - 2, E // 2 - 1, 1, 0, False)
            pe.wait_ge(S["gate_s"], HB * UNITS - 1)
            pe.wait_ge(S["ctx_lo"], 1)
            pe.wait_ge(S["wqk_lo"], 1)
            project(0, 0, 0, 1, early=True)
            sum_turned(0)
            down(UNITS - 1, E // 2 - 1, 1, 1, False)
            sum_turned(1)
            pe.wait_ge(S["ks_s"], 1)
            project(1, 1, 0, 1, early=True)
            turn("ln3", "x3T_ps", 3, 0)
            pe.wait_ge(S["x3T_lo"], 1)
            pe.wait_ge(S["ks_s"], 2)
            project(0, 0, 0, 0, early=True)
            for r in range(2):
                scores(0, 0, r, True)
            project(1, 1, 0, 0, early=True)
            for r in range(2, 4):
                scores(0, 0, r, True)
            turn("ln3", "x3T_ps", 4, 1)
            for a in range(2):
                project(2, 2, 0, a)
            scores(1, 1, 0, False)
            pe.wait_ge(S["x3T_lo"], 2)
            pe.wait_ge(S["setup"], 1)
            pe_batch(0, True, False)
            with pe.Fori(1, BATCH - 1) as b:
                pe_batch(b, False, False)
            pe_batch(BATCH - 1, False, True)
            outputs(G * BATCH - 1, G - 1, BATCH - 1, False, 2)
            pe.wait_ge(S["o_ev"], G * BATCH)
            for t in range(TPB):
                turn_outputs(BATCH - 1, t)
            turn_normalised(BATCH - 1)
            output_layer(BATCH - 1)

            pe.wait_ge(S["ident16_s"], 1)
            def chunk_turn(c):
                pe.wait_ge(S["xq_s"], c + 2)
                for t in range(*CHUNKS[c]):
                    c0 = (t - CHUNKS[c][0]) * P // 2
                    ins = pe.transpose(bk[c][:, c0:c0 + P // 2].bitcast(bf16), xq[:, t * P:(t + 1) * P],
                                       ident16[:, :])
                ins.then_inc(S["fT_ps"], 1)

            def chunk_product(c):
                pe.wait_ge(S["fT_ev"], c + 1)
                for t in range(*CHUNKS[c]):
                    c0 = (t - CHUNKS[c][0]) * P
                    ins = pe.matmul(bk[3 + c][:, c0:c0 + P], xqT[:, t * P:(t + 1) * P], kq[:, :],
                                    start=True, stop=True)
                ins.then_inc(S["f_ps"], 1)

            for c in range(len(CHUNKS)):
                chunk_turn(c)
            for c in range(len(CHUNKS)):
                chunk_product(c)


def kernel(**inputs):
    import numpy as np
    import concourse.bacc as bacc
    from concourse import mybir
    from concourse.bass_utils import run_bass_kernel_spmd as run

    a = {k: np.asarray(v) for k, v in inputs.items()}

    def rows(v):
        return np.ascontiguousarray(np.broadcast_to(v.reshape(1, -1), (P, v.size)))

    def tiles(v):
        return np.ascontiguousarray(v.reshape(NT, P, P).transpose(1, 0, 2))

    def stacked(w):
        out = np.zeros((P, G, HPG, 4, HD), w.dtype)
        out[:, :, :, 0:3, :] = w.reshape(P, G, HPG, 1, HD)
        return out.reshape(P, G * P)

    const = np.zeros((P, N_CONST), np.float32)
    row = np.arange(P) % QUAD
    const[:, C_AQ] = -1.0 * (row // HD == 1)
    const[:, C_AK] = -1.0 * (row // HD == 2) + 1.0 * (row == SHIFT_ROW)
    const[:, C_ONE] = row == SHIFT_ROW
    const[:, C_IOTA:C_IOTA + E] = np.arange(E)
    const[:, C_ID:C_ID + P] = np.eye(P)
    small = np.concatenate(
        [a["L0_xattn_w_cq"].reshape(P, 1), a["L0_xattn_w_q"].reshape(P, 1), a["L0_xattn_w_c"].reshape(P, 1),
         rows(a["L0_xattn_b_cq"]), rows(a["L0_xattn_b_c"]), rows(a["L0_xattn_b_q"]),
         rows(a["L1_ffn_input_scale"]), rows(a["L1_ffn_kernel_scale"])], axis=1)
    arrays = {
        "x": tiles(a["x"]), "ctx": tiles(a["ctx_1024"]), "ctxT": np.ascontiguousarray(a["ctx_1024"].reshape(TOK, P).T),
        "small": small, "const": const,
        "wl": np.ascontiguousarray(a["L0_xattn_W_l"].T.reshape(4, P, P).transpose(1, 0, 2)),
        "bl": rows(a["L0_xattn_b_l"]), "wg": a["L0_ffn_Wg"],
        "w12": np.ascontiguousarray(np.concatenate([a["L0_ffn_W1"], a["L0_ffn_W2"]], axis=2).transpose(1, 0, 2)),
        "w3": np.ascontiguousarray(a["L0_ffn_W3"].reshape(E, HB, P, P).transpose(2, 0, 1, 3).reshape(P, E, HB * P)),
        "wq": stacked(a["L1_xattn_W_q"]), "wk": stacked(a["L1_xattn_W_k"]), "wv": a["L1_xattn_W_v"],
        "wo": a["L1_xattn_W_o"], "bo": a["L1_xattn_b_o"].reshape(1, P), "fk": a["L1_ffn_kernel"], "fb": rows(a["L1_ffn_bias"]),
    }
    nc = bacc.Bacc("TRN2", target_bir_lowering=False, num_devices=1)
    args = [nc.dram_tensor(f"in_{k}", v.shape, mybir.dt.from_np(v.dtype), kind="ExternalInput").ap()
            for k, v in arrays.items()]
    out = nc.dram_tensor("out", (P, NT, P), mybir.dt.float32, kind="ExternalOutput").ap()
    routing = nc.dram_tensor("routing", (E, TOK), mybir.dt.float32, kind="Internal").ap()
    build(nc, *args, routing, out)
    r = run(nc, [{f"in_{k}": np.ascontiguousarray(v) for k, v in arrays.items()}], core_ids=[0])
    return r.results[0]["out"].transpose(1, 0, 2).reshape(BATCH, SEQ, P)
```
